# Optimizing a Trainium2 kernel written in Bass

```python
import numpy as np
import jax
import jax.numpy as jnp

def _softmax(x, axis=-1):
    return jax.nn.softmax(x, axis=axis)

def _gelu(x):
    return jax.nn.gelu(x, approximate=True)

def _silu(x):
    return jax.nn.silu(x)

def _sigmoid(x):
    return jax.nn.sigmoid(x)

def _layernorm(x, axis=-1, eps=1e-05):
    m = jnp.mean(x, axis=axis, keepdims=True)
    v = jnp.var(x, axis=axis, keepdims=True)
    return (x - m) / jnp.sqrt(v + eps)

def _scatter_add(tgt, idx, src, axis=0):
    return tgt.at[idx].add(src)

def _segment_sum(src, seg, n):
    return jax.ops.segment_sum(src, seg, n)
kernel_name = 'mk_decoder_preln_d2_seqx_r4_f2b292'

def setup_inputs(seed: int=0):
    np.random.seed(seed)
    _w = jnp.asarray

    def _rec_inputs():
        import jax
        import jax.numpy as jnp
        _rk = jax.random.key(seed)
        x = -0.0003929 + 0.9999 * jax.random.normal(jax.random.fold_in(_rk, 1), (8, 512, 256), jnp.float32)
        _lenS = 512 - jax.random.randint(jax.random.fold_in(_rk, 7), (8,), 0, max(1, 512 // 4) + 1, jnp.int32)
        _lenS2 = 512 - jax.random.randint(jax.random.fold_in(_rk, 8), (8,), 0, max(1, 512 // 4) + 1, jnp.int32)
        _ctx_1024P = jax.random.normal(jax.random.fold_in(_rk, 11), (8, 16, 256), jnp.float32)
        _ctx_1024c = jax.random.dirichlet(jax.random.fold_in(_rk, 511), 0.3 * jnp.ones((16,), jnp.float32), (8, 512))
        _ctx_1024t = jnp.einsum('bsk,bkd->bsd', _ctx_1024c, _ctx_1024P)
        _ctx_1024t = _ctx_1024t * jax.lax.rsqrt(jnp.mean(jnp.square(_ctx_1024t)) + 1e-12) * 0.953939
        ctx_1024 = 2.81802e-05 + 1.00001 * (_ctx_1024t + 0.3 * jax.random.normal(jax.random.fold_in(_rk, 611), (8, 512, 256), jnp.float32))
        return (x, ctx_1024)
    x, ctx_1024 = _rec_inputs()

    def _L0_attn_setup():
        import jax, jax.numpy as jnp
        import numpy as np
        DIM = 256
        EXPAND = 2
        D_INNER = DIM * EXPAND
        D_STATE = 16
        D_CONV = 4
        DT_RANK = max(16, DIM // 16)
        BATCH = 2
        SEQ = 256
        EPS_RMS = 1e-06

        def _ssm_forward(x, W_in, W_conv, b_conv, W_x, W_dt, b_dt, A_log, D, rms_w, W_out):
            b, s, _ = x.shape
            xz = jnp.einsum('bsd,ed->bse', x, W_in)
            x_in, z = jnp.split(xz, 2, axis=-1)
            xpad = jnp.pad(x_in, ((0, 0), (D_CONV - 1, 0), (0, 0)))
            xc = b_conv
            for k in range(D_CONV):
                xc = xc + W_conv[:, k] * xpad[:, k:k + s, :]
            xc = jax.nn.silu(xc)
            dbl = jnp.einsum('bsd,ed->bse', xc, W_x)
            dt, Bm, Cm = jnp.split(dbl, [DT_RANK, DT_RANK + D_STATE], axis=-1)
            dt = jax.nn.softplus(jnp.einsum('bsr,dr->bsd', dt, W_dt) + b_dt) + 0.0001
            A = -jnp.exp(A_log)
            dA = jnp.exp(jnp.clip(dt[..., None] * A, -10.0, 10.0))
            dBu = dt[..., None] * Bm[:, :, None, :] * xc[..., None]

            def step(h, inp):
                dA_t, dBu_t, C_t = inp
                h = dA_t * h + dBu_t
                y = jnp.einsum('bdn,bn->bd', h, C_t)
                return (h, y)
            h0 = jnp.zeros((b, D_INNER, D_STATE), x.dtype)
            _, ys = jax.lax.scan(step, h0, (jnp.moveaxis(dA, 1, 0), jnp.moveaxis(dBu, 1, 0), jnp.moveaxis(Cm, 1, 0)))
            y = jnp.moveaxis(ys, 0, 1) + xc * D
            y = y * jax.nn.silu(z)
            y = y * jax.lax.rsqrt(jnp.mean(y * y, axis=-1, keepdims=True) + EPS_RMS) * rms_w
            return jnp.einsum('bse,de->bsd', y, W_out)
        key = jax.random.key(seed)
        ks = jax.random.split(key, 10)

        def nrm(k, shape, scale=0.02):
            return jax.random.normal(k, shape, jnp.float32) * scale
        x = jax.random.normal(ks[0], (BATCH, SEQ, DIM), jnp.float32)
        W_in = nrm(ks[1], (2 * D_INNER, DIM))
        W_conv = nrm(ks[2], (D_INNER, D_CONV), 0.1)
        b_conv = nrm(ks[3], (D_INNER,), 0.01)
        W_x = nrm(ks[4], (DT_RANK + 2 * D_STATE, D_INNER))
        dt_std = DT_RANK ** (-0.5) * 0.1
        W_dt = jax.random.uniform(ks[5], (D_INNER, DT_RANK), jnp.float32, -dt_std, dt_std)
        b_dt = jax.random.uniform(ks[6], (D_INNER,), jnp.float32, 0.001, 0.1)
        A = jnp.arange(1, D_STATE + 1, dtype=jnp.float32)[None, :] + 0.01 * jax.random.normal(ks[7], (D_INNER, D_STATE), jnp.float32)
        A_log = jnp.log(A + 1e-08)
        D = jnp.ones((D_INNER,), jnp.float32) * 0.1
        rms_w = jnp.ones((D_INNER,), jnp.float32)
        W_out = nrm(ks[8], (DIM, D_INNER))
        return dict(x=x, W_in=W_in, W_conv=W_conv, b_conv=b_conv, W_x=W_x, W_dt=W_dt, b_dt=b_dt, A_log=A_log, D=D, rms_w=rms_w, W_out=W_out)
    _L0_attn_all = _L0_attn_setup()
    _L0_attn_in = {k: v for k, v in _L0_attn_all.items() if k in ('W_in', 'W_conv', 'b_conv', 'W_x', 'W_dt', 'b_dt', 'A_log', 'D', 'rms_w', 'W_out')}
    del _L0_attn_all

    def _L0_xattn_setup():
        import jax, jax.numpy as jnp
        import numpy as np
        DIM, HEADS, DIM_HEAD, EPS = (256, 16, 64, 1e-12)

        def _phi(x):
            return jax.nn.elu(x) + 1.0
        key = jax.random.key(seed)
        ks = jax.random.split(key, 7)
        B, L = (4, 1024)
        xav = float(np.sqrt(6.0 / (DIM + HEADS * DIM_HEAD)))
        return {'query': jax.random.normal(ks[0], (B, L, DIM), jnp.float32), 'key': jax.random.normal(ks[1], (B, L, DIM), jnp.float32), 'value': jax.random.normal(ks[2], (B, L, DIM), jnp.float32), 'Wq': jax.random.uniform(ks[3], (DIM, HEADS * DIM_HEAD), jnp.float32, -xav, xav), 'Wk': jax.random.uniform(ks[4], (DIM, HEADS * DIM_HEAD), jnp.float32, -xav, xav), 'Wv': jax.random.uniform(ks[5], (DIM, HEADS * DIM_HEAD), jnp.float32, -xav, xav), 'Wo': jax.random.uniform(ks[6], (HEADS * DIM_HEAD, DIM), jnp.float32, -xav, xav), 'causal': 1}
    _L0_xattn_all = _L0_xattn_setup()
    _L0_xattn_in = {k: v for k, v in _L0_xattn_all.items() if k in ('Wq', 'Wk', 'Wv', 'Wo')}
    del _L0_xattn_all

    def _L0_ffn_setup():
        import jax, jax.numpy as jnp
        import numpy as np
        N_EMBD = 256
        N_STATE = 1024
        key = jax.random.key(seed)
        k_x, k_w1, k_b1, k_w2, k_b2 = jax.random.split(key, 5)
        x = jax.random.normal(k_x, (4, 512, N_EMBD), dtype=jnp.float32)
        w1 = jax.random.normal(k_w1, (N_EMBD, N_STATE), dtype=jnp.float32) * (1.0 / np.sqrt(N_EMBD))
        b1 = jax.random.normal(k_b1, (N_STATE,), dtype=jnp.float32) * 0.02
        w2 = jax.random.normal(k_w2, (N_STATE, N_EMBD), dtype=jnp.float32) * (1.0 / np.sqrt(N_STATE))
        b2 = jax.random.normal(k_b2, (N_EMBD,), dtype=jnp.float32) * 0.02
        return {'x': x, 'w1': w1, 'b1': b1, 'w2': w2, 'b2': b2}
    _L0_ffn_all = _L0_ffn_setup()
    _L0_ffn_in = {k: v for k, v in _L0_ffn_all.items() if k in ('w1', 'b1', 'w2', 'b2')}
    del _L0_ffn_all

    def _L1_attn_setup():
        import jax, jax.numpy as jnp
        import numpy as np
        B, T, DM, H, DH = (4, 512, 256, 16, 64)
        DI = H * DH
        CLIP = 1.0
        LN_EPS = 1e-05
        key = jax.random.key(seed)
        ks = jax.random.split(key, 9)

        def xav(k, shape):
            lim = float(np.sqrt(6.0 / (shape[0] + shape[1])))
            return jax.random.uniform(k, shape, jnp.float32, -lim, lim)

        def kai(k, shape):
            lim = float(1.0 / np.sqrt(shape[1]))
            return jax.random.uniform(k, shape, jnp.float32, -lim, lim)
        return {'x': jax.random.normal(ks[0], (B, T, DM), jnp.float32), 'Wq': xav(ks[1], (DI, DM)), 'Wk': xav(ks[2], (DI, DM)), 'Wv': xav(ks[3], (DI, DM)), 'Wa': kai(ks[4], (DI, DM)), 'ba': jnp.full((DI,), 3.0, jnp.float32), 'Wb': kai(ks[5], (H, DM)), 'bb': jnp.zeros((H,), jnp.float32), 'Wg': kai(ks[6], (H, DM)), 'bg': jnp.zeros((H,), jnp.float32), 'WaR': kai(ks[7], (DI, DM)), 'baR': jnp.full((DI,), 3.0, jnp.float32), 'Wo': xav(ks[8], (DM, DI)), 'ln_w': jnp.ones((DM,), jnp.float32), 'ln_b': jnp.zeros((DM,), jnp.float32)}
    _L1_attn_all = _L1_attn_setup()
    _L1_attn_in = {k: v for k, v in _L1_attn_all.items() if k in ('Wq', 'Wk', 'Wv', 'Wa', 'ba', 'Wb', 'bb', 'Wg', 'bg', 'WaR', 'baR', 'Wo', 'ln_w', 'ln_b')}
    del _L1_attn_all

    def _L1_xattn_setup():
        import jax, jax.numpy as jnp
        import numpy as np
        D_MODEL = 256
        HEADS = 16
        D_HEAD = D_MODEL // HEADS
        SEQ = 512
        C = 2
        K_TOP = int(C * np.log(SEQ))
        key = jax.random.key(seed)
        ks = jax.random.split(key, 5)
        s = 0.02
        return {'Q': jax.random.normal(ks[0], (4, SEQ, D_MODEL), jnp.float32), 'K': jax.random.normal(ks[1], (4, SEQ, D_MODEL), jnp.float32), 'V': jax.random.normal(ks[2], (4, SEQ, D_MODEL), jnp.float32), 'Wq': jax.random.normal(ks[3], (D_MODEL, D_HEAD), jnp.float32) * s, 'bq': jnp.zeros((D_HEAD,), jnp.float32), 'Wout': jax.random.normal(ks[4], (HEADS * D_HEAD, D_MODEL), jnp.float32) * s, 'bout': jnp.zeros((D_MODEL,), jnp.float32)}
    _L1_xattn_all = _L1_xattn_setup()
    _L1_xattn_in = {k: v for k, v in _L1_xattn_all.items() if k in ('Wq', 'bq', 'Wout', 'bout')}
    del _L1_xattn_all

    def _L1_ffn_setup():
        import jax, jax.numpy as jnp
        import numpy as np
        D_MODEL = 256
        EXPANSION = 4
        D_HIDDEN = D_MODEL * EXPANSION
        NUM_STAGES = int(np.log2(D_HIDDEN))

        def butterfly(y, weights, dim):
            lead = y.shape[:-1]
            for stage in range(weights.shape[0]):
                s = 2 ** stage
                nb = dim // (2 * s)
                yr = y.reshape(*lead, nb, 2, s)
                a = yr[..., 0, :]
                b = yr[..., 1, :]
                w = weights[stage].reshape(nb, s, 2, 2)
                na = w[..., 0, 0] * a + w[..., 0, 1] * b
                nb2 = w[..., 1, 0] * a + w[..., 1, 1] * b
                y = jnp.stack([na, nb2], axis=-2).reshape(*lead, dim)
            return y
        key = jax.random.key(seed)
        ks = jax.random.split(key, 6)
        B, S = (4, 512)
        x = jax.random.normal(ks[0], (B, S, D_MODEL), jnp.float32)
        W_exp = jax.random.normal(ks[1], (D_MODEL, D_HIDDEN), jnp.float32) * 0.02
        b_exp = jnp.zeros((D_HIDDEN,), jnp.float32)
        up_weights = jax.random.normal(ks[2], (NUM_STAGES, D_HIDDEN // 2, 2, 2), jnp.float32) * 0.02
        up_bias = jnp.zeros((D_HIDDEN,), jnp.float32)
        down_weights = jax.random.normal(ks[3], (NUM_STAGES, D_HIDDEN // 2, 2, 2), jnp.float32) * 0.02
        W_con = jax.random.normal(ks[4], (D_HIDDEN, D_MODEL), jnp.float32) * 0.02
        b_con = jnp.zeros((D_MODEL,), jnp.float32)
        down_bias = jnp.zeros((D_MODEL,), jnp.float32)
        return dict(x=x, W_exp=W_exp, b_exp=b_exp, up_weights=up_weights, up_bias=up_bias, down_weights=down_weights, W_con=W_con, b_con=b_con, down_bias=down_bias)
    _L1_ffn_all = _L1_ffn_setup()
    _L1_ffn_in = {k: v for k, v in _L1_ffn_all.items() if k in ('W_exp', 'b_exp', 'up_weights', 'up_bias', 'down_weights', 'W_con', 'b_con', 'down_bias')}
    del _L1_ffn_all
    return {'x': x, 'ctx_1024': ctx_1024, 'L0_attn_W_in': _L0_attn_in['W_in'], 'L0_attn_W_conv': _L0_attn_in['W_conv'], 'L0_attn_b_conv': _L0_attn_in['b_conv'], 'L0_attn_W_x': _L0_attn_in['W_x'], 'L0_attn_W_dt': _L0_attn_in['W_dt'], 'L0_attn_b_dt': _L0_attn_in['b_dt'], 'L0_attn_A_log': _L0_attn_in['A_log'], 'L0_attn_D': _L0_attn_in['D'], 'L0_attn_rms_w': _L0_attn_in['rms_w'], 'L0_attn_W_out': _L0_attn_in['W_out'], 'L0_xattn_Wq': _L0_xattn_in['Wq'], 'L0_xattn_Wk': _L0_xattn_in['Wk'], 'L0_xattn_Wv': _L0_xattn_in['Wv'], 'L0_xattn_Wo': _L0_xattn_in['Wo'], 'L0_ffn_w1': _L0_ffn_in['w1'], 'L0_ffn_b1': _L0_ffn_in['b1'], 'L0_ffn_w2': _L0_ffn_in['w2'], 'L0_ffn_b2': _L0_ffn_in['b2'], 'L1_attn_Wq': _L1_attn_in['Wq'], 'L1_attn_Wk': _L1_attn_in['Wk'], 'L1_attn_Wv': _L1_attn_in['Wv'], 'L1_attn_Wa': _L1_attn_in['Wa'], 'L1_attn_ba': _L1_attn_in['ba'], 'L1_attn_Wb': _L1_attn_in['Wb'], 'L1_attn_bb': _L1_attn_in['bb'], 'L1_attn_Wg': _L1_attn_in['Wg'], 'L1_attn_bg': _L1_attn_in['bg'], 'L1_attn_WaR': _L1_attn_in['WaR'], 'L1_attn_baR': _L1_attn_in['baR'], 'L1_attn_Wo': _L1_attn_in['Wo'], 'L1_attn_ln_w': _L1_attn_in['ln_w'], 'L1_attn_ln_b': _L1_attn_in['ln_b'], 'L1_xattn_Wq': _L1_xattn_in['Wq'], 'L1_xattn_bq': _L1_xattn_in['bq'], 'L1_xattn_Wout': _L1_xattn_in['Wout'], 'L1_xattn_bout': _L1_xattn_in['bout'], 'L1_ffn_W_exp': _L1_ffn_in['W_exp'], 'L1_ffn_b_exp': _L1_ffn_in['b_exp'], 'L1_ffn_up_weights': _L1_ffn_in['up_weights'], 'L1_ffn_up_bias': _L1_ffn_in['up_bias'], 'L1_ffn_down_weights': _L1_ffn_in['down_weights'], 'L1_ffn_W_con': _L1_ffn_in['W_con'], 'L1_ffn_b_con': _L1_ffn_in['b_con'], 'L1_ffn_down_bias': _L1_ffn_in['down_bias']}

def reference(x, ctx_1024, L0_attn_W_in, L0_attn_W_conv, L0_attn_b_conv, L0_attn_W_x, L0_attn_W_dt, L0_attn_b_dt, L0_attn_A_log, L0_attn_D, L0_attn_rms_w, L0_attn_W_out, L0_xattn_Wq, L0_xattn_Wk, L0_xattn_Wv, L0_xattn_Wo, L0_ffn_w1, L0_ffn_b1, L0_ffn_w2, L0_ffn_b2, L1_attn_Wq, L1_attn_Wk, L1_attn_Wv, L1_attn_Wa, L1_attn_ba, L1_attn_Wb, L1_attn_bb, L1_attn_Wg, L1_attn_bg, L1_attn_WaR, L1_attn_baR, L1_attn_Wo, L1_attn_ln_w, L1_attn_ln_b, L1_xattn_Wq, L1_xattn_bq, L1_xattn_Wout, L1_xattn_bout, L1_ffn_W_exp, L1_ffn_b_exp, L1_ffn_up_weights, L1_ffn_up_bias, L1_ffn_down_weights, L1_ffn_W_con, L1_ffn_b_con, L1_ffn_down_bias):
    import jax
    import jax.numpy as jnp

    def _L0_attn_ref(x, W_in, W_conv, b_conv, W_x, W_dt, b_dt, A_log, D, rms_w, W_out):
        import jax, jax.numpy as jnp
        import numpy as np
        DIM = 256
        EXPAND = 2
        D_INNER = DIM * EXPAND
        D_STATE = 16
        D_CONV = 4
        DT_RANK = max(16, DIM // 16)
        BATCH = 2
        SEQ = 256
        EPS_RMS = 1e-06

        def _ssm_forward(x, W_in, W_conv, b_conv, W_x, W_dt, b_dt, A_log, D, rms_w, W_out):
            b, s, _ = x.shape
            xz = jnp.einsum('bsd,ed->bse', x, W_in)
            x_in, z = jnp.split(xz, 2, axis=-1)
            xpad = jnp.pad(x_in, ((0, 0), (D_CONV - 1, 0), (0, 0)))
            xc = b_conv
            for k in range(D_CONV):
                xc = xc + W_conv[:, k] * xpad[:, k:k + s, :]
            xc = jax.nn.silu(xc)
            dbl = jnp.einsum('bsd,ed->bse', xc, W_x)
            dt, Bm, Cm = jnp.split(dbl, [DT_RANK, DT_RANK + D_STATE], axis=-1)
            dt = jax.nn.softplus(jnp.einsum('bsr,dr->bsd', dt, W_dt) + b_dt) + 0.0001
            A = -jnp.exp(A_log)
            dA = jnp.exp(jnp.clip(dt[..., None] * A, -10.0, 10.0))
            dBu = dt[..., None] * Bm[:, :, None, :] * xc[..., None]

            def step(h, inp):
                dA_t, dBu_t, C_t = inp
                h = dA_t * h + dBu_t
                y = jnp.einsum('bdn,bn->bd', h, C_t)
                return (h, y)
            h0 = jnp.zeros((b, D_INNER, D_STATE), x.dtype)
            _, ys = jax.lax.scan(step, h0, (jnp.moveaxis(dA, 1, 0), jnp.moveaxis(dBu, 1, 0), jnp.moveaxis(Cm, 1, 0)))
            y = jnp.moveaxis(ys, 0, 1) + xc * D
            y = y * jax.nn.silu(z)
            y = y * jax.lax.rsqrt(jnp.mean(y * y, axis=-1, keepdims=True) + EPS_RMS) * rms_w
            return jnp.einsum('bse,de->bsd', y, W_out)
        return _ssm_forward(x, W_in, W_conv, b_conv, W_x, W_dt, b_dt, A_log, D, rms_w, W_out)

    def _L0_xattn_ref(query, key, value, Wq, Wk, Wv, Wo, causal):
        import jax, jax.numpy as jnp
        import numpy as np
        DIM, HEADS, DIM_HEAD, EPS = (256, 16, 64, 1e-12)

        def _phi(x):
            return jax.nn.elu(x) + 1.0
        B, L, _ = query.shape
        H, D = (HEADS, DIM_HEAD)
        q = (query @ Wq).reshape(B, L, H, D).transpose(0, 2, 1, 3)
        k = (key @ Wk).reshape(B, L, H, D).transpose(0, 2, 1, 3)
        v = (value @ Wv).reshape(B, L, H, D).transpose(0, 2, 1, 3)
        q_feat = _phi(q)
        k_feat = _phi(k)
        if causal:
            KV = jnp.cumsum(k_feat * v, axis=2)
            K_sum = jnp.cumsum(k_feat, axis=2)
            numerator = jnp.sum(q_feat * KV, axis=-1)
            denominator = jnp.clip(jnp.sum(q_feat * K_sum, axis=-1), EPS, None)
            out = v * (numerator / denominator)[..., None]
        else:
            kv_state = jnp.sum(k_feat * v, axis=2)
            k_sum = jnp.sum(k_feat, axis=2)
            numerator = jnp.einsum('bhld,bhd->bhl', q_feat, kv_state)
            denominator = jnp.clip(jnp.einsum('bhld,bhd->bhl', q_feat, k_sum), EPS, None)
            out = v * (numerator / denominator)[..., None]
        out = out.transpose(0, 2, 1, 3).reshape(B, L, H * D)
        return out @ Wo

    def _L0_ffn_ref(x, w1, b1, w2, b2):
        import jax, jax.numpy as jnp
        import numpy as np
        N_EMBD = 256
        N_STATE = 1024
        h = jax.nn.gelu(jnp.einsum('bse,eh->bsh', x, w1) + b1, approximate=False)
        return jnp.einsum('bsh,he->bse', h, w2) + b2

    def _L1_attn_ref(x, Wq, Wk, Wv, Wa, ba, Wb, bb, Wg, bg, WaR, baR, Wo, ln_w, ln_b):
        import jax, jax.numpy as jnp
        import numpy as np
        B, T, DM, H, DH = (4, 512, 256, 16, 64)
        DI = H * DH
        CLIP = 1.0
        LN_EPS = 1e-05
        Bs, Ts, _ = x.shape
        residual = x
        mu = jnp.mean(x, -1, keepdims=True)
        var = jnp.mean((x - mu) ** 2, -1, keepdims=True)
        xn = (x - mu) / jnp.sqrt(var + LN_EPS) * ln_w + ln_b
        q = (xn @ Wq.T).reshape(Bs, Ts, H, DH)
        k = (xn @ Wk.T).reshape(Bs, Ts, H, DH)
        v = (xn @ Wv.T).reshape(Bs, Ts, H, DH)
        alpha = jax.nn.sigmoid(xn @ Wa.T + ba).reshape(Bs, Ts, H, DH)
        aR = jax.nn.sigmoid(xn @ WaR.T + baR).reshape(Bs, Ts, H, DH)
        beta = jax.nn.sigmoid(xn @ Wb.T + bb)
        gamma = jax.nn.sigmoid(xn @ Wg.T + bg)
        tm = lambda a: jnp.moveaxis(a, 1, 0)
        xs = (tm(q), tm(k), tm(v), tm(alpha), tm(aR), tm(beta), tm(gamma))
        S0 = jnp.zeros((Bs, H, DH, DH), x.dtype)

        def step(carry, inp):
            S, R = carry
            q_t, k_t, v_t, a_t, aR_t, b_t, g_t = inp
            kn = k_t / jnp.maximum(jnp.linalg.norm(k_t, axis=-1, keepdims=True), 1e-12)
            pred = jnp.einsum('bhji,bhj->bhi', S, kn)
            r = jnp.clip(v_t - pred, -CLIP, CLIP)
            S = a_t[..., None] * S
            kp = jnp.einsum('bhd,bhde->bhe', kn, S)
            S = S + b_t[..., None, None] * kn[..., None] * (v_t - kp)[..., None, :]
            o = jnp.einsum('bhji,bhj->bhi', S, q_t)
            R = aR_t[..., None] * R
            kpR = jnp.einsum('bhd,bhde->bhe', kn, R)
            R = R + g_t[..., None, None] * kn[..., None] * (r - kpR)[..., None, :]
            o = o + jnp.einsum('bhji,bhj->bhi', R, q_t)
            return ((S, R), o)
        _, os = jax.lax.scan(step, (S0, S0), xs)
        out = jnp.moveaxis(os, 0, 1).reshape(Bs, Ts, DI) @ Wo.T
        return out + residual

    def _L1_xattn_ref(Q, K, V, Wq, bq, Wout, bout):
        import jax, jax.numpy as jnp
        import numpy as np
        D_MODEL = 256
        HEADS = 16
        D_HEAD = D_MODEL // HEADS
        SEQ = 512
        C = 2
        K_TOP = int(C * np.log(SEQ))
        B, L, _ = Q.shape
        q = (Q @ Wq + bq).transpose(0, 2, 1)
        k_ = (K @ Wq + bq).transpose(0, 2, 1)
        v = (V @ Wq + bq).transpose(0, 2, 1)
        Qf = jnp.fft.fft(q.astype(jnp.complex64))
        Kf = jnp.fft.fft(k_.astype(jnp.complex64))
        corr = jnp.real(jnp.fft.ifft(Qf * jnp.conj(Kf)))
        corr = corr.mean(axis=(0, 1))
        W_topk, I_topk = jax.lax.top_k(corr, K_TOP)
        W_topk = jax.nn.softmax(W_topk)

        def body(R, ws):
            w, shift = ws
            return (R + w * jnp.roll(v, -shift, axis=-1), None)
        R3, _ = jax.lax.scan(body, jnp.zeros_like(v), (W_topk, I_topk))
        R = jnp.broadcast_to(R3[:, None], (B, HEADS, D_HEAD, L)).reshape(B, L, HEADS * D_HEAD)
        return R @ Wout + bout

    def _L1_ffn_ref(x, W_exp, b_exp, up_weights, up_bias, down_weights, W_con, b_con, down_bias):
        import jax, jax.numpy as jnp
        import numpy as np
        D_MODEL = 256
        EXPANSION = 4
        D_HIDDEN = D_MODEL * EXPANSION
        NUM_STAGES = int(np.log2(D_HIDDEN))

        def butterfly(y, weights, dim):
            lead = y.shape[:-1]
            for stage in range(weights.shape[0]):
                s = 2 ** stage
                nb = dim // (2 * s)
                yr = y.reshape(*lead, nb, 2, s)
                a = yr[..., 0, :]
                b = yr[..., 1, :]
                w = weights[stage].reshape(nb, s, 2, 2)
                na = w[..., 0, 0] * a + w[..., 0, 1] * b
                nb2 = w[..., 1, 0] * a + w[..., 1, 1] * b
                y = jnp.stack([na, nb2], axis=-2).reshape(*lead, dim)
            return y
        h = jnp.einsum('bsd,dh->bsh', x, W_exp) + b_exp
        h = butterfly(h, up_weights, D_HIDDEN)
        h = jax.nn.gelu(h + up_bias, approximate=False)
        h = butterfly(h, down_weights, D_HIDDEN)
        y = jnp.einsum('bsh,hd->bsd', h, W_con) + b_con
        return y + down_bias
    x = x + _L0_attn_ref(_layernorm(x, axis=-1), L0_attn_W_in, L0_attn_W_conv, L0_attn_b_conv, L0_attn_W_x, L0_attn_W_dt, L0_attn_b_dt, L0_attn_A_log, L0_attn_D, L0_attn_rms_w, L0_attn_W_out)
    x = x + _L0_xattn_ref(_layernorm(x, axis=-1), ctx_1024, ctx_1024, L0_xattn_Wq, L0_xattn_Wk, L0_xattn_Wv, L0_xattn_Wo, 1)
    x = x + _L0_ffn_ref(_layernorm(x, axis=-1), L0_ffn_w1, L0_ffn_b1, L0_ffn_w2, L0_ffn_b2)
    x = x + _L1_attn_ref(_layernorm(x, axis=-1), L1_attn_Wq, L1_attn_Wk, L1_attn_Wv, L1_attn_Wa, L1_attn_ba, L1_attn_Wb, L1_attn_bb, L1_attn_Wg, L1_attn_bg, L1_attn_WaR, L1_attn_baR, L1_attn_Wo, L1_attn_ln_w, L1_attn_ln_b)
    x = x + _L1_xattn_ref(_layernorm(x, axis=-1), ctx_1024, ctx_1024, L1_xattn_Wq, L1_xattn_bq, L1_xattn_Wout, L1_xattn_bout)
    x = x + _L1_ffn_ref(_layernorm(x, axis=-1), L1_ffn_W_exp, L1_ffn_b_exp, L1_ffn_up_weights, L1_ffn_up_bias, L1_ffn_down_weights, L1_ffn_W_con, L1_ffn_b_con, L1_ffn_down_bias)
    return x

_drawn_inputs = setup_inputs


def setup_inputs(seed=0):
    import zlib

    import numpy as np

    out = dict(_drawn_inputs(seed))
    spreads = {'L0_attn_D': (0.10000000149011612, 0.2),
     'L0_attn_rms_w': (1.0, 0.2),
     'L1_attn_ba': (3.0, 0.2),
     'L1_attn_bb': (0.0, 0.559),
     'L1_attn_bg': (0.0, 0.583),
     'L1_attn_baR': (3.0, 0.2),
     'L1_attn_ln_w': (1.0, 0.2),
     'L1_attn_ln_b': (0.0, 0.1),
     'L1_xattn_bq': (0.0, 0.8),
     'L1_xattn_bout': (0.0, 0.1),
     'L1_ffn_b_exp': (0.0, 0.1),
     'L1_ffn_up_bias': (0.0, 0.1),
     'L1_ffn_b_con': (0.0, 0.1),
     'L1_ffn_down_bias': (0.0, 0.1)}
    factors = {'L0_attn_W_x': 8.0,
     'L0_attn_W_dt': 64.0,
     'L0_attn_b_dt': 8.0,
     'L0_attn_A_log': 72.88,
     'L0_xattn_Wk': 4.03,
     'L0_ffn_b1': 3.836,
     'L1_xattn_Wq': 2.672}
    for name, (base, spread) in spreads.items():
        noise = np.random.default_rng([zlib.crc32(name.encode()), seed]).standard_normal(out[name].shape)
        drawn = base * np.exp(spread * noise) if base else spread * noise
        out[name] = jnp.asarray(drawn.astype(out[name].dtype))
    for name, factor in factors.items():
        out[name] = (out[name] * factor).astype(out[name].dtype)
    return out
```

```python
from contextlib import ExitStack

import numpy as np

import concourse.bass as bass
from concourse import mybir
from concourse.alu_op_type import AluOpType as ALU

F32 = mybir.dt.float32
ACT = mybir.ActivationFunctionType
AX = mybir.AxisListType

P = 128
B, T, D = 8, 512, 256
DT = D // P
DI, NS, DC, RK = 512, 16, 4, 16
IT = DI // P
H, DH = 16, 64
HP = H // 2
FF = 1024
FT = FF // P
E10 = float(np.exp(-10.0))


class Signal:

    def __init__(self, signals, nc, name, per=1, step=1):
        self.sem = nc.alloc_semaphore(name)
        signals.append(self.sem)
        self.per, self.step = per, step

    def __call__(self, turn, k):
        return self.sem, turn * (self.per * self.step) + k * self.step


class Chain:

    def __init__(self, links, eng, turn):
        self.links, self.eng, self.turn, self.count = links, eng, turn, 0

    def link(self, ins):
        self.count += 1
        ins.then_inc(self.links.sem, 1)
        self.eng.wait_ge(*self.links(self.turn, self.count))

    def close(self):
        assert self.count == self.links.per, (self.links.sem.name, self.count)


def wide(ap, n):
    return ap.unsqueeze(1).broadcast_to([ap.shape[0], n, ap.shape[1]])


def layer0(nc, io, scratch):
    signals = []
    with ExitStack() as ctx:
        def sb(name, *shape):
            return ctx.enter_context(nc.sbuf_tensor("a_" + name, list(shape), F32))

        def sig(name, per=1, step=1):
            return Signal(signals, nc, "a_" + name, per, step)

        ps = [ctx.enter_context(nc.psum_tensor(f"a_bank{i}", [P, T], F32)) for i in range(8)]

        load_list = []

        def const(name, src, *shape):
            t = sb(name, *shape)
            load_list.append((t[tuple(slice(None) for _ in shape)], src))
            return t

        def fm(name, k):
            return io[name].rearrange("(k p) n -> p k n", p=P)

        def vec(name):
            return io[name].unsqueeze(2)

        mean_d = const("mean_d", io["c_mean_d"], P, P)
        mean_di = const("mean_di", io["c_mean_di"], P, P)
        pair_sum = const("pair_sum", io["c_pair"], P, P)
        ident = const("ident", io["c_ident"], P, P)
        sel = const("sel", io["c_sel"].rearrange("p (n m) -> p n m", m=P), 48, 2 * NS, P)
        w_in = const("w_in", fm("w_in", DT), P, DT, 2 * DI)
        w_x = const("w_x", fm("w_x", IT), P, IT, 48)
        w_dt = const("w_dt", io["w_dt"], RK, DI)
        w_out = const("w_out", fm("w_out", IT), P, IT, D)
        w_q = const("w_q", fm("w_q", DT), P, DT, H * DH)
        w_k = const("w_k", fm("w_k", DT), P, DT, H * DH)
        w_v = const("w_v", fm("w_v", DT), P, DT, H * DH)
        w_o = const("w_o", fm("w_o", HP), P, HP, D)
        w_1 = const("w_1", fm("w_1", DT), P, DT, FF)
        w_2 = const("w_2", fm("w_2", FT), P, FT, D)
        w_bg = const("w_bg", io["w_bg"].rearrange("(k p) n -> p k n", p=P), P, DT, 2 * H)
        conv_w = const("conv_w", fm("conv_w", IT), P, IT, DC)
        conv_b = const("conv_b", vec("conv_b"), P, IT, 1)
        b_dt = const("b_dt", vec("b_dt"), P, IT, 1)
        a_log = const("a_log", fm("a_log", IT), P, IT, NS)
        skip_d = const("skip_d", vec("skip_d"), P, IT, 1)
        rms_w = const("rms_w", vec("rms_w"), P, IT, 1)
        b_1 = const("b_1", vec("b_1"), P, FT, 1)
        b_2 = const("b_2", vec("b_2"), P, DT, 1)
        b_bg = const("b_bg", io["b_bg"], H, 2)
        ln_w = const("ln_w", vec("ln_w"), P, DT, 1)
        ln_b = const("ln_b", vec("ln_b"), P, DT, 1)

        a_neg = sb("a_neg", P, IT, NS)
        nb_bg = sb("nb_bg", H, 2)
        eps = sb("eps", P, 2)
        ones = sb("ones", P, T)
        x = sb("x", P, DT, T)
        cx = sb("cx", P, DT, T)
        cen = sb("cen", P, DT, T)
        sq = sb("sq", P, DT, T)
        xn = sb("xn", P, DT, T)
        xl = sb("xl", P, DT, T)
        lnv = sb("lnv", P, T)
        rstd = sb("rstd", P, T)
        bg = sb("bg", H, 2, T)
        xpad = sb("xpad", P, IT, T + DC - 1)
        zs = sb("zs", P, IT, T)
        e1 = sb("e1", P, IT, T)
        e2 = sb("e2", P, IT, T)
        cv = sb("cv", P, IT, T)
        dbl = sb("dbl", 48, T)
        dt = sb("dt", P, IT, T)
        u = sb("u", P, IT, T)
        da = sb("da", P, 2, IT, T)
        hs = sb("hs", P, 2, IT, T)
        bu = e1
        y = e2
        cv_x = cv
        rl = xpad[:, :, DC - 1:]
        eqk = hs
        vs = zs
        qf, kf, kvp, kvs, kss = (u[:, 0, :], u[:, 1, :], u[:, 2, :], u[:, 3, :], dt[:, 0, :])
        rt, tt = dt[:, 1, :], dt[:, 2, :]
        prod = cv
        ov = da[:, :, :, :].rearrange("p a b t -> p (a b) t")
        hid = hs[:, :, :, :].rearrange("p a b t -> p (a b) t")

        n_load = len(load_list)
        consts_in, setup = sig("consts_in", n_load, 16), sig("setup", 6)
        a_capped, setup_act = sig("a_capped"), sig("setup_act")
        x_in, saved = sig("x_in", 2, 16), sig("saved", 4, 16)
        ln_mean, ln_cent, ln_sq, ln_var, ln_log, ln_rstd, ln_out = [
            sig(n, 5) for n in ("ln_mean", "ln_cent", "ln_sq", "ln_var", "ln_log", "ln_rstd", "ln_out")]
        xz, xin, zgate, conv = sig("xz", 8), sig("xin", IT), sig("zgate", IT), sig("conv", IT)
        xcv, dbl_ps, dbl_sb, dtp = sig("xcv", IT), sig("dbl_ps"), sig("dbl_sb"), sig("dtp", IT)
        dt_pre, spl, dt_ready, u_ready = sig("dt_pre"), sig("spl"), sig("dt_ready"), sig("u_ready")
        bn, cn, daexp, damax = sig("bn", NS), sig("cn", NS), sig("daexp", NS), sig("damax", NS)
        bu_ready, scanned, yn, yacc = sig("bu_ready", NS), sig("scanned", NS), sig("yn", NS), sig("yacc", NS)
        ygate, ysq, yvar, yrstd, ynorm, a_out = [sig(n) for n in ("ygate", "ysq", "yvar", "yrstd", "ynorm", "a_out")]
        x_a, x_b, x_c, x_d = [sig(n) for n in ("x_a", "x_b", "x_c", "x_d")]
        qkv, aqkv, emin, feat, prods, nd, ratio, ovs = [
            sig(n, HP) for n in ("qkv", "aqkv", "emin", "feat", "prods", "nd", "ratio", "ovs")]
        b_out, hid_ps, hid_sb, c_out = sig("b_out"), sig("hid_ps", FT), sig("hid_sb", FT), sig("c_out")
        gate_ps, gate_exp, gates = sig("gate_ps"), sig("gate_exp"), sig("gates")
        dve_links, act_links = sig("dve_links", 41), sig("act_links", 3)

        pool_turns, sp_turns = sig("pool_turns"), sig("sp_turns")

        block = ctx.enter_context(nc.Block())

        @block.sync
        def _(sp):
            for dst, src in load_list:
                sp.dma_start(dst, src).then_inc(consts_in.sem, 16)
            with sp.Fori(0, B) as b:
                sp.dma_start(x[:, :, :], io["x"].rearrange("(k p) t -> p k t", p=P)[:, :, bass.ds(b * T, T)]).then_inc(x_in.sem, 16)
                sp.dma_start(cx[:, :, :], io["ctx"].rearrange("(k p) t -> p k t", p=P)[:, :, bass.ds(b * T, T)]).then_inc(x_in.sem, 16)
                sp.wait_ge(*x_d(b, 1))
                sp.dma_start(scratch["x"].rearrange("(k p) t -> p k t", p=P)[:, :, bass.ds(b * T, T)], x[:, :, :]).then_inc(saved.sem, 16)
                sp.wait_ge(*ln_out(b, 5))
                sp.dma_start(scratch["x2"].rearrange("(k p) t -> p k t", p=P)[:, :, bass.ds(b * T, T)], xn[:, :, :]).then_inc(saved.sem, 16)
                sp.wait_ge(*gates(b, 1))
                for g, name in enumerate(("beta", "gamma")):
                    sp.dma_start(scratch[name][:, bass.ds(b * T, T)], bg[:, g, :]).then_inc(saved.sem, 16)
                sp.wait_ge(*saved(b, 4))
                sp.sem_inc(sp_turns.sem, 1)

        @block.tensor
        def _(pe):
            mm = pe.matmul

            def norm(b, k, src):
                for j in range(DT):
                    i = mm(ps[0][:, :], mean_d[:, :], src[:, j, :], start=(j == 0), stop=(j == DT - 1))
                i.then_inc(ln_mean.sem, 1)
                pe.wait_ge(*ln_sq(b, k))
                for j in range(DT):
                    i = mm(ps[1][:, :], mean_d[:, :], sq[:, j, :], start=(j == 0), stop=(j == DT - 1))
                i.then_inc(ln_var.sem, 1)

            pe.wait_ge(*consts_in(0, n_load))
            with pe.Fori(0, B) as b:
                pe.wait_ge(*x_in(b, 2))
                norm(b, 1, x)
                pe.wait_ge(*ln_out(b, 1))
                for m in range(2 * IT):
                    for k in range(DT):
                        i = mm(ps[m][:, :], w_in[:, k, m * P:(m + 1) * P], xn[:, k, :], start=(k == 0), stop=(k == DT - 1))
                    i.then_inc(xz.sem, 1)
                pe.wait_ge(*xcv(b, IT))
                for k in range(IT):
                    i = mm(ps[0][0:48, :], w_x[:, k, :], cv_x[:, k, :], start=(k == 0), stop=(k == IT - 1))
                i.then_inc(dbl_ps.sem, 1)
                pe.wait_ge(*dbl_sb(b, 1))
                for m in range(IT):
                    mm(ps[1 + m][:, :], w_dt[:, m * P:(m + 1) * P], dbl[0:RK, :], start=True, stop=True).then_inc(dtp.sem, 1)
                pe.wait_ge(*dt_ready(b, 1))

                def spread(n):
                    if n >= 2:
                        pe.wait_ge(*bu_ready(b, n - 1))
                    mm(ps[n % 2][:, :], sel[:, n, :], dbl[:, :], start=True, stop=True).then_inc(bn.sem, 1)
                    if n >= 2:
                        pe.wait_ge(*yn(b, n - 1))
                    mm(ps[2 + n % 2][:, :], sel[:, NS + n, :], dbl[:, :], start=True, stop=True).then_inc(cn.sem, 1)

                spread(0)
                for n in range(NS):
                    if n + 1 < NS:
                        spread(n + 1)
                    pe.wait_ge(*yn(b, n + 1))
                    for m in range(IT):
                        i = mm(ps[4 + m][:, :], ident[:, :], hs[:, n % 2, m, :], start=(n == 0), stop=(n == NS - 1))
                    i.then_inc(yacc.sem, 1)
                pe.wait_ge(*ysq(b, 1))
                for m in range(IT):
                    i = mm(ps[0][:, :], mean_di[:, :], u[:, m, :], start=(m == 0), stop=(m == IT - 1))
                i.then_inc(yvar.sem, 1)
                pe.wait_ge(*ynorm(b, 1))
                for m in range(DT):
                    for k in range(IT):
                        i = mm(ps[1 + m][:, :], w_out[:, k, m * P:(m + 1) * P], y[:, k, :], start=(k == 0), stop=(k == IT - 1))
                i.then_inc(a_out.sem, 1)

                pe.wait_ge(*x_a(b, 1))
                norm(b, 2, x)
                pe.wait_ge(*ln_out(b, 2))

                def project(hp):
                    s = 3 * (hp % 2)
                    if hp >= 2:
                        pe.wait_ge(*feat(b, hp - 1))
                        pe.wait_ge(*aqkv(b, hp - 1))
                    for o, w, src in ((0, w_q, xn), (1, w_k, cx), (2, w_v, cx)):
                        for k in range(DT):
                            i = mm(ps[s + o][:, :], w[:, k, hp * P:(hp + 1) * P], src[:, k, :], start=(k == 0), stop=(k == DT - 1))
                    i.then_inc(qkv.sem, 1)

                project(0)
                for hp in range(HP):
                    if hp + 1 < HP:
                        project(hp + 1)
                    pe.wait_ge(*prods(b, hp + 1))
                    if hp >= 1:
                        pe.wait_ge(*ratio(b, hp))
                    mm(ps[6][:, :], pair_sum[:, :], prod[:, 2 * (hp % 2), :], start=True, stop=True)
                    mm(ps[7][:, :], pair_sum[:, :], prod[:, 2 * (hp % 2) + 1, :], start=True, stop=True).then_inc(nd.sem, 1)
                pe.wait_ge(*ovs(b, HP))
                for m in range(DT):
                    for k in range(HP):
                        i = mm(ps[m][:, :], w_o[:, k, m * P:(m + 1) * P], ov[:, k, :], start=(k == 0), stop=(k == HP - 1))
                i.then_inc(b_out.sem, 1)

                pe.wait_ge(*x_b(b, 1))
                norm(b, 3, x)
                pe.wait_ge(*ln_out(b, 3))
                for m in range(FT):
                    for k in range(DT):
                        i = mm(ps[m][:, :], w_1[:, k, m * P:(m + 1) * P], xn[:, k, :], start=(k == 0), stop=(k == DT - 1))
                    i.then_inc(hid_ps.sem, 1)
                pe.wait_ge(*hid_sb(b, 2))
                for k in range(FT):
                    pe.wait_ge(*hid_sb(b, k + 1))
                    for m in range(DT):
                        i = mm(ps[m][:, :], w_2[:, k, m * P:(m + 1) * P], hid[:, k, :], start=(k == 0), stop=(k == FT - 1))
                i.then_inc(c_out.sem, 1)

                pe.wait_ge(*x_c(b, 1))
                norm(b, 4, x)
                pe.wait_ge(*ln_out(b, 4))
                norm(b, 5, xl)
                pe.wait_ge(*ln_out(b, 5))
                for g in range(2):
                    for k in range(DT):
                        i = mm(ps[g][0:H, :], w_bg[:, k, g * H:(g + 1) * H], xn[:, k, :], start=(k == 0), stop=(k == DT - 1))
                i.then_inc(gate_ps.sem, 1)

        @block.scalar
        def _(act):
            A = act.activation

            def norm(b, k, links):
                act.wait_ge(*ln_cent(b, k))
                A(sq[:, :, :], cen[:, :, :], ACT.Square).then_inc(ln_sq.sem, 1)
                act.wait_ge(*ln_var(b, k))
                A(lnv[:, :], ps[1][:, :], ACT.Ln, bias=eps[:, 0:1]).then_inc(ln_log.sem, 1)
                act.wait_ge(*ln_log(b, k))
                A(rstd[:, :], lnv[:, :], ACT.Exp, scale=-0.5).then_inc(ln_rstd.sem, 1)

            act.wait_ge(*consts_in(0, n_load))
            act.wait_ge(*a_capped(0, 1))
            A(a_neg[:, :, :], a_neg[:, :, :], ACT.Exp).then_inc(setup_act.sem, 1)
            act.wait_ge(*setup(0, 6))
            with act.Fori(0, B) as b:
                ch = Chain(act_links, act, b)
                norm(b, 1, ch)
                for m in range(IT):
                    act.wait_ge(*xz(b, m + 1))
                    A(xpad[:, m, DC - 1:], ps[m][:, :], ACT.Copy).then_inc(xin.sem, 1)
                for m in range(IT):
                    act.wait_ge(*xz(b, IT + m + 1))
                    A(zs[:, m, :], ps[IT + m][:, :], ACT.Silu).then_inc(zgate.sem, 1)
                for m in range(IT):
                    act.wait_ge(*conv(b, m + 1))
                    A(cv_x[:, m, :], cv[:, m, :], ACT.Silu).then_inc(xcv.sem, 1)
                act.wait_ge(*dbl_ps(b, 1))
                A(dbl[:, :], ps[0][0:48, :], ACT.Copy).then_inc(dbl_sb.sem, 1)
                act.wait_ge(*dt_pre(b, 1))
                ch.link(A(e1[:, :, :], rl, ACT.Abs))
                i = A(e1[:, :, :], e1[:, :, :], ACT.Exp, scale=-1.0)
                ch.link(i)
                A(e1[:, :, :], e1[:, :, :], ACT.Ln, bias=1.0).then_inc(spl.sem, 1)
                act.wait_ge(*dt_ready(b, 1))
                for n in range(NS):
                    if n >= 2:
                        act.wait_ge(*scanned(b, n - 1))
                    for m in range(IT):
                        i = A(da[:, n % 2, m, 1:T], dt[:, m, 1:T], ACT.Exp, scale=a_neg[:, m, n:n + 1])
                    i.then_inc(daexp.sem, 1)
                act.wait_ge(*ygate(b, 1))
                A(u[:, :, :], y[:, :, :], ACT.Square).then_inc(ysq.sem, 1)
                act.wait_ge(*yvar(b, 1))
                i = A(lnv[:, :], ps[0][:, :], ACT.Ln, bias=eps[:, 1:2])
                ch.link(i)
                A(rstd[:, :], lnv[:, :], ACT.Exp, scale=-0.5).then_inc(yrstd.sem, 1)
                norm(b, 2, ch)
                for hp in range(HP):
                    s = hp % 2
                    act.wait_ge(*qkv(b, hp + 1))
                    if hp >= 2:
                        act.wait_ge(*feat(b, hp - 1))
                        act.wait_ge(*ovs(b, hp - 1))
                    A(eqk[:, s, 0, :], ps[3 * s][:, :], ACT.Exp)
                    A(eqk[:, s, 1, :], ps[3 * s + 1][:, :], ACT.Exp)
                    A(vs[:, s, :], ps[3 * s + 2][:, :], ACT.Copy).then_inc(aqkv.sem, 1)
                norm(b, 3, ch)
                for m in range(FT):
                    act.wait_ge(*hid_ps(b, m + 1))
                    A(hid[:, m, :], ps[m][:, :], ACT.Gelu, bias=b_1[:, m, :]).then_inc(hid_sb.sem, 1)
                norm(b, 4, ch)
                norm(b, 5, ch)
                act.wait_ge(*gate_ps(b, 1))
                for g in range(2):
                    i = A(bg[:, g, :], ps[g][0:H, :], ACT.Exp, scale=-1.0, bias=nb_bg[:, g:g + 1])
                i.then_inc(gate_exp.sem, 1)
                ch.close()

        @block.gpsimd
        def _(pool):
            with pool.Fori(0, B) as b:
                for n in range(NS):
                    pool.wait_ge(*daexp(b, n + 1))
                    pool.sem_inc(pool_turns.sem, 1)
                    pool.tensor_scalar(da[:, n % 2, :, 1:T], da[:, n % 2, :, 1:T], E10, None, ALU.max).then_inc(damax.sem, 1)
                for hp in range(HP):
                    pool.wait_ge(*aqkv(b, hp + 1))
                    pool.sem_inc(pool_turns.sem, 1)
                    pool.tensor_scalar(eqk[:, hp % 2, 0:2, :], eqk[:, hp % 2, 0:2, :], 1.0, None, ALU.min).then_inc(emin.sem, 1)

        @block.vector
        def _(dve):
            dve.memset(xpad[:, :, 0:DC - 1], 0.0).then_inc(setup.sem, 1)
            dve.memset(ones[:, :], 1.0).then_inc(setup.sem, 1)
            dve.memset(eps[:, 0:1], 1e-5).then_inc(setup.sem, 1)
            dve.memset(eps[:, 1:2], 1e-6).then_inc(setup.sem, 1)
            dve.wait_ge(*consts_in(0, n_load))
            dve.tensor_scalar(nb_bg[:, :], b_bg[:, :], -1.0, None, ALU.mult).then_inc(setup.sem, 1)
            dve.tensor_scalar(a_neg[:, :, :], a_log[:, :, :], 14.0, None, ALU.min).then_inc(a_capped.sem, 1)
            dve.wait_ge(*setup_act(0, 1))
            dve.tensor_scalar(a_neg[:, :, :], a_neg[:, :, :], -1.0, None, ALU.mult).then_inc(setup.sem, 1)
            dve.wait_ge(*setup(0, 6))

            def norm(b, k, src, out):
                dve.wait_ge(*ln_mean(b, k))
                dve.tensor_tensor(cen[:, :, :], src[:, :, :], wide(ps[0][:, :], DT), ALU.subtract).then_inc(ln_cent.sem, 1)
                dve.wait_ge(*ln_rstd(b, k))
                return dve.tensor_tensor(out[:, :, :], cen[:, :, :], wide(rstd[:, :], DT), ALU.mult)

            with dve.Fori(0, B) as b:
                ch = Chain(dve_links, dve, b)
                norm(b, 1, x, xn).then_inc(ln_out.sem, 1)
                for m in range(IT):
                    dve.wait_ge(*xin(b, m + 1))
                    ch.link(dve.tensor_scalar(cv[:, m, :], xpad[:, m, 0:T], conv_w[:, m, 0:1], conv_b[:, m, :], ALU.mult, ALU.add))
                    for k in range(1, DC):
                        i = dve.scalar_tensor_tensor(cv[:, m, :], xpad[:, m, k:k + T], conv_w[:, m, k:k + 1], cv[:, m, :], ALU.mult, ALU.add)
                        if k < DC - 1:
                            ch.link(i)
                    i.then_inc(conv.sem, 1)
                dve.wait_ge(*xcv(b, IT))
                for m in range(IT):
                    dve.wait_ge(*dtp(b, m + 1))
                    i = dve.tensor_scalar(rl[:, m, :], ps[1 + m][:, :], b_dt[:, m, :], None, ALU.add)
                i.then_inc(dt_pre.sem, 1)
                dve.wait_ge(*spl(b, 1))
                ch.link(dve.scalar_tensor_tensor(dt[:, :, :], rl, 0.0, e1[:, :, :], ALU.max, ALU.add))
                dve.tensor_scalar(dt[:, :, :], dt[:, :, :], 1e-4, None, ALU.add).then_inc(dt_ready.sem, 1)
                dve.wait_ge(*dt_ready(b, 1))
                dve.tensor_tensor(u[:, :, :], dt[:, :, :], cv_x[:, :, :], ALU.mult).then_inc(u_ready.sem, 1)
                dve.wait_ge(*u_ready(b, 1))
                ch.link(dve.memset(da[:, :, :, 0:1], 0.0))
                for n in range(NS):
                    dve.wait_ge(*bn(b, n + 1))
                    if n >= 1:
                        dve.wait_ge(*scanned(b, n))
                    dve.tensor_tensor(bu[:, :, :], u[:, :, :], wide(ps[n % 2][:, :], IT), ALU.mult).then_inc(bu_ready.sem, 1)
                    dve.wait_ge(*bu_ready(b, n + 1))
                    dve.wait_ge(*damax(b, n + 1))
                    if n >= 2:
                        dve.wait_ge(*yacc(b, n - 1))
                    dve.tensor_tensor_scan(hs[:, n % 2, :, :].rearrange("p m t -> p (m t)"),
                                           da[:, n % 2, :, :].rearrange("p m t -> p (m t)"),
                                           bu[:, :, :].rearrange("p m t -> p (m t)"), 0.0, ALU.mult, ALU.add).then_inc(scanned.sem, 1)
                    dve.wait_ge(*scanned(b, n + 1))
                    dve.wait_ge(*cn(b, n + 1))
                    dve.tensor_tensor(hs[:, n % 2, :, :], hs[:, n % 2, :, :], wide(ps[2 + n % 2][:, :], IT), ALU.mult).then_inc(yn.sem, 1)
                dve.wait_ge(*yacc(b, NS))
                for m in range(IT):
                    i = dve.scalar_tensor_tensor(y[:, m, :], cv_x[:, m, :], skip_d[:, m, :], ps[4 + m][:, :], ALU.mult, ALU.add)
                ch.link(i)
                dve.wait_ge(*zgate(b, IT))
                dve.tensor_tensor(y[:, :, :], y[:, :, :], zs[:, :, :], ALU.mult).then_inc(ygate.sem, 1)
                dve.wait_ge(*ygate(b, 1))
                dve.wait_ge(*yrstd(b, 1))
                for m in range(IT):
                    i = dve.scalar_tensor_tensor(y[:, m, :], y[:, m, :], rms_w[:, m, :], rstd[:, :], ALU.mult, ALU.mult)
                i.then_inc(ynorm.sem, 1)
                dve.wait_ge(*a_out(b, 1))
                for m in range(DT):
                    i = dve.tensor_tensor(x[:, m, :], x[:, m, :], ps[1 + m][:, :], ALU.add)
                i.then_inc(x_a.sem, 1)

                dve.wait_ge(*x_a(b, 1))
                norm(b, 2, x, xn).then_inc(ln_out.sem, 1)

                def finish(hp):
                    dve.wait_ge(*nd(b, hp + 1))
                    ch.link(dve.reciprocal(rt, ps[7][:, :]))
                    dve.scalar_tensor_tensor(tt, rt, 1e12, ps[6][:, :], ALU.min, ALU.mult).then_inc(ratio.sem, 1)
                    dve.wait_ge(*ratio(b, hp + 1))
                    dve.tensor_tensor(ov[:, hp, :], tt, vs[:, hp % 2, :], ALU.mult).then_inc(ovs.sem, 1)

                for hp in range(HP):
                    s = hp % 2
                    dve.wait_ge(*emin(b, hp + 1))
                    dve.scalar_tensor_tensor(qf, ps[3 * s][:, :], 0.0, eqk[:, s, 0, :], ALU.max, ALU.add)
                    dve.scalar_tensor_tensor(kf, ps[3 * s + 1][:, :], 0.0, eqk[:, s, 1, :], ALU.max, ALU.add).then_inc(feat.sem, 1)
                    dve.wait_ge(*feat(b, hp + 1))
                    ch.link(dve.tensor_tensor(kvp, kf, vs[:, s, :], ALU.mult))
                    dve.tensor_tensor_scan(kvs, ones[:, :], kvp, 0.0, ALU.mult, ALU.add)
                    ch.link(dve.tensor_tensor_scan(kss, ones[:, :], kf, 0.0, ALU.mult, ALU.add))
                    if hp >= 2:
                        dve.wait_ge(*nd(b, hp - 1))
                    dve.tensor_tensor(prod[:, 2 * s, :], qf, kvs, ALU.mult)
                    dve.tensor_tensor(prod[:, 2 * s + 1, :], qf, kss, ALU.mult).then_inc(prods.sem, 1)
                    dve.wait_ge(*prods(b, hp + 1))
                    if hp >= 1:
                        finish(hp - 1)
                finish(HP - 1)
                dve.wait_ge(*b_out(b, 1))
                for m in range(DT):
                    i = dve.tensor_tensor(x[:, m, :], x[:, m, :], ps[m][:, :], ALU.add)
                i.then_inc(x_b.sem, 1)

                dve.wait_ge(*x_b(b, 1))
                norm(b, 3, x, xn).then_inc(ln_out.sem, 1)
                dve.wait_ge(*c_out(b, 1))
                for m in range(DT):
                    i = dve.scalar_tensor_tensor(x[:, m, :], ps[m][:, :], b_2[:, m, :], x[:, m, :], ALU.add, ALU.add)
                i.then_inc(x_c.sem, 1)

                dve.wait_ge(*x_c(b, 1))
                norm(b, 4, x, xl).then_inc(ln_out.sem, 1)
                dve.wait_ge(*ln_out(b, 4))
                dve.tensor_tensor(x[:, :, :], x[:, :, :], xl[:, :, :], ALU.add).then_inc(x_d.sem, 1)
                ch.link(norm(b, 5, xl, xn))
                for m in range(DT):
                    i = dve.tensor_scalar(xn[:, m, :], xn[:, m, :], ln_w[:, m, :], ln_b[:, m, :], ALU.mult, ALU.add)
                i.then_inc(ln_out.sem, 1)
                dve.wait_ge(*gate_exp(b, 1))
                ch.link(dve.tensor_scalar(bg[:, :, :], bg[:, :, :], 1.0, None, ALU.add))
                dve.reciprocal(bg[:, :, :], bg[:, :, :]).then_inc(gates.sem, 1)
                ch.close()
    return signals


def delta_rule(nc, io, scratch):
    C = 32
    QB = P // C
    GB = 4
    GT = GB * T
    U_ = GT // P
    UB = T // P
    NC_ = T // C
    PASSES = 2
    LMAX = 85.0

    signals = []
    with ExitStack() as ctx:
        def sb(name, *shape):
            return ctx.enter_context(nc.sbuf_tensor("d_" + name, list(shape), F32))

        def sig(name, per=1, step=1):
            return Signal(signals, nc, "d_" + name, per, step)

        ps = [ctx.enter_context(nc.psum_tensor(f"d_bank{i}", [P, T], F32)) for i in range(8)]
        pair_sum = sb("pair_sum", P, P)
        ident = sb("ident", P, P)
        ident2 = sb("ident2", P, DH)
        masks = sb("masks", P, 3, P)
        restart = sb("restart", P, T)
        w = sb("w", P, DT, 5, P)
        nba = sb("nba", P, 2)
        gate = sb("gate", P, PASSES, C)
        gend = sb("gend", P, U_ * QB)
        kn = sb("kn", P, GT)
        q = sb("q", P, GT)
        L = [sb("L0", P, GT), sb("L1", P, GT)]
        v = sb("v", P, GT)
        o = L[0]
        mov = sb("mov", P, 3, GT)
        km = sb("km", P, GT)
        apm = sb("apm", P, 2 * U_, 3, P)
        tok = sb("tok", P, U_, 4, DH)
        ke = sb("ke", P, U_, P)
        z = sb("z", P, U_, 4 * DH)
        xg = z[:, :, :].rearrange("p u n -> p (u n)").rearrange("p (k t) -> p k t", k=DT)
        state = sb("state", P, NC_ + 1, GB, DH)
        inv = state[:, :, :, :].rearrange("p c b d -> p (c b d)")
        ni = inv[:, 0:C * C].rearrange("p (s t) -> p s t", s=C)
        xi = inv[:, C * C:2 * C * C].rearrange("p (s t) -> p s t", s=C)
        pr = inv[:, 2 * C * C:3 * C * C]
        phi = sb("phi", P, NC_, GB, DH)
        tmp = phi[:, :, :, :].rearrange("p c b d -> p (c b d)")
        ksq, rn, gm, kend = [tmp[:, n * T:(n + 1) * T] for n in range(4)]
        gp = tmp[:, 4 * T:4 * T + NC_ * (C + 1)].rearrange("p (c t) -> p c t", t=C + 1)

        loads = [(pair_sum[:, :], io["c_pair"]), (ident[:, :], io["c_ident"]), (ident2[:, :], io["c_ident2"]),
                 (masks[:, :, :], io["c_masks"].rearrange("p (m t) -> p m t", m=3)), (restart[:, :], io["c_restart"])]
        consts_in = sig("consts_in", len(loads), 16)
        inputs_in = sig("inputs_in", 7, 16)
        stored = sig("stored", 1, 16)
        neg_ba = sig("neg_ba")
        proj, ksq_r, ss, ssc, rn_r, kn_r = [sig(n, GB) for n in ("proj", "ksq", "ss", "ssc", "rn", "kn")]
        la, lsum, lcap, qv_r = sig("la", GB), sig("lsum", GB), sig("lcap", GB), sig("qv")
        gexp, kpm, kend_r, movs = [sig(n, PASSES * GB) for n in ("gexp", "kpm", "kend", "movs")]
        tr, tr_sb = sig("tr", PASSES * GB), sig("tr_sb", PASSES * GB)
        score, score_sb = sig("score", PASSES * 2 * U_), sig("score_sb", PASSES * 2 * U_)
        nt_out, nt_in, x_out, x_back = [sig(n, PASSES * k, 16) for n, k in (("nt_out", QB), ("nt_in", 1), ("x_out", 1), ("x_back", QB))]
        xi_r = sig("xi", PASSES)
        zp, z_sb = sig("zp", PASSES * U_ // 2), sig("z_sb", PASSES * U_ // 2)
        px, px_sb = sig("px", PASSES * U_ // 2), sig("px_sb", PASSES * U_ // 2)
        pp, phi_sb, psi_sb = [sig(n, PASSES * GB) for n in ("pp", "phi_sb", "psi_sb")]
        phi_diag, state0 = sig("phi_diag", PASSES), sig("state0", PASSES)
        step_ps, step_sb = sig("step_ps", PASSES * NC_), sig("step_sb", PASSES * NC_)
        outp, out_sb = sig("outp", PASSES * GB * 2), sig("out_sb", PASSES * GB * 2)
        dve_links, act_links, pe_turns, sp_turns = sig("dve_links", 20 + 2 * (3 + 2 * (C - 1))), sig("act_links", 2 * GB), sig("pe_turns"), sig("sp_turns")

        block = ctx.enter_context(nc.Block())

        @block.sync
        def _(sp):
            def held(*at):
                sp.wait_ge(*at)
                sp.sem_inc(sp_turns.sem, 1)

            for dst, src in loads:
                sp.dma_start(dst, src).then_inc(consts_in.sem, 16)
            with sp.Fori(0, HP) as hp:
                with sp.Fori(0, 2) as g:
                    i = hp * 2 + g
                    sp.dma_start(w[:, :, :, :], io["w_d"].rearrange("p (k n m) -> p k n m", k=DT, n=5)[bass.ds(hp * P, P)]).then_inc(inputs_in.sem, 16)
                    sp.dma_start(nba[:, :], io["b_a"][bass.ds(hp * P, P), :]).then_inc(inputs_in.sem, 16)
                    sp.dma_start(xg, scratch["x2"].rearrange("(k p) t -> p k t", p=P)[:, :, bass.ds(g * GT, GT)]).then_inc(inputs_in.sem, 16)
                    for s, name in enumerate(("beta", "gamma")):
                        for e in range(2):
                            src = scratch[name][bass.ds(hp * 2 + e, 1), bass.ds(g * GT, GT)].rearrange("e (u t) -> (e u) t", t=C)
                            sp.dma_start(gate[e * DH:(e + 1) * DH, s, :], src).then_inc(inputs_in.sem, 16)
                    for s in range(PASSES):
                        nt = scratch["nt"].rearrange("(n q) (s t) -> q s n t", q=QB, t=C)
                        held(*score_sb(i, 2 * U_ * (s + 1)))
                        for c in range(QB):
                            sp.dma_start(nt[c], apm[c * C:(c + 1) * C, :, 0, c * C:(c + 1) * C]).then_inc(nt_out.sem, 16)
                        held(*nt_out(i, QB * (s + 1)))
                        sp.dma_start(inv[:, 0:C * C], scratch["nt"]).then_inc(nt_in.sem, 16)
                        held(*xi_r(i, s + 1))
                        sp.dma_start(scratch["xt"], inv[:, C * C:2 * C * C]).then_inc(x_out.sem, 16)
                        held(*x_out(i, s + 1))
                        xt = scratch["xt"].rearrange("(n q) (s t) -> q s n t", q=QB, t=C)
                        for c in range(QB):
                            sp.dma_start(apm[c * C:(c + 1) * C, :, 0, c * C:(c + 1) * C], xt[c]).then_inc(x_back.sem, 16)
                    held(*out_sb(i, PASSES * GB * 2))
                    sp.dma_start(scratch["o"][bass.ds(hp * P, P), bass.ds(g * GT, GT)], o[:, :]).then_inc(stored.sem, 16)
                    held(*stored(i, 1))

        def vk(e):
            return (1, 0) if e == 0 else (2, 3)

        @block.tensor
        def _(pe):
            mm = pe.matmul

            def held(*at):
                pe.wait_ge(*at)
                pe.sem_inc(pe_turns.sem, 1)

            pe.wait_ge(*consts_in(0, len(loads)))
            with pe.Fori(0, HP) as hp:
                with pe.Fori(0, 2) as g:
                    i = hp * 2 + g
                    held(*inputs_in(i, 7))
                    for b in range(GB):
                        if b >= 1:
                            held(*kn_r(i, b))
                            held(*la(i, b))
                        for n in range(5):
                            for k in range(DT):
                                j = mm(ps[n][:, :], w[:, k, n, :], xg[:, k, b * T:(b + 1) * T], start=(k == 0), stop=(k == DT - 1))
                        j.then_inc(proj.sem, 1)
                        held(*ksq_r(i, b + 1))
                        mm(ps[5][:, :], pair_sum[:, :], ksq, start=True, stop=True).then_inc(ss.sem, 1)
                    for s in range(PASSES):
                        kinds = (0, 1, 2) if s == 0 else (0, 2)
                        m0 = slice(0, 3) if s == 0 else slice(0, 3, 2)
                        m1 = slice(1, 3) if s == 0 else slice(2, 3)
                        for b in range(GB):
                            held(*kend_r(i, s * GB + b + 1))
                            held(*movs(i, s * GB + b + 1))
                            if b == 0 and s == 0:
                                held(*qv_r(i, 1))
                                held(*kn_r(i, GB))
                            if b == 0 and s == 1:
                                held(*out_sb(i, GB * 2))
                            if b >= 1:
                                held(*tr_sb(i, s * GB + b))
                            for u in range(UB):
                                at = slice(b * T + u * P, b * T + (u + 1) * P)
                                pe.transpose(ps[0][:, u * P:(u + 1) * P], mov[:, 0, at], ident[:, :])
                                pe.transpose(ps[1][:, u * P:(u + 1) * P], v[:, at], ident[:, :])
                                j = pe.transpose(ps[2][:, u * P:(u + 1) * P], kend[:, u * P:(u + 1) * P], ident[:, :])
                            j.then_inc(tr.sem, 1)
                            for u in range(UB):
                                for e in range(2):
                                    n = (b * UB + u) * 2 + e
                                    at = slice(b * T + u * P, b * T + (u + 1) * P)
                                    if n >= 4:
                                        held(*score_sb(i, s * 2 * U_ + n - 3))
                                    mm(ps[4 + n % 4][:, 0:len(kinds) * P], km[e * DH:(e + 1) * DH, at], mov[e * DH:(e + 1) * DH, m0, at],
                                       start=True, stop=True).then_inc(score.sem, 1)
                        held(*x_back(i, QB * (s + 1)))
                        held(*tr_sb(i, GB * (s + 1)))
                        held(*score_sb(i, 2 * U_ * (s + 1)))
                        for n in range(U_ // 2):
                            if n >= 2:
                                held(*z_sb(i, s * U_ // 2 + n - 1))
                            for u in (2 * n, 2 * n + 1):
                                for e in range(2):
                                    at = (u % 2) * 2 * P + e * P
                                    j = mm(ps[n % 2][:, at:at + P], apm[:, e * U_ + u, 0, :], tok[:, u, 2 * e:2 * e + 2, :],
                                           start=True, stop=True)
                            j.then_inc(zp.sem, 1)
                        wd = (m1.stop - m1.start) * P
                        for n in range(U_ // 2):
                            held(*z_sb(i, s * U_ // 2 + n + 1))
                            if n >= 1:
                                held(*px_sb(i, s * U_ // 2 + n))
                            for e in range(2):
                                for u in (2 * n, 2 * n + 1):
                                    j = mm(ps[2 + e][:, (u % 2) * wd:(u % 2 + 1) * wd], z[:, u, e * P:(e + 1) * P],
                                           apm[:, e * U_ + u, m1, :], start=True, stop=True)
                            j.then_inc(px.sem, 1)
                            if n % 2 == 0:
                                continue
                            b = n // 2
                            if b >= 1:
                                held(*psi_sb(i, s * GB + b))
                            for u in range(b * UB, (b + 1) * UB):
                                for e in range(2):
                                    row = slice(e * DH, (e + 1) * DH)
                                    vs, ks = vk(e)
                                    col = (u % UB) * DH
                                    for c in range(QB):
                                        part = slice(c * C, (c + 1) * C)
                                        mm(ps[4 + c][row, col:col + DH], z[part, u, ks * DH:(ks + 1) * DH], ke[part, u, row], start=True, stop=True,
                                           tile_position=(c * C, e * DH))
                                        j = mm(ps[4 + c][row, 256 + col:256 + col + DH], ke[part, u, row], z[part, u, vs * DH:(vs + 1) * DH],
                                               start=True, stop=True, tile_position=(c * C, e * DH))
                            j.then_inc(pp.sem, 1)
                        held(*psi_sb(i, GB * (s + 1)))
                        held(*state0(i, s + 1))
                        for c in range(NC_):
                            if c >= 1:
                                held(*step_sb(i, s * NC_ + c))
                            for b in range(GB):
                                for e in range(2):
                                    row = slice(e * DH, (e + 1) * DH)
                                    j = mm(ps[6 + c % 2][row, b * DH:(b + 1) * DH], phi[row, c, b, :], state[row, c, b, :], start=True, stop=True,
                                           tile_position=(e * DH, e * DH))
                            j.then_inc(step_ps.sem, 1)
                        held(*px_sb(i, U_ // 2 * (s + 1)))
                        held(*step_sb(i, NC_ * (s + 1)))
                        nk = m1.stop - m1.start
                        for b in range(GB):
                            for half in range(2):
                                n = b * 2 + half
                                if n >= 2:
                                    held(*out_sb(i, s * GB * 2 + n - 1))
                                for c in range(NC_ // 2):
                                    for e in range(2):
                                        cc = half * NC_ // 2 + c
                                        j = mm(ps[n % 2][(1 - e) * DH:(2 - e) * DH, 0:nk * T // 2].rearrange("p (m t) -> p m t", m=nk)[:, :, c * C:(c + 1) * C],
                                               state[e * DH:(e + 1) * DH, cc, b, :],
                                               mov[e * DH:(e + 1) * DH, m1, b * T + cc * C:b * T + (cc + 1) * C], start=True, stop=True,
                                               tile_position=(e * DH, (1 - e) * DH))
                                j.then_inc(outp.sem, 1)

        @block.scalar
        def _(act):
            A = act.activation
            act.wait_ge(*consts_in(0, len(loads)))
            with act.Fori(0, HP) as hp:
                with act.Fori(0, 2) as g:
                    i = hp * 2 + g
                    ch = Chain(act_links, act, i)
                    act.wait_ge(*neg_ba(i, 1))
                    for b in range(GB):
                        at = slice(b * T, (b + 1) * T)
                        act.wait_ge(*proj(i, b + 1))
                        if b >= 1:
                            act.wait_ge(*ss(i, b))
                        A(ksq, ps[0][:, :], ACT.Square).then_inc(ksq_r.sem, 1)
                        j = A(q[:, at], ps[1][:, :], ACT.Copy)
                        j = A(v[:, at], ps[4][:, :], ACT.Copy)
                        if b == GB - 1:
                            j.then_inc(qv_r.sem, 1)
                        for n in range(2):
                            j = A(L[n][:, at], ps[2 + n][:, :], ACT.Exp, scale=-1.0, bias=nba[:, n:n + 1])
                        ch.link(j)
                        for n in range(2):
                            j = A(L[n][:, at], L[n][:, at], ACT.Ln, bias=1.0)
                        j.then_inc(la.sem, 1)
                        act.wait_ge(*ssc(i, b + 1))
                        ch.link(A(rn, rn, ACT.Ln))
                        A(rn, rn, ACT.Exp, scale=-0.5).then_inc(rn_r.sem, 1)
                    for s in range(PASSES):
                        for b in range(GB):
                            at = slice(b * T, (b + 1) * T)
                            act.wait_ge(*lcap(i, b + 1))
                            n = s * GB + b
                            if n >= 1:
                                act.wait_ge(*kend_r(i, n))
                                act.wait_ge(*movs(i, n))
                            if s == 1 and b == 0:
                                act.wait_ge(*step_sb(i, NC_))
                                act.wait_ge(*outp(i, GB * 2))
                            A(gp[:, :, 1:], L[s][:, at].rearrange("p (c t) -> p c t", t=C), ACT.Exp, scale=-1.0)
                            A(gm, L[s][:, at], ACT.Exp).then_inc(gexp.sem, 1)
                            act.wait_ge(*tr(i, n + 1))
                            us = slice(b * UB, (b + 1) * UB)
                            A(ke[:, us, :], ps[2][:, :].rearrange("p (u d) -> p u d", u=UB), ACT.Copy)
                            for bank, slots in ((0, (0, 3)), (1, (2, 1))):
                                for e, slot in enumerate(slots):
                                    j = A(tok[:, us, slot, :], ps[bank][:, :].rearrange("p (u d) -> p u d", u=UB)[:, :, e * DH:(e + 1) * DH], ACT.Copy)
                            j.then_inc(tr_sb.sem, 1)
                        for n in range(U_ // 2):
                            act.wait_ge(*zp(i, s * U_ // 2 + n + 1))
                            A(z[:, 2 * n:2 * n + 2, :], ps[n % 2][:, :].rearrange("p (u d) -> p u d", u=2), ACT.Copy).then_inc(z_sb.sem, 1)
                        act.wait_ge(*x_out(i, s + 1))
                        for b in range(GB):
                            act.wait_ge(*phi_sb(i, s * GB + b + 1))
                            for c in range(QB):
                                j = A(state[:, 1 + c::QB, b, :], ps[4 + c][:, 256:].rearrange("p (u d) -> p u d", d=DH), ACT.Copy)
                            j.then_inc(psi_sb.sem, 1)

        @block.gpsimd
        def _(pool):
            pool.wait_ge(*consts_in(0, len(loads)))
            with pool.Fori(0, HP) as hp:
                with pool.Fori(0, 2) as g:
                    i = hp * 2 + g
                    for s in range(PASSES):
                        for b in range(GB):
                            at = slice(b * T, (b + 1) * T)
                            chunks = "p (c t) -> p c t"
                            pool.wait_ge(*kpm(i, s * GB + b + 1))
                            if s == 0:
                                pool.tensor_tensor(mov[:, 1, at].rearrange(chunks, t=C), kn[:, at].rearrange(chunks, t=C), gp[:, :, 0:C], ALU.mult)
                            pool.tensor_tensor(mov[:, 2, at].rearrange(chunks, t=C), q[:, at].rearrange(chunks, t=C), gp[:, :, 1:], ALU.mult).then_inc(movs.sem, 1)

        @block.vector
        def _(dve):
            tt, stt = dve.tensor_tensor, dve.scalar_tensor_tensor
            chunks = "p (c t) -> p c t"
            dve.wait_ge(*consts_in(0, len(loads)))
            with dve.Fori(0, HP) as hp:
                with dve.Fori(0, 2) as g:
                    i = hp * 2 + g
                    ch = Chain(dve_links, dve, i)
                    dve.wait_ge(*inputs_in(i, 7))
                    dve.tensor_scalar(nba[:, :], nba[:, :], -1.0, None, ALU.mult).then_inc(neg_ba.sem, 1)
                    for b in range(GB):
                        at = slice(b * T, (b + 1) * T)
                        dve.wait_ge(*ss(i, b + 1))
                        dve.tensor_scalar(rn, ps[5][:, :], 1e-24, 2.0 ** 40, ALU.max, ALU.mult).then_inc(ssc.sem, 1)
                        dve.wait_ge(*la(i, b + 1))
                        for n in range(2):
                            j = dve.tensor_tensor_scan(L[n][:, at], restart[:, :], L[n][:, at], 0.0, ALU.mult, ALU.add)
                        j.then_inc(lsum.sem, 1)
                        dve.wait_ge(*rn_r(i, b + 1))
                        stt(kn[:, at], rn, 2.0 ** 20, ps[0][:, :], ALU.mult, ALU.mult).then_inc(kn_r.sem, 1)
                        dve.wait_ge(*lsum(i, b + 1))
                        for n in range(2):
                            j = dve.tensor_scalar(L[n][:, at], L[n][:, at], LMAX, None, ALU.min)
                        j.then_inc(lcap.sem, 1)
                    for s in range(PASSES):
                        kinds = 3 if s == 0 else 2
                        m1 = slice(1, 3) if s == 0 else slice(2, 3)
                        nk = m1.stop - m1.start
                        if s == 1:
                            dve.wait_ge(*outp(i, GB * 2))
                            dve.wait_ge(*step_ps(i, NC_))
                        else:
                            dve.wait_ge(*kn_r(i, GB))
                        ch.link(dve.memset(gp[:, :, 0:1], 1.0))
                        for b in range(GB):
                            at = slice(b * T, (b + 1) * T)
                            n = s * GB + b
                            dve.wait_ge(*gexp(i, n + 1))
                            tt(km[:, at], kn[:, at], gm, ALU.mult)
                            ch.link(dve.tensor_copy(gend[:, b * NC_:(b + 1) * NC_].unsqueeze(2), gp[:, :, C:]))
                            tt(mov[:, 0, at].rearrange(chunks, t=C), kn[:, at].rearrange(chunks, t=C), gp[:, :, 1:], ALU.mult).then_inc(kpm.sem, 1)
                            if b >= 1:
                                dve.wait_ge(*tr(i, n))
                            tt(kend.rearrange(chunks, t=C), km[:, at].rearrange(chunks, t=C),
                               gend[:, b * NC_:(b + 1) * NC_].unsqueeze(2).broadcast_to([P, NC_, C]), ALU.mult).then_inc(kend_r.sem, 1)
                            for j in range(2 * UB):
                                k = b * 2 * UB + j
                                dve.wait_ge(*score(i, s * 2 * U_ + k + 1))
                                eu = (j % 2) * U_ + k // 2
                                if s == 0:
                                    tt(apm[:, eu, :, :], ps[4 + k % 4][:, 0:3 * P].rearrange("p (m t) -> p m t", m=3), masks[:, :, :], ALU.mult).then_inc(score_sb.sem, 1)
                                else:
                                    tt(apm[:, eu, 0:3:2, :], ps[4 + k % 4][:, 0:2 * P].rearrange("p (m t) -> p m t", m=2), masks[:, 0:3:2, :], ALU.mult).then_inc(score_sb.sem, 1)
                        ch.link(dve.memset(xi, 0.0))
                        ch.link(dve.memset(inv[:, C * C:2 * C * C:C + 1], 1.0))
                        dve.wait_ge(*nt_in(i, s + 1))
                        ch.link(stt(ni, ni, -1.0, gate[:, s, :].unsqueeze(1).broadcast_to([P, C, C]), ALU.mult, ALU.mult))
                        for t in range(1, C):
                            pt = pr[:, 0:t * t].rearrange("p (a b) -> p a b", a=t)
                            ch.link(tt(pt, xi[:, 0:t, 0:t], ni[:, 0:t, t:t + 1].rearrange("p s o -> p o s").broadcast_to([P, t, t]), ALU.mult))
                            ch.link(dve.tensor_reduce(xi[:, 0:t, t], pt, AX.X, ALU.add))
                        tt(xi, xi, gate[:, s, :].unsqueeze(2).broadcast_to([P, C, C]), ALU.mult).then_inc(xi_r.sem, 1)
                        dve.wait_ge(*tr(i, GB * (s + 1)))
                        dve.wait_ge(*movs(i, GB * (s + 1)))
                        for b in range(GB):
                            j = tt(phi[:, :, b, :], ident2[:, :].unsqueeze(1).broadcast_to([P, NC_, DH]),
                                   gend[:, b * NC_:(b + 1) * NC_].unsqueeze(2).broadcast_to([P, NC_, DH]), ALU.mult)
                        ch.link(j)
                        dve.wait_ge(*x_out(i, s + 1))
                        dve.memset(state[:, 0, :, :], 0.0).then_inc(state0.sem, 1)
                        for n in range(U_ // 2):
                            at = slice(2 * n * P, (2 * n + 2) * P)
                            dve.wait_ge(*px(i, s * U_ // 2 + n + 1))
                            for e in range(2):
                                kr, vr = slice(e * DH, (e + 1) * DH), slice((1 - e) * DH, (2 - e) * DH)
                                both = ps[2 + e][:, 0:2 * nk * P].rearrange("p (u m t) -> p m u t", u=2, m=nk)
                                for m in range(nk):
                                    mk = mov[kr, m1.start + m, at].rearrange("p (u t) -> p u t", u=2)
                                    tt(mk, mk, both[kr, m], ALU.subtract)
                                if s == 0:
                                    vv = v[vr, at].rearrange("p (u t) -> p u t", u=2)
                                    tt(vv, vv, both[vr, 0], ALU.subtract)
                                    j = dve.tensor_copy(o[vr, at].rearrange("p (u t) -> p u t", u=2), both[vr, 1])
                                else:
                                    oo = o[vr, at].rearrange("p (u t) -> p u t", u=2)
                                    j = tt(oo, oo, both[vr, 0], ALU.add)
                            j.then_inc(px_sb.sem, 1)
                            if n % 2 == 1:
                                b = n // 2
                                dve.wait_ge(*pp(i, s * GB + b + 1))
                                for c in range(QB):
                                    pf = phi[:, c::QB, b, :]
                                    j = tt(pf, pf, ps[4 + c][:, 0:256].rearrange("p (u d) -> p u d", d=DH), ALU.subtract)
                                j.then_inc(phi_sb.sem, 1)
                        dve.wait_ge(*psi_sb(i, GB * (s + 1)))
                        for c in range(NC_):
                            dve.wait_ge(*step_ps(i, s * NC_ + c + 1))
                            tt(state[:, c + 1, :, :], state[:, c + 1, :, :], ps[6 + c % 2][:, 0:GB * DH].rearrange("p (b d) -> p b d", b=GB), ALU.add).then_inc(step_sb.sem, 1)
                        dve.wait_ge(*px_sb(i, U_ // 2 * (s + 1)))
                        for n in range(GB * 2):
                            at = slice(n * T // 2, (n + 1) * T // 2)
                            dve.wait_ge(*outp(i, s * GB * 2 + n + 1))
                            if s == 0:
                                ch.link(tt(v[:, at], v[:, at], ps[n % 2][:, 0:T // 2], ALU.subtract))
                                dve.tensor_scalar(v[:, at], v[:, at], 1.0, -1.0, ALU.min, ALU.max)
                            tt(o[:, at], o[:, at], ps[n % 2][:, (nk - 1) * T // 2:nk * T // 2], ALU.add).then_inc(out_sb.sem, 1)
                    ch.close()
    return signals


def head_and_mlp(nc, io, scratch, out):
    K_TOP = int(2 * np.log(T))
    KC = 16
    UB = T // P
    LOW = -3.0e38
    NSTAGE = int(np.log2(FF))
    HF = FF // 2

    signals = []
    with ExitStack() as ctx:
        def sb(name, *shape):
            return ctx.enter_context(nc.sbuf_tensor("f_" + name, list(shape), F32))

        def sig(name, per=1, step=1):
            return Signal(signals, nc, "f_" + name, per, step)

        ps = [ctx.enter_context(nc.psum_tensor(f"f_bank{i}", [P, T], F32)) for i in range(8)]
        loads = []

        def const(name, src, *shape):
            t = sb(name, *shape)
            loads.append((t[tuple(slice(None) for _ in shape)], src))
            return t

        def fm(name):
            return io[name].rearrange("(k p) n -> p k n", p=P)

        mean_d = const("mean_d", io["c_mean_d"], P, P)
        mean_bc = const("mean_bc", io["c_mean_bc"], P, P)
        ident = const("ident", io["c_ident"], P, P)
        w_o = const("w_o", fm("w_o1"), P, HP, D)
        w_q = const("w_q", fm("w_xq"), P, DT, KC)
        b_q = const("b_q", io["b_xq"], KC, 1)
        b_qr = const("b_qr", io["b_xqr"], 1, KC)
        w_out = const("w_out", fm("w_xo"), P, DT, D)
        b_out = const("b_out", io["b_xo"].unsqueeze(2), P, DT, 1)
        up_b = const("up_b", io["up_b"], P, FT)
        con_b = const("con_b", io["con_b"], P, DT)
        down_b = const("down_b", io["down_b"], P, DT)
        n_const = len(loads)
        yu = sb("yu", P, 2, 3, FF)
        yd = sb("yd", P, 2, 2, FF)
        bw = [sb("bwu", P, 2, 4, HF), sb("bwd", P, 2, 4, HF)]
        tu = sb("tu", P, 2, 3, HF)
        td = sb("td", P, 2, 2, HF)
        hid = sb("hid", P, FT, T)
        md = sb("md", P, FT, D)
        bu = sb("bu", P, FT)
        bd = sb("bd", P, DT)
        ones = sb("ones", 1, P)
        eps = sb("eps", P, 1)
        oin = hid
        x = sb("x", P, DT, T)
        cx = sb("cx", P, DT, T)
        cen = sb("cen", P, DT, T)
        sq = sb("sq", P, DT, T)
        xn = sb("xn", P, DT, T)
        lnv, rstd = sb("lnv", P, T), sb("rstd", P, T)
        qk = sb("qk", KC, 2, T)
        vt = sb("vt", P, UB, B * KC)
        xo = sb("xo", P, DT, B, 2 * KC)
        qa, ka = sq[:, 0, :], sq[:, 1, :]
        gk = hid[:, 0:UB, :]
        gs = hid[:, UB:2 * UB, :]
        corr, c2, c3, wt, rr = cen[:, 0, :], cen[:, 1, :], xn[:, 0, :], xn[:, 1, :], x[:, 0, :]
        m1, m2, second8, wsum = sb("m1", P, 8), sb("m2", P, 8), sb("second8", P, 8), sb("wsum", P, 2)

        consts_in, setup = sig("consts_in", n_const, 16), sig("setup", 5)
        yin = sig("yin", 4, 16)
        bw_in = [[sig(n + str(j), NSTAGE // 2, 16) for j in range(2)] for n in ("bwu_in", "bwd_in")]
        stage = [sig("stage_u", NSTAGE), sig("stage_d", NSTAGE)]
        half = [sig("half_u", 3 * NSTAGE), sig("half_d", 3 * NSTAGE)]
        in1, o_ps, x_sum, saved1 = sig("in1", 3, 16), sig("o_ps"), sig("x_sum"), sig("saved1", 3, 16)
        qkv_ps, qk_sb, v_sb = sig("qkv_ps"), sig("qk_sb"), sig("v_sb")
        ln = [[sig(n + str(l)) for n in ("mean", "cent", "sq", "var", "log", "rstd", "out")] for l in (1, 2)]
        mid_in, gram, gram_sb, gram_out, skew_in, corr_ps = (
            sig("mid_in", 2, 16), sig("gram", UB), sig("gram_sb"), sig("gram_out", 2, 16), sig("skew_in", 1, 16), sig("corr_ps"))
        mid, shifted_exp = sig("mid", 11), sig("shifted_exp")
        w_outs, circ_in, r_ps, r_sb = sig("w_outs", 5, 16), sig("circ_in", 1, 16), sig("r_ps"), sig("r_sb")
        xo_ps, xo_sb, bu_ps, bu_sb, md_ps, md_sb = sig("xo_ps"), sig("xo_sb"), sig("bu_ps"), sig("bu_sb"), sig("md_ps", 4), sig("md_sb", 4)
        in2, x_e, hid_ps, hid_sb, f_ps, x_f, saved2 = (
            sig("in2", 1, 16), sig("x_e"), sig("hid_ps", FT), sig("hid_sb", FT), sig("f_ps"), sig("x_f"), sig("saved2", 1, 16))
        sp_turns = sig("sp_turns")

        block = ctx.enter_context(nc.Block())

        def tokens(name, b):
            return scratch[name].rearrange("(k p) t -> p k t", p=P)[:, :, bass.ds(b * T, T)]

        @block.sync
        def _(sp):
            def held(*at):
                sp.wait_ge(*at)
                sp.sem_inc(sp_turns.sem, 1)

            for dst, src in loads:
                sp.dma_start(dst, src).then_inc(consts_in.sem, 16)
            sp.wait_ge(*setup(0, 3))
            sp.dma_start(yu[:, 0, 0:2, :], fm("w_exp")).then_inc(yin.sem, 16)
            sp.dma_start(yu[0:1, 0, 2, :], io["b_exp"]).then_inc(yin.sem, 16)
            sp.dma_start(yd[:, 0, :, :], fm("w_con")).then_inc(yin.sem, 16)
            sp.dma_start(bw[0][:, 0, :, :], io["bw_up"][0:1, :].partition_broadcast(P)).then_inc(bw_in[0][0].sem, 16)
            with sp.Fori(0, B) as b:
                sp.dma_start(oin[:, :, :], tokens("o", b)).then_inc(in1.sem, 16)
                sp.dma_start(x[:, :, :], tokens("x", b)).then_inc(in1.sem, 16)
                sp.dma_start(cx[:, :, :], io["ctx"].rearrange("(k p) t -> p k t", p=P)[:, :, bass.ds(b * T, T)]).then_inc(in1.sem, 16)
                held(*x_sum(b, 1))
                sp.dma_start(tokens("x3", b), x[:, :, :]).then_inc(saved1.sem, 16)
                held(*qk_sb(b, 1))
                for n in range(2):
                    sp.dma_start(scratch["qk"][n, bass.ds(b * KC, KC), :], qk[:, n, :]).then_inc(saved1.sem, 16)
                held(*v_sb(b, 1))
                held(*saved1(b, 3))
            for n, t in enumerate((qa, ka)):
                sp.dma_start(t, scratch["qk"][n]).then_inc(mid_in.sem, 16)
            sp.wait_ge(*gram_sb(0, 1))
            rows = scratch["gram"][0:2 * T * T].rearrange("(u p r m) -> p u r m", p=P, r=2, m=T)
            for r in range(2):
                sp.dma_start(rows[:, :, r, :], gk).then_inc(gram_out.sem, 16)
            sp.wait_ge(*gram_out(0, 2))
            sp.dma_start(gs, scratch["gram"].rearrange("(u p m) -> p u m", p=P, m=2 * T + 1)[:, :, 0:T]).then_inc(skew_in.sem, 16)
            sp.wait_ge(*mid(0, 11))
            for n in range(UB):
                sp.dma_start(scratch["wts"][n * P * T:(n + 1) * P * T].rearrange("(p t) -> p t", t=T), wt).then_inc(w_outs.sem, 16)
            sp.dma_start(scratch["wts"][T * T:T * T + 2 * T].rearrange("(p t) -> p t", t=T), wt[0:2, :]).then_inc(w_outs.sem, 16)
            sp.wait_ge(*w_outs(0, 5))
            sp.dma_start(gs, scratch["wts"][1:T * (T + 1) + 1].rearrange("(u p m) -> p u m", p=P, m=T + 1)[:, :, 0:T]).then_inc(circ_in.sem, 16)
            sp.wait_ge(*xo_ps(0, 1))
            with sp.Fori(0, B) as b:
                sp.dma_start(x[:, :, :], tokens("x3", b)).then_inc(in2.sem, 16)
                held(*x_f(b, 1))
                sp.dma_start(out.rearrange("(k p) t -> p k t", p=P)[:, :, bass.ds(b * T, T)], x[:, :, :]).then_inc(saved2.sem, 16)
                held(*saved2(b, 1))

        def norm_pe(pe, b, l):
            mean, cent, sqs, var, log, rst, o = ln[l]
            for j in range(DT):
                i = pe.matmul(ps[2][:, :], mean_d[:, :], x[:, j, :], start=(j == 0), stop=(j == DT - 1))
            i.then_inc(mean.sem, 1)
            pe.wait_ge(*sqs(b, 1))
            for j in range(DT):
                i = pe.matmul(ps[3][:, :], mean_d[:, :], sq[:, j, :], start=(j == 0), stop=(j == DT - 1))
            i.then_inc(var.sem, 1)
            pe.wait_ge(*o(b, 1))

        def norm_act(act, b, l):
            mean, cent, sqs, var, log, rst, o = ln[l]
            act.wait_ge(*cent(b, 1))
            act.activation(sq[:, :, :], cen[:, :, :], ACT.Square).then_inc(sqs.sem, 1)
            act.wait_ge(*var(b, 1))
            act.activation(lnv[:, :], ps[3][:, :], ACT.Ln, bias=eps[:, 0:1]).then_inc(log.sem, 1)
            act.wait_ge(*log(b, 1))
            act.activation(rstd[:, :], lnv[:, :], ACT.Exp, scale=-0.5).then_inc(rst.sem, 1)

        def norm_dve(dve, b, l):
            mean, cent, sqs, var, log, rst, o = ln[l]
            dve.wait_ge(*mean(b, 1))
            dve.tensor_tensor(cen[:, :, :], x[:, :, :], wide(ps[2][:, :], DT), ALU.subtract).then_inc(cent.sem, 1)
            dve.wait_ge(*rst(b, 1))
            dve.tensor_tensor(xn[:, :, :], cen[:, :, :], wide(rstd[:, :], DT), ALU.mult).then_inc(o.sem, 1)

        def butterfly(eng, which, y, tmp, st, hold):
            s = 2 ** st if which == 0 else 2 ** (NSTAGE - 1 - st)
            rows = y.shape[2]
            pairs = y[:, st % 2, :, :].rearrange("p r (n i s) -> p i r n s", i=2, s=s)
            into = y[:, (st + 1) % 2, :, :].rearrange("p r (n i s) -> p i r n s", i=2, s=s)

            def w(i, j):
                return bw[which][:, st % 2, 2 * i + j, :].rearrange("p (n s) -> p n s", s=s).unsqueeze(1).broadcast_to([P, rows, HF // s, s])

            def t(j):
                return tmp[:, j, :, :].rearrange("p r (n s) -> p r n s", s=s)

            hold(*bw_in[which][st % 2](0, st // 2 + 1))
            if st >= 1:
                hold(*stage[which](0, st))
            for i in range(2):
                k = 3 * st + 2 * i
                if i == 1:
                    hold(*half[which](0, k))
                eng.tensor_tensor(t(0), pairs[:, 0], w(i, 0), ALU.mult)
                eng.tensor_tensor(t(1), pairs[:, 1], w(i, 1), ALU.mult).then_inc(half[which].sem, 1)
                hold(*half[which](0, k + 1))
                j = eng.tensor_tensor(into[:, i], t(0), t(1), ALU.add)
                j.then_inc((half if i == 0 else stage)[which].sem, 1)

        def stream(eng, which, name, st):
            if st + 1 < NSTAGE:
                if st >= 1:
                    eng.wait_ge(*stage[which](0, st))
                eng.dma_start(bw[which][:, (st + 1) % 2, :, :], io[name][st + 1:st + 2, :].partition_broadcast(P)).then_inc(bw_in[which][(st + 1) % 2].sem, 16)

        @block.tensor
        def _(pe):
            mm = pe.matmul
            pe.wait_ge(*consts_in(0, n_const))
            pe.wait_ge(*setup(0, 5))
            with pe.Fori(0, B) as b:
                pe.wait_ge(*in1(b, 3))
                for m in range(DT):
                    for k in range(HP):
                        i = mm(ps[m][:, :], w_o[:, k, m * P:(m + 1) * P], oin[:, k, :], start=(k == 0), stop=(k == HP - 1))
                i.then_inc(o_ps.sem, 1)
                pe.wait_ge(*x_sum(b, 1))
                norm_pe(pe, b, 0)
                for bank, src in ((4, xn), (5, cx)):
                    for k in range(DT):
                        mm(ps[bank][0:KC, :], w_q[:, k, :], src[:, k, :], start=(k == 0), stop=(k == DT - 1))
                for u in range(UB):
                    for k in range(DT):
                        mm(ps[6][:, u * KC:(u + 1) * KC], cx[:, k, u * P:(u + 1) * P], w_q[:, k, :], start=(k == 0), stop=False)
                    i = mm(ps[6][:, u * KC:(u + 1) * KC], ones[:, :], b_qr[:, :], start=False, stop=True)
                i.then_inc(qkv_ps.sem, 1)
            pe.wait_ge(*mid_in(0, 2))
            pe.wait_ge(*v_sb(B - 1, 1))
            for u in range(UB):
                mm(ps[u][:, :], ka[:, u * P:(u + 1) * P], qa, start=True, stop=True).then_inc(gram.sem, 1)
            pe.wait_ge(*skew_in(0, 1))
            for u in range(UB):
                i = mm(ps[4][:, :], mean_bc[:, :], gs[:, u, :], start=(u == 0), stop=(u == UB - 1))
            i.then_inc(corr_ps.sem, 1)
            pe.wait_ge(*circ_in(0, 1))
            for n in range(UB):
                for u in range(UB):
                    i = mm(ps[5][:, n * P:(n + 1) * P], gs[:, u, n * P:(n + 1) * P], vt[:, u, :], start=(u == 0), stop=(u == UB - 1))
            i.then_inc(r_ps.sem, 1)
            pe.wait_ge(*r_sb(0, 1))
            for m in range(DT):
                for h in range(2):
                    for k in range(DT):
                        i = mm(ps[7][:, (2 * m + h) * P:(2 * m + h + 1) * P], w_out[:, k, m * P:(m + 1) * P],
                               rr[:, ((1 - h) * 2 + k) * P:((1 - h) * 2 + k + 1) * P], start=(k == 0), stop=(k == DT - 1))
            i.then_inc(xo_ps.sem, 1)
            pe.wait_ge(*stage[0](0, NSTAGE))
            pe.wait_ge(*stage[1](0, NSTAGE))
            fin = NSTAGE % 2
            for m in range(FT):
                i = mm(ps[6][:, m:m + 1], yu[0:1, fin, 2, m * P:(m + 1) * P], ones[0:1, 0:1], start=True, stop=True)
            i.then_inc(bu_ps.sem, 1)
            pe.wait_ge(*gram_sb(0, 1))
            for n in range(4):
                for m in (2 * n, 2 * n + 1):
                    for k in range(DT):
                        i = pe.transpose(ps[n][:, (m % 2) * D + k * P:(m % 2) * D + (k + 1) * P], yd[:, fin, k, m * P:(m + 1) * P], ident[:, :])
                i.then_inc(md_ps.sem, 1)
            pe.wait_ge(*md_sb(0, 4))
            pe.wait_ge(*bu_sb(0, 1))
            with pe.Fori(0, B) as b:
                pe.wait_ge(*x_e(b, 1))
                norm_pe(pe, b, 1)
                for m in range(FT):
                    for k in range(DT):
                        i = mm(ps[m][:, :], yu[:, fin, k, m * P:(m + 1) * P], xn[:, k, :], start=(k == 0), stop=(k == DT - 1))
                    i.then_inc(hid_ps.sem, 1)
                pe.wait_ge(*hid_sb(b, 2))
                for k in range(FT):
                    pe.wait_ge(*hid_sb(b, k + 1))
                    for m in range(DT):
                        i = mm(ps[m][:, :], md[:, k, m * P:(m + 1) * P], hid[:, k, :], start=(k == 0), stop=(k == FT - 1))
                i.then_inc(f_ps.sem, 1)

        @block.scalar
        def _(act):
            A = act.activation
            act.wait_ge(*consts_in(0, n_const))
            act.wait_ge(*setup(0, 5))
            with act.Fori(0, B) as b:
                norm_act(act, b, 0)
                act.wait_ge(*qkv_ps(b, 1))
                for n in range(2):
                    i = A(qk[:, n, :], ps[4 + n][0:KC, :], ACT.Identity, bias=b_q[:, :])
                i.then_inc(qk_sb.sem, 1)
            act.wait_ge(*gram(0, UB))
            for u in range(UB):
                i = A(gk[:, u, :], ps[u][:, :], ACT.Copy)
            i.then_inc(gram_sb.sem, 1)
            for st in range(NSTAGE):
                stream(act, 0, "bw_up", st)
            act.wait_ge(*mid(0, 7))
            A(wt, corr, ACT.Exp, bias=wsum[:, 1:2]).then_inc(shifted_exp.sem, 1)
            act.wait_ge(*r_ps(0, 1))
            A(rr, ps[5][:, :], ACT.Copy).then_inc(r_sb.sem, 1)
            for n in range(4):
                act.wait_ge(*md_ps(0, n + 1))
                A(md[:, 2 * n:2 * n + 2, :], ps[n][:, :].rearrange("p (m d) -> p m d", m=2), ACT.Copy).then_inc(md_sb.sem, 1)
            with act.Fori(0, B) as b:
                norm_act(act, b, 1)
                for m in range(FT):
                    act.wait_ge(*hid_ps(b, m + 1))
                    A(hid[:, m, :], ps[m][:, :], ACT.Gelu, bias=bu[:, m:m + 1]).then_inc(hid_sb.sem, 1)

        @block.gpsimd
        def _(pool):
            pool.dma_start(bw[1][:, 0, :, :], io["bw_down"][0:1, :].partition_broadcast(P)).then_inc(bw_in[1][0].sem, 16)
            pool.wait_ge(*yin(0, 3))
            for st in range(NSTAGE):
                stream(pool, 1, "bw_down", st)
                butterfly(pool, 1, yd, td, st, pool.wait_ge)

        @block.vector
        def _(dve):
            tt, stt = dve.tensor_tensor, dve.scalar_tensor_tensor
            dve.memset(yu[:, 0, 2, :], 0.0).then_inc(setup.sem, 1)
            dve.memset(ones[:, :], 1.0).then_inc(setup.sem, 1)
            dve.memset(eps[:, :], 1e-5).then_inc(setup.sem, 1)
            dve.wait_ge(*consts_in(0, n_const))
            dve.tensor_tensor(bd[:, :], con_b[:, :], down_b[:, :], ALU.add).then_inc(setup.sem, 1)
            dve.memset(m2[:, :], LOW).then_inc(setup.sem, 1)
            with dve.Fori(0, B) as b:
                dve.wait_ge(*o_ps(b, 1))
                for m in range(DT):
                    i = tt(x[:, m, :], x[:, m, :], ps[m][:, :], ALU.add)
                i.then_inc(x_sum.sem, 1)
                dve.wait_ge(*x_sum(b, 1))
                norm_dve(dve, b, 0)
                dve.wait_ge(*qkv_ps(b, 1))
                dve.tensor_copy(vt[:, :, bass.ds(b * KC, KC)], ps[6][:, 0:UB * KC].rearrange("p (u c) -> p u c", c=KC)).then_inc(v_sb.sem, 1)
            dve.wait_ge(*yin(0, 3))
            for st in range(NSTAGE):
                butterfly(dve, 0, yu, tu, st, dve.wait_ge)

            def then(i):
                link[0] += 1
                i.then_inc(mid.sem, 1)
                dve.wait_ge(*mid(0, link[0]))

            link = [0]
            dve.wait_ge(*corr_ps(0, 1))
            then(dve.tensor_copy(corr, ps[4][:, :]))
            then(dve.max(m1[:, :], corr))
            then(dve.match_replace(c2, m1[:, :], corr, LOW))
            then(dve.max(second8[:, :], c2))
            then(dve.tensor_copy(m2[:, 0:K_TOP - 8], second8[:, 0:K_TOP - 8]))
            then(dve.match_replace(c3, m2[:, :], c2, LOW))
            then(dve.tensor_scalar(wsum[:, 1:2], m1[:, 0:1], -1.0, None, ALU.mult))
            dve.wait_ge(*shifted_exp(0, 1))
            then(stt(wt, c3, -1e38, wt, ALU.is_lt, ALU.mult))
            then(dve.tensor_reduce(wsum[:, 0:1], wt, AX.X, ALU.add))
            then(dve.reciprocal(wsum[:, 0:1], wsum[:, 0:1]))
            then(dve.tensor_scalar(wt, wt, wsum[:, 0:1], None, ALU.mult))
            dve.wait_ge(*bu_ps(0, 1))
            tt(bu[:, :], up_b[:, :], ps[6][:, 0:FT], ALU.add).then_inc(bu_sb.sem, 1)
            dve.wait_ge(*xo_ps(0, 1))
            for m in range(DT):
                i = dve.tensor_scalar(xo[:, m, :, :].rearrange("p b (c h) -> p h (b c)", h=2), ps[7][:, 2 * m * P:2 * (m + 1) * P].rearrange("p (h n) -> p h n", h=2),
                                      b_out[:, m, :], None, ALU.add)
            i.then_inc(xo_sb.sem, 1)
            dve.wait_ge(*xo_sb(0, 1))
            with dve.Fori(0, B) as b:
                dve.wait_ge(*in2(b, 1))
                for m in range(DT):
                    i = tt(x[:, m, :].rearrange("p (r t) -> p r t", t=2 * KC), x[:, m, :].rearrange("p (r t) -> p r t", t=2 * KC),
                           xo[:, m, bass.ds(b, 1), :].broadcast_to([P, T // (2 * KC), 2 * KC]), ALU.add)
                i.then_inc(x_e.sem, 1)
                dve.wait_ge(*x_e(b, 1))
                norm_dve(dve, b, 1)
                dve.wait_ge(*f_ps(b, 1))
                for m in range(DT):
                    i = stt(x[:, m, :], ps[m][:, :], bd[:, m:m + 1], x[:, m, :], ALU.add, ALU.add)
                i.then_inc(x_f.sem, 1)


def _masks(c):
    s, t = np.arange(P)[:, None], np.arange(P)[None, :]
    same = s // c == t // c
    return np.concatenate([same & (s < t), same & (s < t), same & (s <= t)], 1).astype(np.float32)


def _pairs_swapped(w):
    return w.reshape(-1, HP, 2, DH)[:, :, ::-1].reshape(-1, H * DH)


CONSTS = {
    "c_mean_d": np.full((P, P), 1.0 / D, np.float32),
    "c_mean_di": np.full((P, P), 1.0 / DI, np.float32),
    "c_pair": np.kron(np.eye(2), np.ones((DH, DH))).astype(np.float32),
    "c_ident": np.eye(P, dtype=np.float32),
    "c_ident2": np.tile(np.eye(DH), (2, 1)).astype(np.float32),
    "c_mean_bc": np.full((P, P), 1.0 / (B * 16), np.float32),
    "c_masks": _masks(32),
    "c_restart": np.tile((np.arange(T) % 32 != 0), (P, 1)).astype(np.float32),
    "c_sel": np.repeat(np.eye(48)[:, RK:RK + 2 * NS], P, axis=1).astype(np.float32),
}


def layouts(v):
    def a(n):
        return np.asarray(v[n])

    def col(n):
        return a(n).reshape(-1, P).T

    return {
        "x": a("x").reshape(B * T, D).T, "ctx": a("ctx_1024").reshape(B * T, D).T,
        "w_in": a("L0_attn_W_in").T, "w_x": a("L0_attn_W_x").T, "w_dt": a("L0_attn_W_dt").T, "w_out": a("L0_attn_W_out").T,
        "conv_w": a("L0_attn_W_conv"), "conv_b": col("L0_attn_b_conv"), "b_dt": col("L0_attn_b_dt"), "a_log": a("L0_attn_A_log"),
        "skip_d": col("L0_attn_D"), "rms_w": col("L0_attn_rms_w"),
        "w_q": a("L0_xattn_Wq"), "w_k": a("L0_xattn_Wk"), "w_v": a("L0_xattn_Wv"), "w_o": a("L0_xattn_Wo"),
        "w_1": a("L0_ffn_w1"), "b_1": col("L0_ffn_b1"), "w_2": a("L0_ffn_w2"), "b_2": col("L0_ffn_b2"),
        "w_bg": np.concatenate([a("L1_attn_Wb").T, a("L1_attn_Wg").T], 1), "b_bg": np.stack([a("L1_attn_bb"), a("L1_attn_bg")], 1),
        "w_d": np.stack([a("L1_attn_Wk").T, a("L1_attn_Wq").T, a("L1_attn_Wa").T, a("L1_attn_WaR").T, _pairs_swapped(a("L1_attn_Wv").T)])
        .reshape(5, DT, P, HP, P).transpose(3, 2, 1, 0, 4).reshape(HP * P, -1),
        "b_a": np.stack([a("L1_attn_ba"), a("L1_attn_baR")], 1),
        "w_o1": _pairs_swapped(a("L1_attn_Wo")).T,
        "w_xq": a("L1_xattn_Wq"), "b_xq": a("L1_xattn_bq").reshape(-1, 1), "b_xqr": a("L1_xattn_bq").reshape(1, -1),
        "w_xo": a("L1_xattn_Wout")[::-1], "b_xo": col("L1_xattn_bout"),
        "w_exp": a("L1_ffn_W_exp"), "b_exp": a("L1_ffn_b_exp").reshape(1, -1), "up_b": col("L1_ffn_up_bias"),
        "w_con": a("L1_ffn_W_con").T, "con_b": col("L1_ffn_b_con"), "down_b": col("L1_ffn_down_bias"),
        "bw_up": a("L1_ffn_up_weights").transpose(0, 2, 3, 1).reshape(-1, 2 * FF),
        "bw_down": a("L1_ffn_down_weights")[::-1].transpose(0, 3, 2, 1).reshape(-1, 2 * FF),
        "ln_w": col("L1_attn_ln_w"), "ln_b": col("L1_attn_ln_b"),
    }


def build(nc, io, out):
    scratch = {n: nc.dram_tensor("s_" + n, s, F32, kind="Internal").ap() for n, s in {
        "x": [D, B * T], "x2": [D, B * T], "beta": [H, B * T], "gamma": [H, B * T],
        "x3": [D, B * T], "qk": [2, B * 16, T], "gram": [T * (2 * T + 1)], "wts": [T * (T + 2)],
        "nt": [P, 32 * 32], "xt": [P, 32 * 32], "o": [H * DH, B * T]}.items()}
    nc.clear_and_free_semaphores(layer0(nc, io, scratch))
    nc.all_engine_barrier()
    nc.clear_and_free_semaphores(delta_rule(nc, io, scratch))
    nc.all_engine_barrier()
    head_and_mlp(nc, io, scratch, out)


def kernel(**inputs):
    import concourse.bacc as _bacc
    from concourse.bass_utils import run_bass_kernel_spmd as _run

    nc = _bacc.Bacc("TRN2", target_bir_lowering=False, num_devices=1)
    arrays = {n: np.ascontiguousarray(a) for n, a in {**layouts(inputs), **CONSTS}.items()}
    io = {n: nc.dram_tensor("in_" + n, a.shape, mybir.dt.from_np(a.dtype), kind="ExternalInput").ap() for n, a in arrays.items()}
    out = nc.dram_tensor("out_y", [D, B * T], F32, kind="ExternalOutput").ap()
    build(nc, io, out)
    r = _run(nc, [{"in_" + n: a for n, a in arrays.items()}], core_ids=[0])
    return np.ascontiguousarray(r.results[0]["out_y"].T).reshape(B, T, D)
```

```python
from contextlib import ExitStack

import numpy as np

import concourse.bass as bass
from concourse import mybir
from concourse.alu_op_type import AluOpType as ALU

F32 = mybir.dt.float32
ACT = mybir.ActivationFunctionType
AX = mybir.AxisListType

P = 128
B, T, D = 8, 512, 256
DT = D // P
DI, NS, DC, RK = 512, 16, 4, 16
IT = DI // P
H, DH = 16, 64
HP = H // 2
FF = 1024
FT = FF // P
E10 = float(np.exp(-10.0))
DEN_SCALE = 2.0 ** 20


class Signal:

    def __init__(self, signals, nc, name, per=1, step=1):
        self.sem = nc.alloc_semaphore(name)
        signals.append(self.sem)
        self.per, self.step = per, step

    def __call__(self, turn, k):
        return self.sem, turn * (self.per * self.step) + k * self.step


class Chain:

    def __init__(self, links, eng, turn):
        self.links, self.eng, self.turn, self.count = links, eng, turn, 0

    def link(self, ins):
        self.count += 1
        ins.then_inc(self.links.sem, 1)
        self.eng.wait_ge(*self.links(self.turn, self.count))

    def close(self):
        assert self.count == self.links.per, (self.links.sem.name, self.count)


def wide(ap, n):
    return ap.unsqueeze(1).broadcast_to([ap.shape[0], n, ap.shape[1]])


def layer0(nc, io, scratch):
    signals = []
    with ExitStack() as ctx:
        def sb(name, *shape):
            return ctx.enter_context(nc.sbuf_tensor("a_" + name, list(shape), F32))

        def sig(name, per=1, step=1):
            return Signal(signals, nc, "a_" + name, per, step)

        ps = [ctx.enter_context(nc.psum_tensor(f"a_bank{i}", [P, T], F32)) for i in range(8)]

        load_list = []

        def const(name, src, *shape):
            t = sb(name, *shape)
            load_list.append((t[tuple(slice(None) for _ in shape)], src))
            return t

        def fm(name, k):
            return io[name].rearrange("(k p) n -> p k n", p=P)

        def vec(name):
            return io[name].unsqueeze(2)

        mean_d = const("mean_d", io["c_mean_d"], P, P)
        mean_di = const("mean_di", io["c_mean_di"], P, P)
        pair_sum = const("pair_sum", io["c_pair"], P, P)
        ident = const("ident", io["c_ident"], P, P)
        sel = const("sel", io["c_sel"].rearrange("p (n m) -> p n m", m=P), 48, 2 * NS, P)
        w_in = const("w_in", fm("w_in", DT), P, DT, 2 * DI)
        w_x = const("w_x", fm("w_x", IT), P, IT, 48)
        w_dt = const("w_dt", io["w_dt"], RK, DI)
        w_out = const("w_out", fm("w_out", IT), P, IT, D)
        w_q = const("w_q", fm("w_q", DT), P, DT, H * DH)
        w_k = const("w_k", fm("w_k", DT), P, DT, H * DH)
        w_v = const("w_v", fm("w_v", DT), P, DT, H * DH)
        w_o = const("w_o", fm("w_o", HP), P, HP, D)
        w_1 = const("w_1", fm("w_1", DT), P, DT, FF)
        w_2 = const("w_2", fm("w_2", FT), P, FT, D)
        w_bg = const("w_bg", io["w_bg"].rearrange("(k p) n -> p k n", p=P), P, DT, 2 * H)
        conv_w = const("conv_w", fm("conv_w", IT), P, IT, DC)
        conv_b = const("conv_b", vec("conv_b"), P, IT, 1)
        b_dt = const("b_dt", vec("b_dt"), P, IT, 1)
        a_log = const("a_log", fm("a_log", IT), P, IT, NS)
        skip_d = const("skip_d", vec("skip_d"), P, IT, 1)
        rms_w = const("rms_w", vec("rms_w"), P, IT, 1)
        b_1 = const("b_1", vec("b_1"), P, FT, 1)
        b_2 = const("b_2", vec("b_2"), P, DT, 1)
        b_bg = const("b_bg", io["b_bg"], H, 2)
        ln_w = const("ln_w", vec("ln_w"), P, DT, 1)
        ln_b = const("ln_b", vec("ln_b"), P, DT, 1)

        a_neg = sb("a_neg", P, IT, NS)
        nb_bg = sb("nb_bg", H, 2)
        eps = sb("eps", P, 3)
        ones = sb("ones", P, T)
        x = sb("x", P, DT, T)
        cx = sb("cx", P, DT, T)
        cen = sb("cen", P, DT, T)
        sq = sb("sq", P, DT, T)
        xn = sb("xn", P, DT, T)
        xl = sb("xl", P, DT, T)
        lnv = sb("lnv", P, T)
        rstd = sb("rstd", P, T)
        bg = sb("bg", H, 2, T)
        xpad = sb("xpad", P, IT, T + DC - 1)
        zs = sb("zs", P, IT, T)
        e1 = sb("e1", P, IT, T)
        e2 = sb("e2", P, IT, T)
        cv = sb("cv", P, IT, T)
        dbl = sb("dbl", 48, T)
        dt = sb("dt", P, IT, T)
        u = sb("u", P, IT, T)
        da = sb("da", P, 2, IT, T)
        hs = sb("hs", P, 2, IT, T)
        bu = e1
        y = e2
        cv_x = cv
        rl = xpad[:, :, DC - 1:]
        eqk = hs
        vs = zs
        qf, kf, kvp, kvs, kss = (u[:, 0, :], u[:, 1, :], u[:, 2, :], u[:, 3, :], dt[:, 0, :])
        rt, tt = dt[:, 1, :], dt[:, 2, :]
        prod = cv
        ov = da[:, :, :, :].rearrange("p a b t -> p (a b) t")
        hid = hs[:, :, :, :].rearrange("p a b t -> p (a b) t")

        n_load = len(load_list)
        consts_in, setup = sig("consts_in", n_load, 16), sig("setup", 7)
        a_capped, setup_act = sig("a_capped"), sig("setup_act")
        x_in, cx_in = sig("x_in", 1, 16), sig("cx_in", 1, 16)
        saved_x, saved_xn, saved_bg = sig("saved_x", 1, 16), sig("saved_xn", 1, 16), sig("saved_bg", 2, 16)
        ln_mean, ln_cent, ln_sq, ln_var, ln_log, ln_rstd, ln_out = [
            sig(n, 5) for n in ("ln_mean", "ln_cent", "ln_sq", "ln_var", "ln_log", "ln_rstd", "ln_out")]
        xz, xin, zgate, conv = sig("xz", 8), sig("xin", IT), sig("zgate", IT), sig("conv", IT)
        xcv, dbl_ps, dbl_sb, dtp = sig("xcv", IT), sig("dbl_ps"), sig("dbl_sb"), sig("dtp", IT)
        dt_pre, spl, dt_ready, u_ready = sig("dt_pre"), sig("spl"), sig("dt_ready"), sig("u_ready")
        bn, cn, daexp, damax = sig("bn", NS), sig("cn", NS), sig("daexp", NS), sig("damax", NS)
        bu_ready, scanned, yn, yacc = sig("bu_ready", NS), sig("scanned", NS), sig("yn", NS), sig("yacc", NS)
        ygate, ysq, yvar, yrstd, ynorm, a_out = [sig(n) for n in ("ygate", "ysq", "yvar", "yrstd", "ynorm", "a_out")]
        x_a, x_b, x_c, x_d = [sig(n) for n in ("x_a", "x_b", "x_c", "x_d")]
        qkv, aqkv, emin, feat, prods, nd, ratio, ovs = [
            sig(n, HP) for n in ("qkv", "aqkv", "emin", "feat", "prods", "nd", "ratio", "ovs")]
        den, den_inv = sig("den", HP), sig("den_inv", HP)
        b_out, hid_ps, hid_sb, c_out = sig("b_out"), sig("hid_ps", FT), sig("hid_sb", FT), sig("c_out")
        gate_ps, gates = sig("gate_ps"), sig("gates")
        dve_links, act_links = sig("dve_links", 32), sig("act_links", 5 + HP)

        pool_turns, sp_turns = sig("pool_turns"), sig("sp_turns")

        block = ctx.enter_context(nc.Block())

        @block.sync
        def _(sp):
            for dst, src in load_list:
                sp.dma_start(dst, src).then_inc(consts_in.sem, 16)

            def load_x(b):
                sp.dma_start(x[:, :, :], io["x"].rearrange("(k p) t -> p k t", p=P)[:, :, bass.ds(b * T, T)]).then_inc(x_in.sem, 16)

            def held(*at):
                sp.wait_ge(*at)
                sp.sem_inc(sp_turns.sem, 1)

            def batch(b, more):
                sp.dma_start(cx[:, :, :], io["ctx"].rearrange("(k p) t -> p k t", p=P)[:, :, bass.ds(b * T, T)]).then_inc(cx_in.sem, 16)
                held(*x_d(b, 1))
                sp.dma_start(scratch["x"].rearrange("(k p) t -> p k t", p=P)[:, :, bass.ds(b * T, T)], x[:, :, :]).then_inc(saved_x.sem, 16)
                held(*saved_x(b, 1))
                if more:
                    load_x(b + 1)
                held(*ln_out(b, 5))
                sp.dma_start(scratch["x2"].rearrange("(k p) t -> p k t", p=P)[:, :, bass.ds(b * T, T)], xn[:, :, :]).then_inc(saved_xn.sem, 16)
                held(*gates(b, 1))
                for g, name in enumerate(("beta", "gamma")):
                    sp.dma_start(scratch[name][:, bass.ds(b * T, T)], bg[:, g, :]).then_inc(saved_bg.sem, 16)
                held(*saved_xn(b, 1))
                held(*saved_bg(b, 2))

            load_x(0)
            with sp.Fori(0, B - 1) as b:
                batch(b, True)
            batch(B - 1, False)

        @block.tensor
        def _(pe):
            mm = pe.matmul

            def norm(b, k, src):
                for j in range(DT):
                    i = mm(ps[0][:, :], mean_d[:, :], src[:, j, :], start=(j == 0), stop=(j == DT - 1))
                i.then_inc(ln_mean.sem, 1)
                pe.wait_ge(*ln_sq(b, k))
                for j in range(DT):
                    i = mm(ps[1][:, :], mean_d[:, :], sq[:, j, :], start=(j == 0), stop=(j == DT - 1))
                i.then_inc(ln_var.sem, 1)

            pe.wait_ge(*consts_in(0, n_load))
            with pe.Fori(0, B) as b:
                pe.wait_ge(*x_in(b, 1))
                norm(b, 1, x)
                pe.wait_ge(*ln_out(b, 1))
                for m in range(2 * IT):
                    for k in range(DT):
                        i = mm(ps[m][:, :], w_in[:, k, m * P:(m + 1) * P], xn[:, k, :], start=(k == 0), stop=(k == DT - 1))
                    i.then_inc(xz.sem, 1)
                pe.wait_ge(*xcv(b, IT))
                for k in range(IT):
                    i = mm(ps[0][0:48, :], w_x[:, k, :], cv_x[:, k, :], start=(k == 0), stop=(k == IT - 1))
                i.then_inc(dbl_ps.sem, 1)
                pe.wait_ge(*dbl_sb(b, 1))
                for m in range(IT):
                    mm(ps[1 + m][:, :], w_dt[:, m * P:(m + 1) * P], dbl[0:RK, :], start=True, stop=True).then_inc(dtp.sem, 1)
                pe.wait_ge(*dt_ready(b, 1))

                def spread(n):
                    if n >= 2:
                        pe.wait_ge(*bu_ready(b, n - 1))
                    mm(ps[n % 2][:, :], sel[:, n, :], dbl[:, :], start=True, stop=True).then_inc(bn.sem, 1)
                    if n >= 2:
                        pe.wait_ge(*yn(b, n - 1))
                    mm(ps[2 + n % 2][:, :], sel[:, NS + n, :], dbl[:, :], start=True, stop=True).then_inc(cn.sem, 1)

                spread(0)
                for n in range(NS):
                    if n + 1 < NS:
                        spread(n + 1)
                    pe.wait_ge(*yn(b, n + 1))
                    for m in range(IT):
                        i = mm(ps[4 + m][:, :], ident[:, :], hs[:, n % 2, m, :], start=(n == 0), stop=(n == NS - 1))
                    i.then_inc(yacc.sem, 1)
                pe.wait_ge(*ysq(b, 1))
                for m in range(IT):
                    i = mm(ps[0][:, :], mean_di[:, :], u[:, m, :], start=(m == 0), stop=(m == IT - 1))
                i.then_inc(yvar.sem, 1)
                pe.wait_ge(*ynorm(b, 1))
                for m in range(DT):
                    for k in range(IT):
                        i = mm(ps[1 + m][:, :], w_out[:, k, m * P:(m + 1) * P], y[:, k, :], start=(k == 0), stop=(k == IT - 1))
                i.then_inc(a_out.sem, 1)

                pe.wait_ge(*x_a(b, 1))
                norm(b, 2, x)
                pe.wait_ge(*ln_out(b, 2))

                def project(hp):
                    s = 3 * (hp % 2)
                    if hp >= 2:
                        pe.wait_ge(*feat(b, hp - 1))
                        pe.wait_ge(*aqkv(b, hp - 1))
                    for o, w, src in ((0, w_q, xn), (1, w_k, cx), (2, w_v, cx)):
                        for k in range(DT):
                            i = mm(ps[s + o][:, :], w[:, k, hp * P:(hp + 1) * P], src[:, k, :], start=(k == 0), stop=(k == DT - 1))
                    i.then_inc(qkv.sem, 1)

                pe.wait_ge(*cx_in(b, 1))
                project(0)
                for hp in range(HP):
                    if hp + 1 < HP:
                        project(hp + 1)
                    pe.wait_ge(*prods(b, hp + 1))
                    if hp >= 1:
                        pe.wait_ge(*ratio(b, hp))
                    mm(ps[6][:, :], pair_sum[:, :], prod[:, 2 * (hp % 2), :], start=True, stop=True)
                    mm(ps[7][:, :], pair_sum[:, :], prod[:, 2 * (hp % 2) + 1, :], start=True, stop=True).then_inc(nd.sem, 1)
                pe.wait_ge(*ovs(b, HP))
                for m in range(DT):
                    for k in range(HP):
                        i = mm(ps[m][:, :], w_o[:, k, m * P:(m + 1) * P], ov[:, k, :], start=(k == 0), stop=(k == HP - 1))
                i.then_inc(b_out.sem, 1)

                pe.wait_ge(*x_b(b, 1))
                norm(b, 3, x)
                pe.wait_ge(*ln_out(b, 3))
                for m in range(FT):
                    for k in range(DT):
                        i = mm(ps[m][:, :], w_1[:, k, m * P:(m + 1) * P], xn[:, k, :], start=(k == 0), stop=(k == DT - 1))
                    i.then_inc(hid_ps.sem, 1)
                pe.wait_ge(*hid_sb(b, 2))
                for k in range(FT):
                    pe.wait_ge(*hid_sb(b, k + 1))
                    for m in range(DT):
                        i = mm(ps[m][:, :], w_2[:, k, m * P:(m + 1) * P], hid[:, k, :], start=(k == 0), stop=(k == FT - 1))
                i.then_inc(c_out.sem, 1)

                pe.wait_ge(*x_c(b, 1))
                norm(b, 4, x)
                pe.wait_ge(*ln_out(b, 4))
                norm(b, 5, xl)
                pe.wait_ge(*ln_out(b, 5))
                for g in range(2):
                    for k in range(DT):
                        i = mm(ps[2 + g][0:H, :], w_bg[:, k, g * H:(g + 1) * H], xn[:, k, :], start=(k == 0), stop=(k == DT - 1))
                i.then_inc(gate_ps.sem, 1)

        @block.scalar
        def _(act):
            A = act.activation

            def norm(b, k, links):
                act.wait_ge(*ln_cent(b, k))
                A(sq[:, :, :], cen[:, :, :], ACT.Square).then_inc(ln_sq.sem, 1)
                act.wait_ge(*ln_var(b, k))
                A(lnv[:, :], ps[1][:, :], ACT.Ln, bias=eps[:, 0:1]).then_inc(ln_log.sem, 1)
                act.wait_ge(*ln_log(b, k))
                A(rstd[:, :], lnv[:, :], ACT.Exp, scale=-0.5).then_inc(ln_rstd.sem, 1)

            act.wait_ge(*consts_in(0, n_load))
            act.wait_ge(*a_capped(0, 1))
            A(a_neg[:, :, :], a_neg[:, :, :], ACT.Exp).then_inc(setup_act.sem, 1)
            act.wait_ge(*setup(0, 7))
            with act.Fori(0, B) as b:
                ch = Chain(act_links, act, b)
                norm(b, 1, ch)
                for m in range(IT):
                    act.wait_ge(*xz(b, m + 1))
                    A(xpad[:, m, DC - 1:], ps[m][:, :], ACT.Copy).then_inc(xin.sem, 1)
                for m in range(IT):
                    act.wait_ge(*xz(b, IT + m + 1))
                    A(zs[:, m, :], ps[IT + m][:, :], ACT.Silu).then_inc(zgate.sem, 1)
                for m in range(IT):
                    act.wait_ge(*conv(b, m + 1))
                    A(cv_x[:, m, :], cv[:, m, :], ACT.Silu).then_inc(xcv.sem, 1)
                act.wait_ge(*dbl_ps(b, 1))
                A(dbl[:, :], ps[0][0:48, :], ACT.Copy).then_inc(dbl_sb.sem, 1)
                act.wait_ge(*dt_pre(b, 1))
                ch.link(A(e1[:, :, :], rl, ACT.Abs))
                i = A(e1[:, :, :], e1[:, :, :], ACT.Exp, scale=-1.0)
                ch.link(i)
                A(e1[:, :, :], e1[:, :, :], ACT.Ln, bias=1.0).then_inc(spl.sem, 1)
                act.wait_ge(*dt_ready(b, 1))
                for n in range(NS):
                    if n >= 2:
                        act.wait_ge(*scanned(b, n - 1))
                    for m in range(IT):
                        i = A(da[:, n % 2, m, 1:T], dt[:, m, 1:T], ACT.Exp, scale=a_neg[:, m, n:n + 1])
                    i.then_inc(daexp.sem, 1)
                act.wait_ge(*ygate(b, 1))
                A(u[:, :, :], y[:, :, :], ACT.Square).then_inc(ysq.sem, 1)
                act.wait_ge(*yvar(b, 1))
                i = A(lnv[:, :], ps[0][:, :], ACT.Ln, bias=eps[:, 1:2])
                ch.link(i)
                A(rstd[:, :], lnv[:, :], ACT.Exp, scale=-0.5).then_inc(yrstd.sem, 1)
                norm(b, 2, ch)

                def invert_den(hp):
                    act.wait_ge(*den(b, hp + 1))
                    ch.link(A(rt, rt, ACT.Ln, scale=DEN_SCALE))
                    A(rt, rt, ACT.Exp, scale=-1.0, bias=eps[:, 2:3]).then_inc(den_inv.sem, 1)

                for hp in range(HP):
                    s = hp % 2
                    act.wait_ge(*qkv(b, hp + 1))
                    if hp >= 2:
                        act.wait_ge(*feat(b, hp - 1))
                        act.wait_ge(*ratio(b, hp - 1))
                    A(eqk[:, s, 0, :], ps[3 * s][:, :], ACT.Exp)
                    A(eqk[:, s, 1, :], ps[3 * s + 1][:, :], ACT.Exp)
                    A(vs[:, s, :], ps[3 * s + 2][:, :], ACT.Copy).then_inc(aqkv.sem, 1)
                    if hp >= 1:
                        invert_den(hp - 1)
                invert_den(HP - 1)
                norm(b, 3, ch)
                for m in range(FT):
                    act.wait_ge(*hid_ps(b, m + 1))
                    A(hid[:, m, :], ps[m][:, :], ACT.Gelu, bias=b_1[:, m, :]).then_inc(hid_sb.sem, 1)
                norm(b, 4, ch)
                norm(b, 5, ch)
                act.wait_ge(*gate_ps(b, 1))
                for g in range(2):
                    i = A(bg[:, g, :], ps[2 + g][0:H, :], ACT.Exp, scale=-1.0, bias=nb_bg[:, g:g + 1])
                ch.link(i)
                ch.link(A(bg[:, :, :], bg[:, :, :], ACT.Ln, bias=1.0))
                A(bg[:, :, :], bg[:, :, :], ACT.Exp, scale=-1.0).then_inc(gates.sem, 1)
                ch.close()

        @block.gpsimd
        def _(pool):
            with pool.Fori(0, B) as b:
                for n in range(NS):
                    pool.wait_ge(*daexp(b, n + 1))
                    pool.sem_inc(pool_turns.sem, 1)
                    pool.tensor_scalar(da[:, n % 2, :, 1:T], da[:, n % 2, :, 1:T], E10, None, ALU.max).then_inc(damax.sem, 1)
                for hp in range(HP):
                    pool.wait_ge(*aqkv(b, hp + 1))
                    pool.sem_inc(pool_turns.sem, 1)
                    pool.tensor_scalar(eqk[:, hp % 2, 0:2, :], eqk[:, hp % 2, 0:2, :], 1.0, None, ALU.min).then_inc(emin.sem, 1)

        @block.vector
        def _(dve):
            dve.memset(xpad[:, :, 0:DC - 1], 0.0).then_inc(setup.sem, 1)
            dve.memset(ones[:, :], 1.0).then_inc(setup.sem, 1)
            dve.memset(eps[:, 0:1], 1e-5).then_inc(setup.sem, 1)
            dve.memset(eps[:, 1:2], 1e-6).then_inc(setup.sem, 1)
            dve.memset(eps[:, 2:3], float(np.log(DEN_SCALE))).then_inc(setup.sem, 1)
            dve.wait_ge(*consts_in(0, n_load))
            dve.tensor_scalar(nb_bg[:, :], b_bg[:, :], -1.0, None, ALU.mult).then_inc(setup.sem, 1)
            dve.tensor_scalar(a_neg[:, :, :], a_log[:, :, :], 14.0, None, ALU.min).then_inc(a_capped.sem, 1)
            dve.wait_ge(*setup_act(0, 1))
            dve.tensor_scalar(a_neg[:, :, :], a_neg[:, :, :], -1.0, None, ALU.mult).then_inc(setup.sem, 1)
            dve.wait_ge(*setup(0, 7))

            def norm(b, k, src, out):
                dve.wait_ge(*ln_mean(b, k))
                dve.tensor_tensor(cen[:, :, :], src[:, :, :], wide(ps[0][:, :], DT), ALU.subtract).then_inc(ln_cent.sem, 1)
                dve.wait_ge(*ln_rstd(b, k))
                return dve.tensor_tensor(out[:, :, :], cen[:, :, :], wide(rstd[:, :], DT), ALU.mult)

            with dve.Fori(0, B) as b:
                ch = Chain(dve_links, dve, b)
                norm(b, 1, x, xn).then_inc(ln_out.sem, 1)
                for m in range(IT):
                    dve.wait_ge(*xin(b, m + 1))
                    ch.link(dve.tensor_scalar(cv[:, m, :], xpad[:, m, 0:T], conv_w[:, m, 0:1], conv_b[:, m, :], ALU.mult, ALU.add))
                    for k in range(1, DC):
                        i = dve.scalar_tensor_tensor(cv[:, m, :], xpad[:, m, k:k + T], conv_w[:, m, k:k + 1], cv[:, m, :], ALU.mult, ALU.add)
                        if k < DC - 1:
                            ch.link(i)
                    i.then_inc(conv.sem, 1)
                dve.wait_ge(*xcv(b, IT))
                for m in range(IT):
                    dve.wait_ge(*dtp(b, m + 1))
                    i = dve.tensor_scalar(rl[:, m, :], ps[1 + m][:, :], b_dt[:, m, :], None, ALU.add)
                i.then_inc(dt_pre.sem, 1)
                dve.wait_ge(*spl(b, 1))
                ch.link(dve.scalar_tensor_tensor(dt[:, :, :], rl, 0.0, e1[:, :, :], ALU.max, ALU.add))
                dve.tensor_scalar(dt[:, :, :], dt[:, :, :], 1e-4, None, ALU.add).then_inc(dt_ready.sem, 1)
                dve.wait_ge(*dt_ready(b, 1))
                dve.tensor_tensor(u[:, :, :], dt[:, :, :], cv_x[:, :, :], ALU.mult).then_inc(u_ready.sem, 1)
                dve.wait_ge(*u_ready(b, 1))
                ch.link(dve.memset(da[:, :, :, 0:1], 0.0))
                for n in range(NS):
                    dve.wait_ge(*bn(b, n + 1))
                    if n >= 1:
                        dve.wait_ge(*scanned(b, n))
                    dve.tensor_tensor(bu[:, :, :], u[:, :, :], wide(ps[n % 2][:, :], IT), ALU.mult).then_inc(bu_ready.sem, 1)
                    dve.wait_ge(*bu_ready(b, n + 1))
                    dve.wait_ge(*damax(b, n + 1))
                    if n >= 2:
                        dve.wait_ge(*yacc(b, n - 1))
                    dve.tensor_tensor_scan(hs[:, n % 2, :, :].rearrange("p m t -> p (m t)"),
                                           da[:, n % 2, :, :].rearrange("p m t -> p (m t)"),
                                           bu[:, :, :].rearrange("p m t -> p (m t)"), 0.0, ALU.mult, ALU.add).then_inc(scanned.sem, 1)
                    dve.wait_ge(*scanned(b, n + 1))
                    dve.wait_ge(*cn(b, n + 1))
                    dve.tensor_tensor(hs[:, n % 2, :, :], hs[:, n % 2, :, :], wide(ps[2 + n % 2][:, :], IT), ALU.mult).then_inc(yn.sem, 1)
                dve.wait_ge(*yacc(b, NS))
                for m in range(IT):
                    i = dve.scalar_tensor_tensor(y[:, m, :], cv_x[:, m, :], skip_d[:, m, :], ps[4 + m][:, :], ALU.mult, ALU.add)
                ch.link(i)
                dve.wait_ge(*zgate(b, IT))
                dve.tensor_tensor(y[:, :, :], y[:, :, :], zs[:, :, :], ALU.mult).then_inc(ygate.sem, 1)
                dve.wait_ge(*ygate(b, 1))
                dve.wait_ge(*yrstd(b, 1))
                for m in range(IT):
                    i = dve.scalar_tensor_tensor(y[:, m, :], y[:, m, :], rms_w[:, m, :], rstd[:, :], ALU.mult, ALU.mult)
                i.then_inc(ynorm.sem, 1)
                dve.wait_ge(*a_out(b, 1))
                for m in range(DT):
                    i = dve.tensor_tensor(x[:, m, :], x[:, m, :], ps[1 + m][:, :], ALU.add)
                i.then_inc(x_a.sem, 1)

                dve.wait_ge(*x_a(b, 1))
                norm(b, 2, x, xn).then_inc(ln_out.sem, 1)

                def divide(hp):
                    dve.wait_ge(*den_inv(b, hp + 1))
                    dve.wait_ge(*ratio(b, hp + 1))
                    dve.tensor_tensor(ov[:, hp, :], tt, rt, ALU.mult).then_inc(ovs.sem, 1)

                def floor(hp):
                    dve.wait_ge(*nd(b, hp + 1))
                    dve.tensor_scalar(rt, ps[7][:, :], 1e-12, None, ALU.max).then_inc(den.sem, 1)
                    dve.tensor_tensor(tt, ps[6][:, :], vs[:, hp % 2, :], ALU.mult).then_inc(ratio.sem, 1)

                for hp in range(HP):
                    s = hp % 2
                    dve.wait_ge(*emin(b, hp + 1))
                    dve.scalar_tensor_tensor(qf, ps[3 * s][:, :], 0.0, eqk[:, s, 0, :], ALU.max, ALU.add)
                    dve.scalar_tensor_tensor(kf, ps[3 * s + 1][:, :], 0.0, eqk[:, s, 1, :], ALU.max, ALU.add).then_inc(feat.sem, 1)
                    dve.wait_ge(*feat(b, hp + 1))
                    ch.link(dve.tensor_tensor(kvp, kf, vs[:, s, :], ALU.mult))
                    dve.tensor_tensor_scan(kvs, ones[:, :], kvp, 0.0, ALU.mult, ALU.add)
                    ch.link(dve.tensor_tensor_scan(kss, ones[:, :], kf, 0.0, ALU.mult, ALU.add))
                    if hp >= 2:
                        dve.wait_ge(*nd(b, hp - 1))
                    dve.tensor_tensor(prod[:, 2 * s, :], qf, kvs, ALU.mult)
                    dve.tensor_tensor(prod[:, 2 * s + 1, :], qf, kss, ALU.mult).then_inc(prods.sem, 1)
                    dve.wait_ge(*prods(b, hp + 1))
                    if hp >= 2:
                        divide(hp - 2)
                        dve.wait_ge(*ovs(b, hp - 1))
                    if hp >= 1:
                        floor(hp - 1)
                divide(HP - 2)
                dve.wait_ge(*ovs(b, HP - 1))
                floor(HP - 1)
                divide(HP - 1)
                dve.wait_ge(*b_out(b, 1))
                for m in range(DT):
                    i = dve.tensor_tensor(x[:, m, :], x[:, m, :], ps[m][:, :], ALU.add)
                i.then_inc(x_b.sem, 1)

                dve.wait_ge(*x_b(b, 1))
                norm(b, 3, x, xn).then_inc(ln_out.sem, 1)
                dve.wait_ge(*c_out(b, 1))
                for m in range(DT):
                    i = dve.scalar_tensor_tensor(x[:, m, :], ps[m][:, :], b_2[:, m, :], x[:, m, :], ALU.add, ALU.add)
                i.then_inc(x_c.sem, 1)

                dve.wait_ge(*x_c(b, 1))
                norm(b, 4, x, xl).then_inc(ln_out.sem, 1)
                dve.wait_ge(*ln_out(b, 4))
                dve.tensor_tensor(x[:, :, :], x[:, :, :], xl[:, :, :], ALU.add).then_inc(x_d.sem, 1)
                ch.link(norm(b, 5, xl, xn))
                for m in range(DT):
                    i = dve.tensor_scalar(xn[:, m, :], xn[:, m, :], ln_w[:, m, :], ln_b[:, m, :], ALU.mult, ALU.add)
                i.then_inc(ln_out.sem, 1)
                dve.wait_ge(*saved_xn(b, 1))
                ch.close()
    return signals


def delta_rule(nc, io, scratch):
    C = 32
    QB = P // C
    GB = 4
    GT = GB * T
    U_ = GT // P
    UB = T // P
    NC_ = T // C
    PASSES = 2
    LMAX = 85.0

    signals = []
    with ExitStack() as ctx:
        def sb(name, *shape):
            return ctx.enter_context(nc.sbuf_tensor("d_" + name, list(shape), F32))

        def sig(name, per=1, step=1):
            return Signal(signals, nc, "d_" + name, per, step)

        ps = [ctx.enter_context(nc.psum_tensor(f"d_bank{i}", [P, T], F32)) for i in range(8)]
        pair_sum = sb("pair_sum", P, P)
        ident = sb("ident", P, P)
        ident2 = sb("ident2", P, DH)
        masks = sb("masks", P, 2, P)
        minus_before = sb("minus_before", P, C)
        restart = sb("restart", P, T)
        w = sb("w", P, DT, 5, P)
        nba = sb("nba", P, 2)
        gate = sb("gate", P, PASSES, C)
        gend = sb("gend", P, PASSES, U_ * QB)
        kn = sb("kn", P, GT)
        q = sb("q", P, GT)
        L = [sb("L0", P, GT), sb("L1", P, GT)]
        v = sb("v", P, GT)
        o = L[0]
        mov = sb("mov", P, 3, GT)
        km = sb("km", P, GT)
        apm = sb("apm", P, 2 * U_, 3, P)
        tok = sb("tok", P, U_, 4, DH)
        ke = sb("ke", P, U_, P)
        z = sb("z", P, U_, 4 * DH)
        xg = z[:, :, :].rearrange("p u n -> p (u n)").rearrange("p (k t) -> p k t", k=DT)
        state = sb("state", P, NC_, GB, DH)
        phi = sb("phi", P, NC_, GB, DH)
        early = state[:, :, :, :].rearrange("p c b d -> p (c b d)")
        x_r = sb("x_r", P, C * C)
        x_of = [early[:, 0:C * C], x_r[:, :]]
        pr_of = [early[:, 3 * C * C:3 * C * C + C * C // 4], sb("pr_r", P, C * C // 4)[:, :]]
        blocks = [early[:, (1 + s) * C * C:(2 + s) * C * C].rearrange("p (n t) -> p n t", t=C) for s in range(PASSES)]
        tmp = phi[:, :, :, :].rearrange("p c b d -> p (c b d)")
        ksq, rn = [[tmp[:, (2 * n + m) * T:(2 * n + m + 1) * T] for n in range(2)] for m in range(2)]
        gm, kend = ksq, rn
        gp = [tmp[:, 4 * T + n * NC_ * (C + 1):4 * T + (n + 1) * NC_ * (C + 1)].rearrange("p (c t) -> p c t", t=C + 1) for n in range(2)]

        loads = [(pair_sum[:, :], io["c_pair"]), (ident[:, :], io["c_ident"]), (ident2[:, :], io["c_ident2"]),
                 (masks[:, :, :], io["c_masks"].rearrange("p (m t) -> p m t", m=2)), (minus_before[:, :], io["c_minus_before"]), (restart[:, :], io["c_restart"])]
        consts_in = sig("consts_in", len(loads), 16)
        inputs_in = sig("inputs_in", 7, 16)
        stored = sig("stored", 1, 16)
        neg_ba = sig("neg_ba")
        kproj, proj, ksq_r, ss, ssc, rn_r, kn_r = [sig(n, GB) for n in ("kproj", "proj", "ksq", "ss", "ssc", "rn", "kn")]
        la, lsum, lcap, q_r = sig("la", GB), sig("lsum", GB), sig("lcap", GB), sig("q")
        late, late_sb, la_r, lsum_r, lcap_r, kpm_r = [sig(n, GB) for n in ("late", "late_sb", "la_r", "lsum_r", "lcap_r", "kpm_r")]
        trv, trv_sb = sig("trv", GB), sig("trv_sb", GB)
        gexp = sig("gexp", (PASSES + 1) * GB)
        kpm = sig("kpm", GB)
        kend_r, movs = sig("kend", PASSES * GB), sig("movs", PASSES * GB)
        ablk, ablk_sb = sig("ablk", PASSES), sig("ablk_sb", PASSES)
        tr, tr_sb = sig("tr", PASSES * GB), sig("tr_sb", PASSES * GB)
        PM = [U_, 2 * GB]
        score, score_sb = sig("score", sum(PM)), sig("score_sb", sum(PM))
        nt_out, nt_in, x_out, x_back = [sig(n, PASSES * k, 16) for n, k in (("nt_out", 1), ("nt_in", 1), ("x_out", 1), ("x_back", QB))]
        xi_s, xi_r = sig("xi_s"), sig("xi_r")
        zp, z_sb = sig("zp", PASSES * U_ // 2), sig("z_sb", PASSES * U_ // 2)
        px, px_sb = sig("px", PASSES * U_ // 2), sig("px_sb", PASSES * U_ // 2)
        pp, phi_sb, psi_sb = [sig(n, PASSES * GB) for n in ("pp", "phi_sb", "psi_sb")]
        state0, apm0 = sig("state0"), sig("apm0")
        STEPS = NC_ - 1
        step_ps, step_sb = sig("step_ps", PASSES * STEPS), sig("step_sb", PASSES * STEPS)
        outp, out_sb = sig("outp", PASSES * GB * 2), sig("out_sb", PASSES * GB * 2)
        dve_links, act_links, pool_links = sig("dve_links", 1 + 2 + 2 + GB + 2 * GB + 2 * (C - 2)), sig("act_links", 2 * GB), sig("pool_links", 2 + 2 * (C - 2))
        pe_turns, sp_turns, act_turns, pool_turns = sig("pe_turns"), sig("sp_turns"), sig("act_turns"), sig("pool_turns")

        def invert(eng, ch, s, done, at_step=()):
            x = x_of[s].rearrange("p (s t) -> p s t", s=C)
            g = gate[:, s, :]
            ch.link(eng.tensor_tensor(x, x, g.unsqueeze(1).broadcast_to([P, C, C]), ALU.mult))
            for j in range(1, C - 1):
                n = C - 1 - j
                through = pr_of[s][:, 0:j * n].rearrange("p (m i) -> p m i", m=j)
                ch.link(eng.tensor_tensor(through, x[:, 0:j, j:j + 1].broadcast_to([P, j, n]), x[:, j:j + 1, j + 1:].broadcast_to([P, j, n]), ALU.mult))
                ch.link(eng.tensor_tensor(x[:, 0:j, j + 1:], x[:, 0:j, j + 1:], through, ALU.add))
                if j in at_step:
                    at_step[j]()
            ch.link(eng.tensor_tensor(x, x, g.unsqueeze(2).broadcast_to([P, C, C]), ALU.mult))
            diagonal = x_of[s][:, 0:C * C:C + 1]
            eng.tensor_tensor(diagonal, diagonal, g, ALU.add).then_inc(done.sem, 1)

        block = ctx.enter_context(nc.Block())

        @block.sync
        def _(sp):
            def held(*at):
                sp.wait_ge(*at)
                sp.sem_inc(sp_turns.sem, 1)

            for dst, src in loads:
                sp.dma_start(dst, src).then_inc(consts_in.sem, 16)
            with sp.Fori(0, HP) as hp:
                with sp.Fori(0, 2) as g:
                    i = hp * 2 + g
                    sp.dma_start(w[:, :, :, :], io["w_d"].rearrange("p (k n m) -> p k n m", k=DT, n=5)[bass.ds(hp * P, P)]).then_inc(inputs_in.sem, 16)
                    sp.dma_start(nba[:, :], io["b_a"][bass.ds(hp * P, P), :]).then_inc(inputs_in.sem, 16)
                    sp.dma_start(xg, scratch["x2"].rearrange("(k p) t -> p k t", p=P)[:, :, bass.ds(g * GT, GT)]).then_inc(inputs_in.sem, 16)
                    for s, name in enumerate(("beta", "gamma")):
                        for e in range(2):
                            src = scratch[name][bass.ds(hp * 2 + e, 1), bass.ds(g * GT, GT)].rearrange("e (u t) -> (e u) t", t=C)
                            sp.dma_start(gate[e * DH:(e + 1) * DH, s, :], src).then_inc(inputs_in.sem, 16)
                    nt = scratch["nt"].rearrange("p m -> (p m)").rearrange("(n p t) -> p n t", n=2 * U_, t=C)
                    xt = scratch["xt"].rearrange("(n q) (s t) -> q s n t", q=QB, t=C)
                    for s in range(PASSES):
                        held(*ablk_sb(i, s + 1))
                        sp.dma_start(nt, blocks[s]).then_inc(nt_out.sem, 16)
                        held(*nt_out(i, s + 1))
                        sp.dma_start(x_of[s], scratch["nt"]).then_inc(nt_in.sem, 16)
                        if s == 0:
                            held(*apm0(0, 1))
                        else:
                            held(*zp(i, U_ // 2))
                        held(*(xi_s, xi_r)[s](i, 1))
                        sp.dma_start(scratch["xt"], x_of[s]).then_inc(x_out.sem, 16)
                        held(*x_out(i, s + 1))
                        for c in range(QB):
                            sp.dma_start(apm[c * C:(c + 1) * C, :, 0, c * C:(c + 1) * C], xt[c]).then_inc(x_back.sem, 16)
                    held(*x_back(i, PASSES * QB))
                    held(*px(i, PASSES * U_ // 2))
                    held(*pp(i, PASSES * GB))

        def vk(e):
            return (1, 0) if e == 0 else (2, 3)

        @block.tensor
        def _(pe):
            mm = pe.matmul

            def held(*at):
                pe.wait_ge(*at)
                pe.sem_inc(pe_turns.sem, 1)

            pe.wait_ge(*consts_in(0, len(loads)))
            with pe.Fori(0, HP) as hp:
                with pe.Fori(0, 2) as g:
                    i = hp * 2 + g
                    held(*inputs_in(i, 7))
                    for b in range(GB):
                        if b >= 2:
                            held(*la(i, b - 1))
                            held(*kn_r(i, b - 1))
                        for n in range(3):
                            bank = (0, 1, 2, 6, 3, 4)[3 * (b % 2) + n]
                            for k in range(DT):
                                j = mm(ps[bank][:, :], w[:, k, n, :], xg[:, k, b * T:(b + 1) * T], start=(k == 0), stop=(k == DT - 1))
                            if n == 0:
                                j.then_inc(kproj.sem, 1)
                        j.then_inc(proj.sem, 1)
                        held(*ksq_r(i, b + 1))
                        mm(ps[5 + 2 * (b % 2)][:, :], pair_sum[:, :], ksq[b % 2], start=True, stop=True).then_inc(ss.sem, 1)

                    def chunk_blocks(s, b):
                        held(*(kpm, kpm_r)[s](i, b + 1))
                        for u in range(b * UB, (b + 1) * UB):
                            for e in range(2):
                                for c in range(QB):
                                    at = slice(u * P + c * C, u * P + (c + 1) * C)
                                    j = mm(ps[6 - 4 * s + e][c * C:(c + 1) * C, u * C:(u + 1) * C], km[e * DH:(e + 1) * DH, at], mov[e * DH:(e + 1) * DH, 0, at],
                                           start=True, stop=True, tile_position=(e * DH, c * C))
                        return j

                    for b in range(GB):
                        j = chunk_blocks(0, b)
                    j.then_inc(ablk.sem, 1)
                    for s in range(PASSES):
                        m1 = slice(1, 3) if s == 0 else slice(2, 3)
                        nk = m1.stop - m1.start
                        each = 4 // nk
                        for b in range(GB):
                            held(*kend_r(i, s * GB + b + 1))
                            if b == 0 and s == 0:
                                held(*q_r(i, 1))
                                held(*kn_r(i, GB))
                            if s == 1:
                                held(*out_sb(i, GB + b + 1))
                            if b >= 1:
                                held(*tr_sb(i, s * GB + b))
                            for u in range(UB):
                                at = slice(b * T + u * P, b * T + (u + 1) * P)
                                pe.transpose(ps[0][:, u * P:(u + 1) * P], mov[:, 0, at], ident[:, :])
                                if s == 1:
                                    pe.transpose(ps[1][:, u * P:(u + 1) * P], v[:, at], ident[:, :])
                                j = pe.transpose(ps[2][:, u * P:(u + 1) * P], kend[b % 2][:, u * P:(u + 1) * P], ident[:, :])
                            j.then_inc(tr.sem, 1)
                            held(*movs(i, s * GB + b + 1))
                            for first in range(b * UB, (b + 1) * UB, each):
                                for e in range(2):
                                    k = first // each * 2 + e
                                    if s == 0 and k == 2:
                                        held(*ablk_sb(i, 1))
                                    if s == 1 and k == 0:
                                        held(*out_sb(i, GB * 2))
                                    if k >= 4:
                                        held(*score_sb(i, s * PM[0] + k - 3))
                                    for n in range(each):
                                        at = slice((first + n) * P, (first + n + 1) * P)
                                        j = mm(ps[4 + k % 4][:, n * nk * P:(n + 1) * nk * P], km[e * DH:(e + 1) * DH, at], mov[e * DH:(e + 1) * DH, m1, at],
                                               start=True, stop=True)
                                    j.then_inc(score.sem, 1)
                        held(*tr_sb(i, GB * (s + 1)))
                        if s == 0:
                            for b in range(GB):
                                if b >= 2:
                                    held(*late_sb(i, b - 1))
                                for n in (3, 4):
                                    for k in range(DT):
                                        j = mm(ps[2 * (b % 2) + n - 3][:, :], w[:, k, n, :], xg[:, k, b * T:(b + 1) * T], start=(k == 0), stop=(k == DT - 1))
                                j.then_inc(late.sem, 1)
                            held(*score_sb(i, PM[0]))
                            for b in range(GB):
                                held(*late_sb(i, b + 1))
                                if b >= 2:
                                    held(*trv_sb(i, b - 1))
                                for u in range(UB):
                                    j = pe.transpose(ps[4 + b % 2][:, u * P:(u + 1) * P], v[:, b * T + u * P:b * T + (u + 1) * P], ident[:, :])
                                j.then_inc(trv.sem, 1)
                            held(*trv_sb(i, GB))
                        held(*x_back(i, QB * (s + 1)))
                        for n in range(U_ // 2):
                            if n >= 2:
                                held(*z_sb(i, s * U_ // 2 + n - 1))
                            for u in (2 * n, 2 * n + 1):
                                for e in range(2):
                                    at = (u % 2) * 2 * P + e * P
                                    j = mm(ps[n % 2][:, at:at + P], apm[:, e * U_ + u, 0, :], tok[:, u, 2 * e:2 * e + 2, :],
                                           start=True, stop=True)
                            j.then_inc(zp.sem, 1)
                        held(*score_sb(i, PM[0] + s * PM[1]))
                        if s == 0:
                            for b in range(GB):
                                j = chunk_blocks(1, b)
                            j.then_inc(ablk.sem, 1)
                        for b in range(GB):
                            held(*z_sb(i, s * U_ // 2 + (2 * (b + 1) if b != 1 else U_ // 2)))
                            if b == 1:
                                held(*ablk_sb(i, PASSES))
                            if b >= 2:
                                held(*psi_sb(i, s * GB + b - 1))
                            for u in range(b * UB, (b + 1) * UB):
                                for e in range(2):
                                    row = slice(e * DH, (e + 1) * DH)
                                    vs, ks = vk(e)
                                    col = (u % UB) * DH
                                    for c in range(QB):
                                        if (u % UB) * QB + c == STEPS:
                                            continue
                                        part = slice(c * C, (c + 1) * C)
                                        bank = ps[(4 if b % 2 == 0 else 0) + c]
                                        mm(bank[row, col:col + DH], z[part, u, ks * DH:(ks + 1) * DH], ke[part, u, row], start=True, stop=True,
                                           tile_position=(c * C, e * DH))
                                        j = mm(bank[row, 256 + col:256 + col + DH], ke[part, u, row], z[part, u, vs * DH:(vs + 1) * DH],
                                               start=True, stop=True, tile_position=(c * C, e * DH))
                            j.then_inc(pp.sem, 1)

                        def out_products(n):
                            b, half = n % GB, n // GB
                            if n >= 2:
                                held(*out_sb(i, s * GB * 2 + n - 1))
                            for c in range(NC_ // 2):
                                for e in range(2):
                                    cc = half * NC_ // 2 + c
                                    j = mm(ps[4 + n % 2][(1 - e) * DH:(2 - e) * DH, 0:nk * T // 2].rearrange("p (m t) -> p m t", m=nk)[:, :, c * C:(c + 1) * C],
                                           state[e * DH:(e + 1) * DH, cc, b, :],
                                           mov[e * DH:(e + 1) * DH, m1, b * T + cc * C:b * T + (cc + 1) * C], start=True, stop=True,
                                           tile_position=(e * DH, (1 - e) * DH))
                            j.then_inc(outp.sem, 1)

                        held(*psi_sb(i, GB * (s + 1)))
                        held(*state0(i, 1))
                        for c in range(STEPS):
                            if c >= 1:
                                held(*step_sb(i, s * STEPS + c))
                            for b in range(GB):
                                for e in range(2):
                                    row = slice(e * DH, (e + 1) * DH)
                                    j = mm(ps[6 + c % 2][row, b * DH:(b + 1) * DH], phi[row, c, b, :], state[row, c, b, :], start=True, stop=True,
                                           tile_position=(e * DH, e * DH))
                            j.then_inc(step_ps.sem, 1)
                            if c < U_ // 2:
                                n = c
                                if n >= 2:
                                    held(*px_sb(i, s * U_ // 2 + n - 1))
                                for e in range(2):
                                    for u in (2 * n, 2 * n + 1):
                                        j = mm(ps[2 * (n % 2) + e][:, (u % 2) * nk * P:(u % 2 + 1) * nk * P], z[:, u, e * P:(e + 1) * P],
                                               apm[:, e * U_ + u, m1, :], start=True, stop=True)
                                j.then_inc(px.sem, 1)
                            elif c % 2 == 1:
                                if c == U_ // 2 + 1:
                                    held(*px_sb(i, U_ // 2 * (s + 1)))
                                out_products((c - U_ // 2) // 2)
                        held(*step_sb(i, STEPS * (s + 1)))
                        for n in range((STEPS - U_ // 2) // 2, 2 * GB):
                            out_products(n)
                    held(*out_sb(i, PASSES * GB * 2))

        @block.scalar
        def _(act):
            A = act.activation
            act.wait_ge(*consts_in(0, len(loads)))
            with act.Fori(0, HP) as hp:
                with act.Fori(0, 2) as g:
                    i = hp * 2 + g
                    ch = Chain(act_links, act, i)
                    act.wait_ge(*neg_ba(i, 1))
                    for b in range(GB):
                        at = slice(b * T, (b + 1) * T)
                        act.wait_ge(*kproj(i, b + 1))
                        A(ksq[b % 2], ps[6 * (b % 2)][:, :], ACT.Square).then_inc(ksq_r.sem, 1)
                        act.wait_ge(*proj(i, b + 1))
                        j = A(q[:, at], ps[1 + 2 * (b % 2)][:, :], ACT.Copy)
                        if b == GB - 1:
                            j.then_inc(q_r.sem, 1)
                        ch.link(A(L[0][:, at], ps[2 + 2 * (b % 2)][:, :], ACT.Exp, scale=-1.0, bias=nba[:, 0:1]))
                        A(L[0][:, at], L[0][:, at], ACT.Ln, bias=1.0).then_inc(la.sem, 1)
                        act.wait_ge(*ssc(i, b + 1))
                        ch.link(A(rn[b % 2], rn[b % 2], ACT.Ln))
                        A(rn[b % 2], rn[b % 2], ACT.Exp, scale=-0.5).then_inc(rn_r.sem, 1)

                    def exponentials(s, b, minus):
                        at = slice(b * T, (b + 1) * T)
                        j = A(gp[b % 2][:, :, 1:], L[s][:, at].rearrange("p (c t) -> p c t", t=C), ACT.Exp, scale=-1.0)
                        if minus:
                            j = A(gm[b % 2], L[s][:, at], ACT.Exp)
                        j.then_inc(gexp.sem, 1)

                    act.wait_ge(*kn_r(i, GB))
                    act.wait_ge(*lcap(i, GB))
                    for b in range(GB):
                        if b >= 2:
                            act.wait_ge(*kpm(i, b - 1))
                            act.wait_ge(*movs(i, b - 1))
                        exponentials(0, b, True)
                    for s in range(PASSES):
                        if s == 1:
                            act.wait_ge(*step_ps(i, STEPS))
                            for b in range(GB):
                                if b >= 2:
                                    act.wait_ge(*movs(i, GB + b - 1))
                                    act.wait_ge(*kend_r(i, GB + b - 1))
                                exponentials(1, b, False)
                        for b in range(GB):
                            act.wait_ge(*tr(i, s * GB + b + 1))
                            us = slice(b * UB, (b + 1) * UB)
                            A(ke[:, us, :], ps[2][:, :].rearrange("p (u d) -> p u d", u=UB), ACT.Copy)
                            for bank, slots in ((0, (0, 3)), (1, (2, 1)))[:1 + s]:
                                for e, slot in enumerate(slots):
                                    j = A(tok[:, us, slot, :], ps[bank][:, :].rearrange("p (u d) -> p u d", u=UB)[:, :, e * DH:(e + 1) * DH], ACT.Copy)
                            j.then_inc(tr_sb.sem, 1)
                        if s == 0:
                            for b in range(GB):
                                at = slice(b * T, (b + 1) * T)
                                act.wait_ge(*late(i, b + 1))
                                A(v[:, at], ps[2 * (b % 2) + 1][:, :], ACT.Copy)
                                j = A(L[1][:, at], ps[2 * (b % 2)][:, :], ACT.Exp, scale=-1.0, bias=nba[:, 1:2])
                                j.then_inc(late_sb.sem, 1)
                            act.wait_ge(*late_sb(i, GB))
                            for b in range(GB):
                                at = slice(b * T, (b + 1) * T)
                                A(L[1][:, at], L[1][:, at], ACT.Ln, bias=1.0).then_inc(la_r.sem, 1)
                            for b in range(GB):
                                act.wait_ge(*trv(i, b + 1))
                                us = slice(b * UB, (b + 1) * UB)
                                for e, slot in enumerate((2, 1)):
                                    j = A(tok[:, us, slot, :], ps[4 + b % 2][:, :].rearrange("p (u d) -> p u d", u=UB)[:, :, e * DH:(e + 1) * DH], ACT.Copy)
                                j.then_inc(trv_sb.sem, 1)
                            act.wait_ge(*movs(i, GB))
                            act.wait_ge(*kpm(i, GB))
                            for b in range(GB):
                                act.wait_ge(*lcap_r(i, b + 1))
                                if b >= 2:
                                    act.wait_ge(*kpm_r(i, b - 1))
                                exponentials(1, b, True)
                        for n in range(U_ // 2):
                            act.wait_ge(*zp(i, s * U_ // 2 + n + 1))
                            A(z[:, 2 * n:2 * n + 2, :], ps[n % 2][:, :].rearrange("p (u d) -> p u d", u=2), ACT.Copy).then_inc(z_sb.sem, 1)
                        if s == 0:
                            act.wait_ge(*x_out(i, 1))
                            act.wait_ge(*nt_out(i, PASSES))
                        else:
                            act.wait_ge(*outp(i, 2 * GB))
                        for b in range(GB):
                            act.wait_ge(*phi_sb(i, s * GB + b + 1))
                            for c in range(QB):
                                us = UB - (c == QB - 1)
                                j = A(state[:, 1 + c::QB, b, :], ps[(4 if b % 2 == 0 else 0) + c][:, 256:256 + us * DH].rearrange("p (u d) -> p u d", d=DH), ACT.Copy)
                            j.then_inc(psi_sb.sem, 1)
                    act.wait_ge(*out_sb(i, PASSES * GB * 2))
                    act.sem_inc(act_turns.sem, 1)
                    act.dma_start(scratch["o"][bass.ds(hp * P, P), bass.ds(g * GT, GT)], o[:, :]).then_inc(stored.sem, 16)
                    act.wait_ge(*stored(i, 1))
                    act.sem_inc(act_turns.sem, 1)

        @block.gpsimd
        def _(pool):
            pool.wait_ge(*consts_in(0, len(loads)))
            with pool.Fori(0, HP) as hp:
                with pool.Fori(0, 2) as g:
                    i = hp * 2 + g
                    chunks = "p (c t) -> p c t"
                    ch = Chain(pool_links, pool, i)
                    for b in range(GB):
                        at = slice(b * T, (b + 1) * T)
                        pool.wait_ge(*kpm(i, b + 1))
                        pool.tensor_tensor(mov[:, 1, at].rearrange(chunks, t=C), kn[:, at].rearrange(chunks, t=C), gp[b % 2][:, :, 0:C], ALU.mult)
                        pool.tensor_tensor(mov[:, 2, at].rearrange(chunks, t=C), q[:, at].rearrange(chunks, t=C), gp[b % 2][:, :, 1:], ALU.mult).then_inc(movs.sem, 1)
                    for b in range(GB):
                        at = slice(b * T, (b + 1) * T)
                        pool.wait_ge(*lsum_r(i, b + 1))
                        pool.sem_inc(pool_turns.sem, 1)
                        pool.tensor_scalar(L[1][:, at], L[1][:, at], LMAX, None, ALU.min).then_inc(lcap_r.sem, 1)
                    pool.wait_ge(*tr(i, GB))
                    pool.sem_inc(pool_turns.sem, 1)
                    pool.wait_ge(*score(i, PM[0]))
                    pool.sem_inc(pool_turns.sem, 1)
                    for b in range(GB):
                        at = slice(b * T, (b + 1) * T)
                        pool.wait_ge(*gexp(i, GB + b + 1))
                        pool.tensor_tensor(km[:, at], kn[:, at], gm[b % 2], ALU.mult)
                        pool.tensor_tensor(mov[:, 0, at].rearrange(chunks, t=C), kn[:, at].rearrange(chunks, t=C), gp[b % 2][:, :, 1:], ALU.mult).then_inc(kpm_r.sem, 1)
                    pool.wait_ge(*nt_in(i, PASSES))
                    invert(pool, ch, 1, xi_r)
                    for b in range(GB):
                        at = slice(b * T, (b + 1) * T)
                        if b == 0:
                            pool.wait_ge(*outp(i, 2 * GB))
                        pool.wait_ge(*gexp(i, 2 * GB + b + 1))
                        pool.tensor_tensor(mov[:, 2, at].rearrange(chunks, t=C), q[:, at].rearrange(chunks, t=C), gp[b % 2][:, :, 1:], ALU.mult).then_inc(movs.sem, 1)
                    ch.close()

        @block.vector
        def _(dve):
            tt, stt = dve.tensor_tensor, dve.scalar_tensor_tensor
            chunks = "p (c t) -> p c t"
            dve.wait_ge(*consts_in(0, len(loads)))
            dve.memset(apm[:, :, 0, :], 0.0).then_inc(apm0.sem, 1)
            with dve.Fori(0, HP) as hp:
                with dve.Fori(0, 2) as g:
                    i = hp * 2 + g
                    ch = Chain(dve_links, dve, i)
                    dve.wait_ge(*inputs_in(i, 7))
                    dve.tensor_scalar(nba[:, :], nba[:, :], -1.0, None, ALU.mult).then_inc(neg_ba.sem, 1)
                    for b in range(GB):
                        at = slice(b * T, (b + 1) * T)
                        dve.wait_ge(*ss(i, b + 1))
                        dve.tensor_scalar(rn[b % 2], ps[5 + 2 * (b % 2)][:, :], 1e-24, 2.0 ** 40, ALU.max, ALU.mult).then_inc(ssc.sem, 1)
                        dve.wait_ge(*la(i, b + 1))
                        dve.tensor_tensor_scan(L[0][:, at], restart[:, :], L[0][:, at], 0.0, ALU.mult, ALU.add).then_inc(lsum.sem, 1)
                        dve.wait_ge(*rn_r(i, b + 1))
                        stt(kn[:, at], rn[b % 2], 2.0 ** 20, ps[6 * (b % 2)][:, :], ALU.mult, ALU.mult).then_inc(kn_r.sem, 1)
                        dve.wait_ge(*lsum(i, b + 1))
                        dve.tensor_scalar(L[0][:, at], L[0][:, at], LMAX, None, ALU.min).then_inc(lcap.sem, 1)

                    def keys_by_decay(b):
                        at = slice(b * T, (b + 1) * T)
                        dve.wait_ge(*gexp(i, b + 1))
                        tt(km[:, at], kn[:, at], gm[b % 2], ALU.mult)
                        dve.tensor_copy(gend[:, 0, b * NC_:(b + 1) * NC_].unsqueeze(2), gp[b % 2][:, :, C:])
                        tt(mov[:, 0, at].rearrange(chunks, t=C), kn[:, at].rearrange(chunks, t=C), gp[b % 2][:, :, 1:], ALU.mult).then_inc(kpm.sem, 1)

                    def keys_at_end(s, b):
                        at = slice(b * T, (b + 1) * T)
                        if b >= 2:
                            dve.wait_ge(*tr(i, s * GB + b - 1))
                        if s == 1:
                            dve.wait_ge(*gexp(i, 2 * GB + b + 1))
                            ch.link(dve.tensor_copy(gend[:, 1, b * NC_:(b + 1) * NC_].unsqueeze(2), gp[b % 2][:, :, C:]))
                        tt(kend[b % 2].rearrange(chunks, t=C), km[:, at].rearrange(chunks, t=C),
                           gend[:, s, b * NC_:(b + 1) * NC_].unsqueeze(2).broadcast_to([P, NC_, C]), ALU.mult).then_inc(kend_r.sem, 1)

                    def chunk_blocks(s):
                        dve.wait_ge(*ablk(i, s + 1))
                        for e in range(2):
                            j = tt(blocks[s][:, e * U_:(e + 1) * U_, :], ps[6 - 4 * s + e][:, :].rearrange("p (u t) -> p u t", t=C),
                                   minus_before[:, :].unsqueeze(1).broadcast_to([P, U_, C]), ALU.mult)
                        j.then_inc(ablk_sb.sem, 1)

                    def scores(s, b):
                        nk = 2 - s
                        each = 4 // nk
                        for first in range(b * UB, (b + 1) * UB, each):
                            for e in range(2):
                                k = first // each * 2 + e
                                dve.wait_ge(*score(i, s * PM[0] + k + 1))
                                tt(apm[:, e * U_ + first:e * U_ + first + each, 1 + s:3, :],
                                   ps[4 + k % 4][:, :].rearrange("p (n m t) -> p n m t", n=each, m=nk),
                                   masks[:, s:2, :].unsqueeze(1).broadcast_to([P, each, nk, P]), ALU.mult).then_inc(score_sb.sem, 1)

                    def sum_r(b):
                        at = slice(b * T, (b + 1) * T)
                        dve.wait_ge(*la_r(i, b + 1))
                        dve.tensor_tensor_scan(L[1][:, at], restart[:, :], L[1][:, at], 0.0, ALU.mult, ALU.add).then_inc(lsum_r.sem, 1)

                    dve.wait_ge(*kn_r(i, GB))
                    for n in range(2):
                        j = dve.memset(gp[n][:, :, 0:1], 1.0)
                    ch.link(j)
                    for b in range(GB):
                        keys_by_decay(b)
                    dve.wait_ge(*kpm(i, GB))
                    keys_at_end(0, 0)
                    keys_at_end(0, 1)
                    chunk_blocks(0)
                    for b in range(GB):
                        scores(0, b)
                        if b + 2 < GB:
                            keys_at_end(0, b + 2)
                    dve.wait_ge(*nt_in(i, 1))
                    at_step = {16 + 2 * b: (lambda b=b: sum_r(b)) for b in range(GB)}
                    invert(dve, ch, 0, xi_s, at_step)
                    for s in range(PASSES):
                        m1 = slice(1, 3) if s == 0 else slice(2, 3)
                        nk = m1.stop - m1.start
                        if s == 1:
                            for b in range(GB):
                                scores(1, b)
                                if b + 2 < GB:
                                    keys_at_end(1, b + 2)
                        dve.wait_ge(*tr(i, GB * (s + 1)))
                        dve.wait_ge(*movs(i, GB * (s + 1)))
                        if s == 0:
                            dve.wait_ge(*kpm_r(i, GB))
                        for b in range(GB):
                            j = tt(phi[:, :, b, :], ident2[:, :].unsqueeze(1).broadcast_to([P, NC_, DH]),
                                   gend[:, s, b * NC_:(b + 1) * NC_].unsqueeze(2).broadcast_to([P, NC_, DH]), ALU.mult)
                        ch.link(j)
                        if s == 0:
                            dve.wait_ge(*x_out(i, 1))
                            dve.memset(state[:, 0, :, :], 0.0).then_inc(state0.sem, 1)
                            chunk_blocks(1)
                        for b in range(GB):
                            dve.wait_ge(*pp(i, s * GB + b + 1))
                            for c in range(QB):
                                us = UB - (c == QB - 1)
                                pf = phi[:, c:STEPS:QB, b, :]
                                j = tt(pf, pf, ps[(4 if b % 2 == 0 else 0) + c][:, 0:us * DH].rearrange("p (u d) -> p u d", d=DH), ALU.subtract)
                            j.then_inc(phi_sb.sem, 1)

                        def through_units(n):
                            at = slice(2 * n * P, (2 * n + 2) * P)
                            dve.wait_ge(*px(i, s * U_ // 2 + n + 1))
                            for e in range(2):
                                kr, vr = slice(e * DH, (e + 1) * DH), slice((1 - e) * DH, (2 - e) * DH)
                                both = ps[2 * (n % 2) + e][:, 0:2 * nk * P].rearrange("p (u m t) -> p m u t", u=2, m=nk)
                                mk = mov[kr, m1, at].rearrange("p m (u t) -> p m u t", u=2)
                                tt(mk, mk, both[kr], ALU.subtract)
                                if s == 0:
                                    vv = v[vr, at].rearrange("p (u t) -> p u t", u=2)
                                    tt(vv, vv, both[vr, 0], ALU.subtract)
                                    j = dve.tensor_copy(o[vr, at].rearrange("p (u t) -> p u t", u=2), both[vr, 1])
                                else:
                                    oo = o[vr, at].rearrange("p (u t) -> p u t", u=2)
                                    j = tt(oo, oo, both[vr, 0], ALU.add)
                            j.then_inc(px_sb.sem, 1)

                        def add_states(n):
                            b, half = n % GB, n // GB
                            at = slice(b * T + half * T // 2, b * T + (half + 1) * T // 2)
                            dve.wait_ge(*outp(i, s * GB * 2 + n + 1))
                            if s == 0:
                                ch.link(tt(v[:, at], v[:, at], ps[4 + n % 2][:, 0:T // 2], ALU.subtract))
                                dve.tensor_scalar(v[:, at], v[:, at], 1.0, -1.0, ALU.min, ALU.max)
                            tt(o[:, at], o[:, at], ps[4 + n % 2][:, (nk - 1) * T // 2:nk * T // 2], ALU.add).then_inc(out_sb.sem, 1)

                        dve.wait_ge(*psi_sb(i, GB * (s + 1)))
                        done = 0
                        for c in range(STEPS):
                            dve.wait_ge(*step_ps(i, s * STEPS + c + 1))
                            tt(state[:, c + 1, :, :], state[:, c + 1, :, :], ps[6 + c % 2][:, 0:GB * DH].rearrange("p (b d) -> p b d", b=GB), ALU.add).then_inc(step_sb.sem, 1)
                            if 1 <= c <= U_ // 2:
                                through_units(c - 1)
                            elif c > U_ // 2 + 1 and c % 2 == 0:
                                if c == U_ // 2 + 2:
                                    dve.wait_ge(*px_sb(i, U_ // 2 * (s + 1)))
                                add_states(done)
                                done += 1
                        if s == 0:
                            keys_at_end(1, 0)
                            keys_at_end(1, 1)
                        for n in range(done, GB * 2):
                            add_states(n)
                    ch.close()
    return signals


def head_and_mlp(nc, io, scratch, out):
    K_TOP = int(2 * np.log(T))
    KC = 16
    UB = T // P
    LOW = -3.0e38
    NSTAGE = int(np.log2(FF))
    HF = FF // 2

    signals = []
    with ExitStack() as ctx:
        def sb(name, *shape):
            return ctx.enter_context(nc.sbuf_tensor("f_" + name, list(shape), F32))

        def sig(name, per=1, step=1):
            return Signal(signals, nc, "f_" + name, per, step)

        ps = [ctx.enter_context(nc.psum_tensor(f"f_bank{i}", [P, T], F32)) for i in range(8)]
        loads = []

        def const(name, src, *shape):
            t = sb(name, *shape)
            loads.append((t[tuple(slice(None) for _ in shape)], src))
            return t

        def fm(name):
            return io[name].rearrange("(k p) n -> p k n", p=P)

        mean_d = const("mean_d", io["c_mean_d"], P, P)
        mean_bc = const("mean_bc", io["c_mean_bc"], P, P)
        ident = const("ident", io["c_ident"], P, P)
        w_o = const("w_o", fm("w_o1"), P, HP, D)
        w_q = const("w_q", fm("w_xq"), P, DT, KC)
        b_q = const("b_q", io["b_xq"], KC, 1)
        b_qr = const("b_qr", io["b_xqr"], 1, KC)
        w_out = const("w_out", fm("w_xo"), P, DT, D)
        b_out = const("b_out", io["b_xo"].unsqueeze(2), P, DT, 1)
        up_b = const("up_b", io["up_b"], P, FT)
        con_b = const("con_b", io["con_b"], P, DT)
        down_b = const("down_b", io["down_b"], P, DT)
        n_const = len(loads)
        yu = sb("yu", P, 2, 3, FF)
        yd = sb("yd", P, 2, 2, FF)
        bw = [sb("bwu", P, 2, 4, HF), sb("bwd", P, 2, 4, HF)]
        tu = sb("tu", P, 2, 3, HF)
        td = sb("td", P, 2, 2, HF)
        hid = sb("hid", P, FT, T)
        md = sb("md", P, FT, D)
        bu = sb("bu", P, FT)
        bd = sb("bd", P, DT)
        ones = sb("ones", 1, P)
        eps = sb("eps", P, 1)
        oin_of = [hid, sb("oin1", P, FT, T)]
        x_of = [sb("x0", P, DT, T), sb("x1", P, DT, T)]
        cx_of = [sb("cx0", P, DT, T), sb("cx1", P, DT, T)]
        cen = sb("cen", P, DT, T)
        sq = sb("sq", P, DT, T)
        xn = sb("xn", P, DT, T)
        lnv, rstd = sb("lnv", P, T), sb("rstd", P, T)
        qk_of = [sb("qk0", KC, 2, T), sb("qk1", KC, 2, T)]
        vt = sb("vt", P, UB, B * KC)
        xo = sb("xo", P, DT, B, 2 * KC)
        qa, ka = sq[:, 0, :], sq[:, 1, :]
        gk = hid[:, 0:UB, :]
        gs = hid[:, UB:2 * UB, :]
        corr, c2, c3, wt, rr = cen[:, 0, :], cen[:, 1, :], xn[:, 0, :], xn[:, 1, :], x_of[0][:, 0, :]
        m1, m2, second8, wsum = sb("m1", P, 8), sb("m2", P, 8), sb("second8", P, 8), sb("wsum", P, 2)

        consts_in, setup = sig("consts_in", n_const, 16), sig("setup", 5)
        yin = sig("yin", 4, 16)
        bw_in = [[sig(n + str(j), NSTAGE // 2, 16) for j in range(2)] for n in ("bwu_in", "bwd_in")]
        stage = [sig("stage_u", NSTAGE), sig("stage_d", NSTAGE)]
        half = [sig("half_u", 3 * NSTAGE), sig("half_d", 3 * NSTAGE)]
        in1 = [sig(f"in1_{n}", 3, 16) for n in range(2)]
        o_ps, x_sum, saved1 = sig("o_ps"), sig("x_sum"), sig("saved1", 3, 16)
        qkv_ps, qk_sb, v_sb = sig("qkv_ps"), sig("qk_sb"), sig("v_sb")
        ln = [[sig(n + str(l)) for n in ("mean", "cent", "sq", "var", "log", "rstd", "out")] for l in (1, 2)]
        mid_in, gram, gram_sb, gram_out, skew_in, corr_ps = (
            sig("mid_in", 2, 16), sig("gram", UB), sig("gram_sb"), sig("gram_out", 2, 16), sig("skew_in", 1, 16), sig("corr_ps"))
        mid, shifted_exp = sig("mid", 11), sig("shifted_exp")
        w_outs, circ_in, r_ps, r_sb = sig("w_outs", 5, 16), sig("circ_in", 1, 16), sig("r_ps"), sig("r_sb")
        xo_ps, xo_sb, bu_ps, bu_sb, md_ps, md_sb = sig("xo_ps"), sig("xo_sb"), sig("bu_ps"), sig("bu_sb"), sig("md_ps", 4), sig("md_sb", 4)
        in2 = [sig(f"in2_{n}", 1, 16) for n in range(2)]
        x_e, hid_ps, hid_sb, f_ps, x_f, saved2 = (
            sig("x_e"), sig("hid_ps", FT), sig("hid_sb", FT), sig("f_ps"), sig("x_f"), sig("saved2", 1, 16))
        sp_turns = sig("sp_turns")

        block = ctx.enter_context(nc.Block())

        def tokens(name, b):
            return scratch[name].rearrange("(k p) t -> p k t", p=P)[:, :, bass.ds(b * T, T)]

        @block.sync
        def _(sp):
            def held(*at):
                sp.wait_ge(*at)
                sp.sem_inc(sp_turns.sem, 1)

            for dst, src in loads:
                sp.dma_start(dst, src).then_inc(consts_in.sem, 16)
            sp.wait_ge(*setup(0, 3))
            sp.dma_start(yu[:, 0, 0:2, :], fm("w_exp")).then_inc(yin.sem, 16)
            sp.dma_start(yu[0:1, 0, 2, :], io["b_exp"]).then_inc(yin.sem, 16)
            sp.dma_start(yd[:, 0, :, :], fm("w_con")).then_inc(yin.sem, 16)

            def load(j, n):
                b = j * 2 + n
                sp.dma_start(oin_of[n][:, :, :], tokens("o", b)).then_inc(in1[n].sem, 16)
                sp.dma_start(x_of[n][:, :, :], tokens("x", b)).then_inc(in1[n].sem, 16)
                sp.dma_start(cx_of[n][:, :, :], io["ctx"].rearrange("(k p) t -> p k t", p=P)[:, :, bass.ds(b * T, T)]).then_inc(in1[n].sem, 16)

            def store(j, n):
                b = j * 2 + n
                held(*x_sum(b, 1))
                sp.dma_start(tokens("x3", b), x_of[n][:, :, :]).then_inc(saved1.sem, 16)
                held(*qk_sb(b, 1))
                for m in range(2):
                    sp.dma_start(scratch["qk"][m, bass.ds(b * KC, KC), :], qk_of[n][:, m, :]).then_inc(saved1.sem, 16)
                held(*v_sb(b, 1))
                held(*saved1(b, 3))

            load(0, 0)
            with sp.Fori(0, B // 2 - 1) as j:
                load(j, 1)
                store(j, 0)
                load(j + 1, 0)
                store(j, 1)
            load(B // 2 - 1, 1)
            store(B // 2 - 1, 0)
            store(B // 2 - 1, 1)
            for n, t in enumerate((qa, ka)):
                sp.dma_start(t, scratch["qk"][n]).then_inc(mid_in.sem, 16)
            sp.wait_ge(*gram_sb(0, 1))
            rows = scratch["gram"][0:2 * T * T].rearrange("(u p r m) -> p u r m", p=P, r=2, m=T)
            for r in range(2):
                sp.dma_start(rows[:, :, r, :], gk).then_inc(gram_out.sem, 16)
            sp.wait_ge(*gram_out(0, 2))
            sp.dma_start(gs, scratch["gram"].rearrange("(u p m) -> p u m", p=P, m=2 * T + 1)[:, :, 0:T]).then_inc(skew_in.sem, 16)
            sp.wait_ge(*mid(0, 11))
            for n in range(UB):
                sp.dma_start(scratch["wts"][n * P * T:(n + 1) * P * T].rearrange("(p t) -> p t", t=T), wt).then_inc(w_outs.sem, 16)
            sp.dma_start(scratch["wts"][T * T:T * T + 2 * T].rearrange("(p t) -> p t", t=T), wt[0:2, :]).then_inc(w_outs.sem, 16)
            sp.wait_ge(*w_outs(0, 5))
            sp.dma_start(gs, scratch["wts"][1:T * (T + 1) + 1].rearrange("(u p m) -> p u m", p=P, m=T + 1)[:, :, 0:T]).then_inc(circ_in.sem, 16)
            sp.wait_ge(*xo_ps(0, 1))

            def load_again(j, n):
                sp.dma_start(x_of[n][:, :, :], tokens("x3", j * 2 + n)).then_inc(in2[n].sem, 16)

            def result(j, n):
                b = j * 2 + n
                held(*x_f(b, 1))
                sp.dma_start(out.rearrange("(k p) t -> p k t", p=P)[:, :, bass.ds(b * T, T)], x_of[n][:, :, :]).then_inc(saved2.sem, 16)
                held(*saved2(b, 1))

            load_again(0, 0)
            with sp.Fori(0, B // 2 - 1) as j:
                load_again(j, 1)
                result(j, 0)
                load_again(j + 1, 0)
                result(j, 1)
            load_again(B // 2 - 1, 1)
            result(B // 2 - 1, 0)
            result(B // 2 - 1, 1)

        def norm_pe(pe, b, l, x):
            mean, cent, sqs, var, log, rst, o = ln[l]
            for j in range(DT):
                i = pe.matmul(ps[2][:, :], mean_d[:, :], x[:, j, :], start=(j == 0), stop=(j == DT - 1))
            i.then_inc(mean.sem, 1)
            pe.wait_ge(*sqs(b, 1))
            for j in range(DT):
                i = pe.matmul(ps[3][:, :], mean_d[:, :], sq[:, j, :], start=(j == 0), stop=(j == DT - 1))
            i.then_inc(var.sem, 1)
            pe.wait_ge(*o(b, 1))

        def norm_act(act, b, l):
            mean, cent, sqs, var, log, rst, o = ln[l]
            act.wait_ge(*cent(b, 1))
            act.activation(sq[:, :, :], cen[:, :, :], ACT.Square).then_inc(sqs.sem, 1)
            act.wait_ge(*var(b, 1))
            act.activation(lnv[:, :], ps[3][:, :], ACT.Ln, bias=eps[:, 0:1]).then_inc(log.sem, 1)
            act.wait_ge(*log(b, 1))
            act.activation(rstd[:, :], lnv[:, :], ACT.Exp, scale=-0.5).then_inc(rst.sem, 1)

        def norm_dve(dve, b, l, x):
            mean, cent, sqs, var, log, rst, o = ln[l]
            dve.wait_ge(*mean(b, 1))
            dve.tensor_tensor(cen[:, :, :], x[:, :, :], wide(ps[2][:, :], DT), ALU.subtract).then_inc(cent.sem, 1)
            dve.wait_ge(*rst(b, 1))
            dve.tensor_tensor(xn[:, :, :], cen[:, :, :], wide(rstd[:, :], DT), ALU.mult).then_inc(o.sem, 1)

        def butterfly(eng, which, y, tmp, st, hold):
            s = 2 ** st if which == 0 else 2 ** (NSTAGE - 1 - st)
            rows = y.shape[2]
            pairs = y[:, st % 2, :, :].rearrange("p r (n i s) -> p i r n s", i=2, s=s)
            into = y[:, (st + 1) % 2, :, :].rearrange("p r (n i s) -> p i r n s", i=2, s=s)

            def w(i, j):
                return bw[which][:, st % 2, 2 * i + j, :].rearrange("p (n s) -> p n s", s=s).unsqueeze(1).broadcast_to([P, rows, HF // s, s])

            def t(j):
                return tmp[:, j, :, :].rearrange("p r (n s) -> p r n s", s=s)

            hold(*bw_in[which][st % 2](0, st // 2 + 1))
            if st >= 1:
                hold(*stage[which](0, st))
            for i in range(2):
                k = 3 * st + 2 * i
                if i == 1:
                    hold(*half[which](0, k))
                eng.tensor_tensor(t(0), pairs[:, 0], w(i, 0), ALU.mult)
                eng.tensor_tensor(t(1), pairs[:, 1], w(i, 1), ALU.mult).then_inc(half[which].sem, 1)
                hold(*half[which](0, k + 1))
                j = eng.tensor_tensor(into[:, i], t(0), t(1), ALU.add)
                j.then_inc((half if i == 0 else stage)[which].sem, 1)

        def stream(eng, which, name, st):
            if st + 1 < NSTAGE:
                if st >= 1:
                    eng.wait_ge(*stage[which](0, st))
                eng.dma_start(bw[which][:, (st + 1) % 2, :, :], io[name][st + 1:st + 2, :].partition_broadcast(P)).then_inc(bw_in[which][(st + 1) % 2].sem, 16)

        @block.tensor
        def _(pe):
            mm = pe.matmul
            pe.wait_ge(*consts_in(0, n_const))
            pe.wait_ge(*setup(0, 5))
            with pe.Fori(0, B // 2) as j:
                for n in range(2):
                    b = j * 2 + n
                    oin, x, cx = oin_of[n], x_of[n], cx_of[n]
                    pe.wait_ge(*in1[n](j, 3))
                    for m in range(DT):
                        for k in range(HP):
                            i = mm(ps[m][:, :], w_o[:, k, m * P:(m + 1) * P], oin[:, k, :], start=(k == 0), stop=(k == HP - 1))
                    i.then_inc(o_ps.sem, 1)
                    pe.wait_ge(*x_sum(b, 1))
                    norm_pe(pe, b, 0, x)
                    for bank, src in ((4, xn), (5, cx)):
                        for k in range(DT):
                            mm(ps[bank][0:KC, :], w_q[:, k, :], src[:, k, :], start=(k == 0), stop=(k == DT - 1))
                    for u in range(UB):
                        for k in range(DT):
                            mm(ps[6][:, u * KC:(u + 1) * KC], cx[:, k, u * P:(u + 1) * P], w_q[:, k, :], start=(k == 0), stop=False)
                        i = mm(ps[6][:, u * KC:(u + 1) * KC], ones[:, :], b_qr[:, :], start=False, stop=True)
                    i.then_inc(qkv_ps.sem, 1)
            pe.wait_ge(*mid_in(0, 2))
            pe.wait_ge(*v_sb(B - 1, 1))
            for u in range(UB):
                mm(ps[u][:, :], ka[:, u * P:(u + 1) * P], qa, start=True, stop=True).then_inc(gram.sem, 1)
            pe.wait_ge(*stage[0](0, NSTAGE))
            pe.wait_ge(*stage[1](0, NSTAGE))
            fin = NSTAGE % 2
            for m in range(FT):
                i = mm(ps[6][:, m:m + 1], yu[0:1, fin, 2, m * P:(m + 1) * P], ones[0:1, 0:1], start=True, stop=True)
            i.then_inc(bu_ps.sem, 1)
            pe.wait_ge(*gram_sb(0, 1))
            for n in range(4):
                for m in (2 * n, 2 * n + 1):
                    for k in range(DT):
                        i = pe.transpose(ps[n][:, (m % 2) * D + k * P:(m % 2) * D + (k + 1) * P], yd[:, fin, k, m * P:(m + 1) * P], ident[:, :])
                i.then_inc(md_ps.sem, 1)
            pe.wait_ge(*skew_in(0, 1))
            for u in range(UB):
                i = mm(ps[4][:, :], mean_bc[:, :], gs[:, u, :], start=(u == 0), stop=(u == UB - 1))
            i.then_inc(corr_ps.sem, 1)
            pe.wait_ge(*circ_in(0, 1))
            for n in range(UB):
                for u in range(UB):
                    i = mm(ps[5][:, n * P:(n + 1) * P], gs[:, u, n * P:(n + 1) * P], vt[:, u, :], start=(u == 0), stop=(u == UB - 1))
            i.then_inc(r_ps.sem, 1)
            pe.wait_ge(*r_sb(0, 1))
            for m in range(DT):
                for h in range(2):
                    for k in range(DT):
                        i = mm(ps[7][:, (2 * m + h) * P:(2 * m + h + 1) * P], w_out[:, k, m * P:(m + 1) * P],
                               rr[:, ((1 - h) * 2 + k) * P:((1 - h) * 2 + k + 1) * P], start=(k == 0), stop=(k == DT - 1))
            i.then_inc(xo_ps.sem, 1)
            pe.wait_ge(*md_sb(0, 4))
            pe.wait_ge(*bu_sb(0, 1))
            with pe.Fori(0, B // 2) as j:
                for n in range(2):
                    b = j * 2 + n
                    pe.wait_ge(*x_e(b, 1))
                    norm_pe(pe, b, 1, x_of[n])
                    for m in range(FT):
                        for k in range(DT):
                            i = mm(ps[m][:, :], yu[:, fin, k, m * P:(m + 1) * P], xn[:, k, :], start=(k == 0), stop=(k == DT - 1))
                        i.then_inc(hid_ps.sem, 1)
                    pe.wait_ge(*hid_sb(b, 2))
                    for k in range(FT):
                        pe.wait_ge(*hid_sb(b, k + 1))
                        for m in range(DT):
                            i = mm(ps[m][:, :], md[:, k, m * P:(m + 1) * P], hid[:, k, :], start=(k == 0), stop=(k == FT - 1))
                    i.then_inc(f_ps.sem, 1)

        @block.scalar
        def _(act):
            A = act.activation
            act.wait_ge(*consts_in(0, n_const))
            act.wait_ge(*setup(0, 5))
            with act.Fori(0, B // 2) as j:
                for n in range(2):
                    b = j * 2 + n
                    norm_act(act, b, 0)
                    act.wait_ge(*qkv_ps(b, 1))
                    for m in range(2):
                        i = A(qk_of[n][:, m, :], ps[4 + m][0:KC, :], ACT.Identity, bias=b_q[:, :])
                    i.then_inc(qk_sb.sem, 1)
            act.wait_ge(*gram(0, UB))
            for u in range(UB):
                i = A(gk[:, u, :], ps[u][:, :], ACT.Copy)
            i.then_inc(gram_sb.sem, 1)
            for n in range(4):
                act.wait_ge(*md_ps(0, n + 1))
                A(md[:, 2 * n:2 * n + 2, :], ps[n][:, :].rearrange("p (m d) -> p m d", m=2), ACT.Copy).then_inc(md_sb.sem, 1)
            act.wait_ge(*mid(0, 7))
            A(wt, corr, ACT.Exp, bias=wsum[:, 1:2]).then_inc(shifted_exp.sem, 1)
            act.wait_ge(*r_ps(0, 1))
            A(rr, ps[5][:, :], ACT.Copy).then_inc(r_sb.sem, 1)
            with act.Fori(0, B) as b:
                norm_act(act, b, 1)
                for m in range(FT):
                    act.wait_ge(*hid_ps(b, m + 1))
                    A(hid[:, m, :], ps[m][:, :], ACT.Gelu, bias=bu[:, m:m + 1]).then_inc(hid_sb.sem, 1)

        @block.gpsimd
        def _(pool):
            pool.dma_start(bw[0][:, 0, :, :], io["bw_up"][0:1, :].partition_broadcast(P)).then_inc(bw_in[0][0].sem, 16)
            stream(pool, 0, "bw_up", 0)
            pool.dma_start(bw[1][:, 0, :, :], io["bw_down"][0:1, :].partition_broadcast(P)).then_inc(bw_in[1][0].sem, 16)
            pool.wait_ge(*yin(0, 3))
            for st in range(NSTAGE):
                stream(pool, 1, "bw_down", st)
                butterfly(pool, 1, yd, td, st, pool.wait_ge)
            for st in range(1, NSTAGE):
                stream(pool, 0, "bw_up", st)

        @block.vector
        def _(dve):
            tt, stt = dve.tensor_tensor, dve.scalar_tensor_tensor
            dve.memset(yu[:, 0, 2, :], 0.0).then_inc(setup.sem, 1)
            dve.memset(ones[:, :], 1.0).then_inc(setup.sem, 1)
            dve.memset(eps[:, :], 1e-5).then_inc(setup.sem, 1)
            dve.wait_ge(*consts_in(0, n_const))
            dve.tensor_tensor(bd[:, :], con_b[:, :], down_b[:, :], ALU.add).then_inc(setup.sem, 1)
            dve.memset(m2[:, :], LOW).then_inc(setup.sem, 1)
            stages_after = {0: (0,), 1: (1,), 4: (2, 3), 5: (4, 5), 6: (6, 7), 7: (8, 9)}
            for b in range(B):
                x = x_of[b % 2]
                dve.wait_ge(*o_ps(b, 1))
                for m in range(DT):
                    i = tt(x[:, m, :], x[:, m, :], ps[m][:, :], ALU.add)
                i.then_inc(x_sum.sem, 1)
                dve.wait_ge(*x_sum(b, 1))
                norm_dve(dve, b, 0, x)
                dve.wait_ge(*qkv_ps(b, 1))
                dve.tensor_copy(vt[:, :, b * KC:(b + 1) * KC], ps[6][:, 0:UB * KC].rearrange("p (u c) -> p u c", c=KC)).then_inc(v_sb.sem, 1)
                if b == 0:
                    dve.wait_ge(*yin(0, 3))
                for st in stages_after.get(b, ()):
                    butterfly(dve, 0, yu, tu, st, dve.wait_ge)
            dve.wait_ge(*bu_ps(0, 1))
            tt(bu[:, :], up_b[:, :], ps[6][:, 0:FT], ALU.add).then_inc(bu_sb.sem, 1)

            def then(i):
                link[0] += 1
                i.then_inc(mid.sem, 1)
                dve.wait_ge(*mid(0, link[0]))

            link = [0]
            dve.wait_ge(*corr_ps(0, 1))
            then(dve.tensor_copy(corr, ps[4][:, :]))
            then(dve.max(m1[:, :], corr))
            then(dve.match_replace(c2, m1[:, :], corr, LOW))
            then(dve.max(second8[:, :], c2))
            then(dve.tensor_copy(m2[:, 0:K_TOP - 8], second8[:, 0:K_TOP - 8]))
            then(dve.match_replace(c3, m2[:, :], c2, LOW))
            then(dve.tensor_scalar(wsum[:, 1:2], m1[:, 0:1], -1.0, None, ALU.mult))
            dve.wait_ge(*shifted_exp(0, 1))
            then(stt(wt, c3, -1e38, wt, ALU.is_lt, ALU.mult))
            then(dve.tensor_reduce(wsum[:, 0:1], wt, AX.X, ALU.add))
            then(dve.reciprocal(wsum[:, 0:1], wsum[:, 0:1]))
            then(dve.tensor_scalar(wt, wt, wsum[:, 0:1], None, ALU.mult))
            dve.wait_ge(*xo_ps(0, 1))
            for m in range(DT):
                i = dve.tensor_scalar(xo[:, m, :, :].rearrange("p b (c h) -> p h (b c)", h=2), ps[7][:, 2 * m * P:2 * (m + 1) * P].rearrange("p (h n) -> p h n", h=2),
                                      b_out[:, m, :], None, ALU.add)
            i.then_inc(xo_sb.sem, 1)
            dve.wait_ge(*xo_sb(0, 1))
            with dve.Fori(0, B // 2) as j:
                for n in range(2):
                    b = j * 2 + n
                    x = x_of[n]
                    dve.wait_ge(*in2[n](j, 1))
                    for m in range(DT):
                        i = tt(x[:, m, :].rearrange("p (r t) -> p r t", t=2 * KC), x[:, m, :].rearrange("p (r t) -> p r t", t=2 * KC),
                               xo[:, m, bass.ds(b, 1), :].broadcast_to([P, T // (2 * KC), 2 * KC]), ALU.add)
                    i.then_inc(x_e.sem, 1)
                    dve.wait_ge(*x_e(b, 1))
                    norm_dve(dve, b, 1, x)
                    dve.wait_ge(*f_ps(b, 1))
                    for m in range(DT):
                        i = stt(x[:, m, :], ps[m][:, :], bd[:, m:m + 1], x[:, m, :], ALU.add, ALU.add)
                    i.then_inc(x_f.sem, 1)


def _masks(c):
    s, t = np.arange(P)[:, None], np.arange(P)[None, :]
    same = s // c == t // c
    return np.concatenate([same & (s < t), same & (s <= t)], 1).astype(np.float32)


def _pairs_swapped(w):
    return w.reshape(-1, HP, 2, DH)[:, :, ::-1].reshape(-1, H * DH)


CONSTS = {
    "c_mean_d": np.full((P, P), 1.0 / D, np.float32),
    "c_mean_di": np.full((P, P), 1.0 / DI, np.float32),
    "c_pair": np.kron(np.eye(2), np.ones((DH, DH))).astype(np.float32),
    "c_ident": np.eye(P, dtype=np.float32),
    "c_ident2": np.tile(np.eye(DH), (2, 1)).astype(np.float32),
    "c_mean_bc": np.full((P, P), 1.0 / (B * 16), np.float32),
    "c_masks": _masks(32),
    "c_minus_before": -(np.arange(P)[:, None] % 32 < np.arange(32)[None, :]).astype(np.float32),
    "c_restart": np.tile((np.arange(T) % 32 != 0), (P, 1)).astype(np.float32),
    "c_sel": np.repeat(np.eye(48)[:, RK:RK + 2 * NS], P, axis=1).astype(np.float32),
}


def layouts(v):
    def a(n):
        return np.asarray(v[n])

    def col(n):
        return a(n).reshape(-1, P).T

    return {
        "x": a("x").reshape(B * T, D).T, "ctx": a("ctx_1024").reshape(B * T, D).T,
        "w_in": a("L0_attn_W_in").T, "w_x": a("L0_attn_W_x").T, "w_dt": a("L0_attn_W_dt").T, "w_out": a("L0_attn_W_out").T,
        "conv_w": a("L0_attn_W_conv"), "conv_b": col("L0_attn_b_conv"), "b_dt": col("L0_attn_b_dt"), "a_log": a("L0_attn_A_log"),
        "skip_d": col("L0_attn_D"), "rms_w": col("L0_attn_rms_w"),
        "w_q": a("L0_xattn_Wq"), "w_k": a("L0_xattn_Wk"), "w_v": a("L0_xattn_Wv"), "w_o": a("L0_xattn_Wo"),
        "w_1": a("L0_ffn_w1"), "b_1": col("L0_ffn_b1"), "w_2": a("L0_ffn_w2"), "b_2": col("L0_ffn_b2"),
        "w_bg": np.concatenate([a("L1_attn_Wb").T, a("L1_attn_Wg").T], 1), "b_bg": np.stack([a("L1_attn_bb"), a("L1_attn_bg")], 1),
        "w_d": np.stack([a("L1_attn_Wk").T, a("L1_attn_Wq").T, a("L1_attn_Wa").T, a("L1_attn_WaR").T, _pairs_swapped(a("L1_attn_Wv").T)])
        .reshape(5, DT, P, HP, P).transpose(3, 2, 1, 0, 4).reshape(HP * P, -1),
        "b_a": np.stack([a("L1_attn_ba"), a("L1_attn_baR")], 1),
        "w_o1": _pairs_swapped(a("L1_attn_Wo")).T,
        "w_xq": a("L1_xattn_Wq"), "b_xq": a("L1_xattn_bq").reshape(-1, 1), "b_xqr": a("L1_xattn_bq").reshape(1, -1),
        "w_xo": a("L1_xattn_Wout")[::-1], "b_xo": col("L1_xattn_bout"),
        "w_exp": a("L1_ffn_W_exp"), "b_exp": a("L1_ffn_b_exp").reshape(1, -1), "up_b": col("L1_ffn_up_bias"),
        "w_con": a("L1_ffn_W_con").T, "con_b": col("L1_ffn_b_con"), "down_b": col("L1_ffn_down_bias"),
        "bw_up": a("L1_ffn_up_weights").transpose(0, 2, 3, 1).reshape(-1, 2 * FF),
        "bw_down": a("L1_ffn_down_weights")[::-1].transpose(0, 3, 2, 1).reshape(-1, 2 * FF),
        "ln_w": col("L1_attn_ln_w"), "ln_b": col("L1_attn_ln_b"),
    }


def build(nc, io, out):
    scratch = {n: nc.dram_tensor("s_" + n, s, F32, kind="Internal").ap() for n, s in {
        "x": [D, B * T], "x2": [D, B * T], "beta": [H, B * T], "gamma": [H, B * T],
        "x3": [D, B * T], "qk": [2, B * 16, T], "gram": [T * (2 * T + 1)], "wts": [T * (T + 2)],
        "nt": [P, 32 * 32], "xt": [P, 32 * 32], "o": [H * DH, B * T]}.items()}
    nc.clear_and_free_semaphores(layer0(nc, io, scratch))
    nc.all_engine_barrier()
    nc.clear_and_free_semaphores(delta_rule(nc, io, scratch))
    nc.all_engine_barrier()
    head_and_mlp(nc, io, scratch, out)


def kernel(**inputs):
    import concourse.bacc as _bacc
    from concourse.bass_utils import run_bass_kernel_spmd as _run

    nc = _bacc.Bacc("TRN2", target_bir_lowering=False, num_devices=1)
    arrays = {n: np.ascontiguousarray(a) for n, a in {**layouts(inputs), **CONSTS}.items()}
    io = {n: nc.dram_tensor("in_" + n, a.shape, mybir.dt.from_np(a.dtype), kind="ExternalInput").ap() for n, a in arrays.items()}
    out = nc.dram_tensor("out_y", [D, B * T], F32, kind="ExternalOutput").ap()
    build(nc, io, out)
    r = _run(nc, [{"in_" + n: a for n, a in arrays.items()}], core_ids=[0])
    return np.ascontiguousarray(r.results[0]["out_y"].T).reshape(B, T, D)
```
